# Optimizing a Trainium2 kernel written in Bass

```python
import numpy as np
import jax
import jax.numpy as jnp

def _softmax(x, axis=-1):
    return jax.nn.softmax(x, axis=axis)

def _gelu(x):
    return jax.nn.gelu(x, approximate=True)

def _silu(x):
    return jax.nn.silu(x)

def _sigmoid(x):
    return jax.nn.sigmoid(x)

def _layernorm(x, axis=-1, eps=1e-05):
    m = jnp.mean(x, axis=axis, keepdims=True)
    v = jnp.var(x, axis=axis, keepdims=True)
    return (x - m) / jnp.sqrt(v + eps)

def _scatter_add(tgt, idx, src, axis=0):
    return tgt.at[idx].add(src)

def _segment_sum(src, seg, n):
    return jax.ops.segment_sum(src, seg, n)
kernel_name = 'mk_adaln_d1_jaxref_r4_1923bd'

def setup_inputs(seed: int=0):
    np.random.seed(seed)
    _w = jnp.asarray

    def _L0_attn_setup():
        import jax, jax.numpy as jnp
        import numpy as np
        D = 256
        HS = 128
        NKV = 2

        def apply_rope(x):
            d = x.shape[-1]
            T = x.shape[-2]
            positions = jnp.arange(0, d, 2, dtype=jnp.float32)
            theta = 10000.0 ** (-2.0 * positions / d)
            angles = jnp.arange(T, dtype=jnp.float32)[:, None] * theta[None, :]
            cos, sin = (jnp.cos(angles), jnp.sin(angles))
            xr = x.reshape(x.shape[:-1] + (d // 2, 2))
            out = jnp.stack([xr[..., 0] * cos - xr[..., 1] * sin, xr[..., 1] * cos + xr[..., 0] * sin], axis=-1)
            return out.reshape(x.shape)
        key = jax.random.key(seed)
        k1, k2, k3, k4, k5 = jax.random.split(key, 5)
        B, T = (4, 512)
        x = jax.random.normal(k1, (B, T, D), dtype=jnp.float32)
        s = 1.0 / np.sqrt(D)
        Wq = jax.random.normal(k2, (NKV, HS, D), dtype=jnp.float32) * s
        Wk = jax.random.normal(k3, (HS, D), dtype=jnp.float32) * s
        Wv = jax.random.normal(k4, (HS, D), dtype=jnp.float32) * s
        Wo = jax.random.normal(k5, (D, NKV * HS), dtype=jnp.float32) * (1.0 / np.sqrt(NKV * HS))
        return {'x': x, 'Wq': Wq, 'Wk': Wk, 'Wv': Wv, 'Wo': Wo}
    _L0_attn_in = _L0_attn_setup()

    def _L0_ffn_setup():
        import jax, jax.numpy as jnp
        import numpy as np
        MAX_THRESHOLD = 0.125
        key = jax.random.key(seed)
        ks = jax.random.split(key, 5)
        B, S, D, FF, E = (2, 512, 256, 1024, 8)
        sd = 1.0 / np.sqrt(D)
        sf = 1.0 / np.sqrt(FF)
        return {'inputs': jax.random.normal(ks[0], (B, S, D), dtype=jnp.float32), 'Wg': jax.random.normal(ks[1], (D, E), dtype=jnp.float32) * sd, 'bg': jnp.zeros((E,), dtype=jnp.float32), 'Wt': jax.random.normal(ks[2], (D, 1), dtype=jnp.float32) * sd, 'bt': jnp.zeros((1,), dtype=jnp.float32), 'W1': jax.random.normal(ks[3], (E, D, FF), dtype=jnp.float32) * sd, 'b1': jnp.zeros((E, FF), dtype=jnp.float32), 'W2': jax.random.normal(ks[4], (E, FF, D), dtype=jnp.float32) * sf, 'b2': jnp.zeros((E, D), dtype=jnp.float32)}
    _L0_ffn_in = _L0_ffn_setup()
    _L0_c = _w((lambda *s: np.random.randn(*s).astype(np.float32) * 0.05)(2, 256))
    _L0_wmod = _w((lambda *s: np.random.randn(*s).astype(np.float32) * 0.05)(256, 6 * 256) * 256 ** (-0.5))
    _d = {'L0_attn_x': _L0_attn_in['x'], 'L0_attn_Wq': _L0_attn_in['Wq'], 'L0_attn_Wk': _L0_attn_in['Wk'], 'L0_attn_Wv': _L0_attn_in['Wv'], 'L0_attn_Wo': _L0_attn_in['Wo'], 'L0_ffn_Wg': _L0_ffn_in['Wg'], 'L0_ffn_bg': _L0_ffn_in['bg'], 'L0_ffn_Wt': _L0_ffn_in['Wt'], 'L0_ffn_bt': _L0_ffn_in['bt'], 'L0_ffn_W1': _L0_ffn_in['W1'], 'L0_ffn_b1': _L0_ffn_in['b1'], 'L0_ffn_W2': _L0_ffn_in['W2'], 'L0_ffn_b2': _L0_ffn_in['b2'], 'L0_c': _L0_c, 'L0_wmod': _L0_wmod}
    _x0 = _d['L0_attn_x']
    _d['L0_attn_x'] = jax.random.normal(jax.random.fold_in(jax.random.key(seed), 1), (2, 2048, 256), dtype=_x0.dtype)
    del _x0
    return _d

def reference(L0_attn_x, L0_attn_Wq, L0_attn_Wk, L0_attn_Wv, L0_attn_Wo, L0_ffn_Wg, L0_ffn_bg, L0_ffn_Wt, L0_ffn_bt, L0_ffn_W1, L0_ffn_b1, L0_ffn_W2, L0_ffn_b2, L0_c, L0_wmod):

    def _L0_attn_ref(x, Wq, Wk, Wv, Wo):
        import jax, jax.numpy as jnp
        import numpy as np
        D = 256
        HS = 128
        NKV = 2

        def apply_rope(x):
            d = x.shape[-1]
            T = x.shape[-2]
            positions = jnp.arange(0, d, 2, dtype=jnp.float32)
            theta = 10000.0 ** (-2.0 * positions / d)
            angles = jnp.arange(T, dtype=jnp.float32)[:, None] * theta[None, :]
            cos, sin = (jnp.cos(angles), jnp.sin(angles))
            xr = x.reshape(x.shape[:-1] + (d // 2, 2))
            out = jnp.stack([xr[..., 0] * cos - xr[..., 1] * sin, xr[..., 1] * cos + xr[..., 0] * sin], axis=-1)
            return out.reshape(x.shape)
        B, T, _ = x.shape
        k = apply_rope(x @ Wk.T)
        v = x @ Wv.T
        q = jnp.einsum('btd,hkd->bhtk', x, Wq)
        q = apply_rope(q)
        scale = HS ** (-0.5)
        scores = jnp.einsum('bhtk,bsk->bhts', q, k) * scale
        causal = jnp.tril(jnp.ones((T, T), dtype=bool))
        scores = jnp.where(causal, scores, -jnp.inf)
        w = jax.nn.softmax(scores, axis=-1)
        out = jnp.einsum('bhts,bsk->bhtk', w, v)
        out = out.transpose(0, 2, 1, 3).reshape(B, T, NKV * HS)
        return out @ Wo.T

    def _L0_ffn_ref(inputs, Wg, bg, Wt, bt, W1, b1, W2, b2):
        import jax, jax.numpy as jnp
        import numpy as np
        MAX_THRESHOLD = 0.125
        x = inputs.reshape(-1, inputs.shape[-1])
        gate = jax.nn.softmax(x @ Wg + bg, axis=-1)
        thr = jax.nn.sigmoid(x @ Wt + bt) * MAX_THRESHOLD
        adapted = gate - thr
        mask = (adapted >= 0).astype(x.dtype)
        w = adapted * mask
        s = jnp.sum(w, axis=-1, keepdims=True)
        s = jnp.where(s == 0, jnp.ones_like(s), s)
        w = w / s
        h = jax.nn.gelu(jnp.einsum('td,edf->etf', x, W1) + b1[:, None, :])
        eo = jnp.einsum('etf,efd->etd', h, W2) + b2[:, None, :]
        out = jnp.einsum('te,etd->td', w, eo)
        return out.reshape(inputs.shape)
    x = L0_attn_x
    mod = (_silu(L0_c) @ L0_wmod).reshape(L0_c.shape[0], 6, 1, -1)
    sa, ca, ga, sb, cb, gb = (mod[:, 0], mod[:, 1], mod[:, 2], mod[:, 3], mod[:, 4], mod[:, 5])
    ga = (2 * (ga >= 0) - 1) * jnp.maximum(jnp.abs(ga), 0.25)
    gb = (2 * (gb >= 0) - 1) * jnp.maximum(jnp.abs(gb), 0.25)
    h = _layernorm(x, axis=-1) * (1 + ca) + sa
    x = x + ga * _L0_attn_ref(h, L0_attn_Wq, L0_attn_Wk, L0_attn_Wv, L0_attn_Wo)
    h = _layernorm(x, axis=-1) * (1 + cb) + sb
    x = x + gb * _L0_ffn_ref(h, L0_ffn_Wg, L0_ffn_bg, L0_ffn_Wt, L0_ffn_bt, L0_ffn_W1, L0_ffn_b1, L0_ffn_W2, L0_ffn_b2)
    return x

_drawn_inputs = setup_inputs


def setup_inputs(seed=0):
    import zlib

    import numpy as np

    out = dict(_drawn_inputs(seed))
    spreads = {'L0_ffn_bg': (0.0, 0.8), 'L0_ffn_b1': (0.0, 0.758), 'L0_ffn_b2': (0.0, 0.514)}
    factors = {'L0_ffn_Wt': 3.948}
    for name, (base, spread) in spreads.items():
        noise = np.random.default_rng([zlib.crc32(name.encode()), seed]).standard_normal(out[name].shape)
        drawn = base * np.exp(spread * noise) if base else spread * noise
        out[name] = jnp.asarray(drawn.astype(out[name].dtype))
    for name, factor in factors.items():
        out[name] = (out[name] * factor).astype(out[name].dtype)
    return out
```

```python
from contextlib import ExitStack

import concourse.bass as bass
from concourse import mybir

F32 = mybir.dt.float32
F32R = mybir.dt.float32r
ALU = mybir.AluOpType
ACT = mybir.ActivationFunctionType
AX_X = mybir.AxisListType.X

P = 128
B, T, D = 2, 2048, 256
HS, NH = 128, 2
E, FF = 8, 1024
KD = D // P
NT = T // P
TILES = B * NT
FT = FF // P
UNIT = 4
UTOK = UNIT * P
UNITS = TILES // UNIT
QKV = (NH + 2) * HS
ROT = (NH + 1) * HS
SCALE = float(HS) ** -0.5
EPS = 1e-5
XS = 6
NG = E + 1
MAX_THRESHOLD = 0.125


def groups_of(t):
    return (t + 2) // 2


def blocks_of(t, g):
    return range(2 * g, min(2 * g + 2, t + 1))


def step_stages(s):
    ok = lambda t: 0 <= t < NT
    pv = []
    if ok(s - 1):
        n = groups_of(s - 1)
        pv = [("T", s - 1, 0)]
        for g in range(1, n):
            pv.append(("T", s - 1, g))
            pv.append(("PV", s - 1, g - 1))
        pv.append(("PV", s - 1, n - 1))
    half = max(3, (len(pv) // 4) * 2 + 1)
    stages = pv[:1]
    stages += [("scores", s, 0)] * ok(s)
    stages += [("O", s - 2)] * ok(s - 2)
    stages += [("gate", s - 4)] * ok(s - 4)
    stages += pv[1:2]
    stages += [("softmax", s, 0)] * ok(s)
    stages += [("Y", s - 2)] * ok(s - 2)
    stages += pv[2:3]
    stages += [("qkv", s + 1)] * ok(s + 1)
    stages += [("norm", s)] * (ok(s + 3) or ok(s - 2))
    stages += pv[3:half]
    stages += [("rope", s + 1)] * ok(s + 1)
    stages += [("scores", s, 1)] * ok(s)
    stages += [("normT", s)] * (ok(s + 2) or ok(s - 3))
    stages += pv[half:half + 4]
    stages += [("softmax", s, 1)] * ok(s)
    stages += [("hT", s + 2)] * ok(s + 2)
    stages += [("h2", s - 3)] * ok(s - 3)
    stages += [("xn", s)] * (ok(s + 3) or ok(s - 2))
    stages += [("rotT", s + 1)] * ok(s + 1)
    stages += pv[half + 4:]
    return [(*stage, 0)[:3] for stage in stages]


PLAN = [stage for s in range(-3, NT + 4) for stage in step_stages(s)]


def count_stages():
    at, total = {}, {}
    for kind, t, g in PLAN:
        total[kind] = total.get(kind, 0) + 1
        at[kind, t, g] = total[kind]
    return at, total


AT, TOTAL = count_stages()


def turns(kinds, banks):
    bank, before, last = {}, {}, [None] * banks
    for n, stage in enumerate(stage for stage in PLAN if stage[0] in kinds):
        bank[stage], before[stage] = n % banks, last[n % banks]
        last[n % banks] = stage
    return bank, before


T_BANK, T_BEFORE = turns(("T", "normT"), 2)
_, M_BEFORE = turns(("qkv", "Y", "rotT"), 1)


def adaln_block(nc, x, wqkvT, woT, wgt, bgt, w1, b1, w2, b2, c, wmod, cos, sin, ident, mask, lo_rows, out):
    xf = x.rearrange("b (t p) d -> p (b t) d", p=P)
    of = out.rearrange("b (t p) d -> p (b t) d", p=P)
    x1_dram = nc.dram_tensor("x1_scratch", [P, TILES, D], F32).ap()

    outer = ExitStack()
    with outer:
        def sem(name):
            return outer.enter_context(nc.semaphore(name))

        def psum(name, shape):
            return outer.enter_context(nc.psum_tensor(name, shape, F32))

        def keep(name, shape, dt=F32):
            return outer.enter_context(nc.sbuf_tensor(name, shape, dt))

        score_ps = psum("score_ps", [P, 4, 512])
        tr_ps = psum("tr_ps", [P, 2, 512])
        o_ps = psum("o_ps", [P, 512])
        m_ps = psum("m_ps", [P, 512])

        h2_hi = keep("h2_hi", [P, KD, TILES * P], F32R)
        h2_lo = keep("h2_lo", [P, KD, TILES * P], F32R)
        w1_raw = keep("w1_raw", [P, KD, FF])
        ident_sb = keep("ident_sb", [P, P])
        logits = keep("logits", [P, TILES, NG])
        gates = keep("gates", [P, TILES, E])
        gb_rows = keep("gb_rows", [P, B, D])
        b1_cols = keep("b1_cols", [P, E * FT])

        s_ld = [sem(f"s_ld{i}") for i in range(14)]
        (l_ident, l_c, l_wmod, l_wqkv, l_wo, l_cos, l_sin, l_mask, l_wgt, l_bgt, l_b1, l_w1, l_b2, l_lor) = s_ld
        s_x = [sem(f"s_x{i}") for i in range(XS)]
        s_st = [sem(f"s_st{i}") for i in range(2)]
        s_pre_e = sem("s_pre_e")
        s_pre_a = sem("s_pre_a")
        s_pre_d = sem("s_pre_d")
        s_pre_p = sem("s_pre_p")
        s_batch = sem("s_batch")
        pe_scores, pe_T, pe_PV = sem("pe_scores"), sem("pe_T"), sem("pe_PV")
        pe_qkv, pe_rotT, pe_Y, pe_gate = sem("pe_qkv"), sem("pe_rotT"), sem("pe_Y"), sem("pe_gate")
        pe_normT = sem("pe_normT")
        act_exp, act_T, act_O = sem("act_exp"), sem("act_T"), sem("act_O")
        act_hT, act_qkv, act_V = sem("act_hT"), sem("act_qkv"), sem("act_V")
        act_rot, act_h2, act_ln, act_rstd = sem("act_rot"), sem("act_h2"), sem("act_ln"), sem("act_rstd")
        dve_max, dve_negmax = sem("dve_max"), sem("dve_negmax")
        dve_T, dve_O, dve_rot = sem("dve_T"), sem("dve_O"), sem("dve_rot")
        dve_logits, act_hf = sem("dve_logits"), sem("act_hf")
        dve_recip, dve_y0, dve_x1 = sem("dve_recip"), sem("dve_y0"), sem("dve_x1")
        dve_stats, dve_norm = sem("dve_stats"), sem("dve_norm")
        pool_sin, dve_even = sem("pool_sin"), sem("dve_even")
        pool_cos, dve_odd = sem("pool_cos"), sem("dve_odd")
        pool_hT, pool_V, pool_h2 = sem("pool_hT"), sem("pool_V"), sem("pool_h2")
        pool_ln, dve_xn = sem("pool_ln"), sem("dve_xn")
        s_gate = sem("s_gate")
        s_gexp = sem("s_gexp")
        s_b2 = sem("s_b2")
        s_wst, s_wtr, s_wtc, s_init, s_acc = (sem("s_wst"), sem("s_wtr"), sem("s_wtc"),
                                              sem("s_init"), sem("s_acc"))
        s_first1, s_first2 = sem("s_first1"), sem("s_first2")
        l_w2 = sem("l_w2")
        split_chain, w_split = sem("split_chain"), sem("w_split")
        up_done, up_free, lo_done, h_free = sem("up_done"), sem("up_free"), sem("lo_done"), sem("h_free")
        g_done = sem("g_done")
        down_done, dve_first, dve_evict = sem("down_done"), sem("dve_first"), sem("dve_evict")
        act_evict, pool_first, pool_evict = sem("act_evict"), sem("pool_first"), sem("pool_evict")
        pool_scaled, pool_out = sem("pool_scaled"), sem("pool_out")
        l_x1 = [sem(f"l_x1_{i}") for i in range(2)]
        s_out = [sem(f"s_out{i}") for i in range(2)]

        def wait_alone(eng, *waits):
            waits = [(w, v if isinstance(v, int) else eng.to_reg(v)) for w, v in waits]
            eng.wait_ge(l_ident, 16)
            for w in waits:
                eng.wait_ge(*w)

        attention = ExitStack()
        with attention:
            def sb(name, shape, dt=F32):
                return attention.enter_context(nc.sbuf_tensor(name, shape, dt))

            k_hi, k_lo = sb("k_hi", [P, T], F32R), sb("k_lo", [P, T], F32R)
            v_hi, v_lo = sb("v_hi", [P, NT, HS], F32R), sb("v_lo", [P, NT, HS], F32R)
            probs = sb("probs", [P, 2, NH, T])
            wmod_raw = probs[:, 0, :, :].rearrange("p h t -> p (h t)")[:, 0:KD * 6 * D].rearrange(
                "p (k n) -> p k n", k=KD)
            wqkv_raw = probs[:, 1, 0, 0:KD * QKV].rearrange("p (k n) -> p k n", k=KD)
            s_rows = probs[:, 1, 1, 0:KD * B * P].rearrange("p (k b n) -> p k b n", k=KD, b=B)
            gates_raw = probs[:, 1, 1, 1024:2048].rearrange("p (b n) -> p b n", b=B)
            gates_abs = probs[:, 1, 0, 1024:2048].rearrange("p (b n) -> p b n", b=B)
            pT_hi, pT_lo = sb("pT_hi", [P, 2, 512], F32R), sb("pT_lo", [P, 2, 512], F32R)
            cos_sb, sin_sb = sb("cos_sb", [P, NT, HS // 2]), sb("sin_sb", [P, NT, HS // 2])
            wqkv_hi, wqkv_lo = sb("wqkv_hi", [P, KD, QKV], F32R), sb("wqkv_lo", [P, KD, QKV], F32R)
            wo_raw, wo_ga = sb("wo_raw", [P, NH, D]), sb("wo_ga", [P, NH, D])
            wo_hi, wo_lo = sb("wo_hi", [P, NH, D], F32R), sb("wo_lo", [P, NH, D], F32R)
            ga_rows = sb("ga_rows", [P, B, D])
            mask_raw, mask_r, ident_r = sb("mask_raw", [P, P]), sb("mask_r", [P, P], F32R), sb("ident_r", [P, P], F32R)
            wgt_sb = sb("wgt_sb", [P, KD, NG])
            c_cols = sb("c_cols", [P, KD, B])
            c_exp, c_sig, c_rec, s_cols = (sb(n, [P, KD, B]) for n in ("c_exp", "c_sig", "c_rec", "s_cols"))
            mod_cols = sb("mod_cols", [P, B, 4, KD])
            mod_b = sb("mod_b", [P, 4, KD])
            x_sb = sb("x_sb", [P, XS, D])
            x1_sb, y0_sb = sb("x1_sb", [P, 2, D]), sb("y0_sb", [P, D])
            xn = sb("xn", [P, 2, D])
            hf = sb("hf", [P, 2, KD, P])
            hT_hi, hT_lo = sb("hT_hi", [P, KD, P], F32R), sb("hT_lo", [P, KD, P], F32R)
            qkv = sb("qkv", [P, QKV])
            rot_c, rot_s, rot = sb("rot_c", [P, ROT]), sb("rot_s", [P, ROT]), sb("rot", [P, ROT])
            q_hi, q_lo = sb("q_hi", [P, 2, NH * P], F32R), sb("q_lo", [P, 2, NH * P], F32R)
            o_hi, o_lo = sb("o_hi", [P, NH * P], F32R), sb("o_lo", [P, NH * P], F32R)
            top, neg = sb("top", [P, 2]), sb("neg", [P, 2])
            sums, rsums = sb("sums", [P, 4, NH]), sb("rsums", [P, NH])
            stats, mv = sb("stats", [P, 2, 6]), sb("mv", [P, 2, 2])
            var_eps, ln_v, rs0, rs1, rs2, rs3, rstd = (sb(n, [P, 2]) for n in (
                "var_eps", "ln_v", "rs0", "rs1", "rs2", "rs3", "rstd"))

            ok = lambda t: 0 <= t < NT

            def done(sem_, b, kind, t, g=0, times=1, minus=0):
                return (sem_, b * (TOTAL[kind] * times) + AT[kind, t, g] * times - minus)

            def batch_end(eng, b):
                wait_alone(eng, (act_h2, b * NT + NT), (pool_h2, b * NT + NT), (dve_logits, b * NT + NT),
                           (s_st[0], b * (NT // 2 * 16) + NT // 2 * 16), (s_st[1], b * (NT // 2 * 16) + NT // 2 * 16))

            attention_block = ExitStack()
            block = attention_block.enter_context(nc.Block())

            @block.sync
            def _(sp):
                sp.dma_start(ident_sb[:], ident).then_inc(l_ident, 16)
                sp.dma_start(c_cols[:], c).then_inc(l_c, 16)
                sp.dma_start(wmod_raw, wmod.rearrange("(k p) n -> p k n", p=P)).then_inc(l_wmod, 16)
                sp.dma_start(wqkv_raw, wqkvT.rearrange("(k p) n -> p k n", p=P)).then_inc(l_wqkv, 16)
                sp.dma_start(wo_raw[:], woT.rearrange("(h p) n -> p h n", p=P)).then_inc(l_wo, 16)
                sp.dma_start(cos_sb[:], cos.rearrange("(t p) n -> p t n", p=P)).then_inc(l_cos, 16)
                sp.dma_start(sin_sb[:], sin.rearrange("(t p) n -> p t n", p=P)).then_inc(l_sin, 16)
                sp.dma_start(mask_raw[:], mask).then_inc(l_mask, 16)
                sp.dma_start(wgt_sb[:], wgt.rearrange("(k p) n -> p k n", p=P)).then_inc(l_wgt, 16)
                sp.dma_start(b1_cols[:], b1).then_inc(l_b1, 16)
                sp.dma_start(w1_raw[:], w1[0].rearrange("(k p) n -> p k n", p=P)).then_inc(l_w1, 16)
                with sp.Fori(0, B) as b:
                    for t in range(NT + XS):
                        if t >= XS:
                            sp.wait_ge(*done(dve_x1, b, "Y", t - XS))
                            sp.dma_start(x1_dram[:, bass.ds(b * NT + (t - XS), 1), :],
                                         x1_sb[:, (t - XS) % 2:(t - XS) % 2 + 1, :]).then_inc(s_st[t % 2], 16)
                        if t < NT:
                            sp.dma_start(x_sb[:, t % XS:t % XS + 1, :],
                                         xf[:, bass.ds(b * NT + t, 1), :]).then_inc(s_x[t % XS], 16)
                    batch_end(sp, b)

            def x_loaded(b, t):
                per = len(range(t % XS, NT, XS))
                return s_x[t % XS], b * (per * 16) + (t // XS + 1) * 16

            @block.tensor
            def _(pe):
                pe.wait_ge(l_wmod, 16)
                pe.wait_ge(s_pre_d, 4)
                for m, part in enumerate((1, 0, 4, 3)):
                    for j in range(KD):
                        for k in range(KD):
                            last = nc.tensor.matmul(m_ps[:, (m * KD + j) * B:(m * KD + j + 1) * B],
                                                    wmod_raw[:, k, part * D + j * P:part * D + (j + 1) * P],
                                                    s_cols[:, k, :], start=(k == 0), stop=(k == KD - 1))
                last.then_inc(s_pre_e, 1)
                for b in range(B):
                    for n, part in enumerate((2, 5)):
                        for k in range(KD):
                            last = nc.tensor.matmul(score_ps[:, b, n * D:(n + 1) * D], s_rows[:, k, b, :],
                                                    wmod_raw[:, k, part * D:(part + 1) * D],
                                                    start=(k == 0), stop=(k == KD - 1))
                last.then_inc(s_pre_e, 1)
                pe.wait_ge(s_pre_p, 2)
                pe.wait_ge(l_wgt, 16)

                def m_bank_free(b, stage):
                    was = M_BEFORE[stage]
                    if was:
                        reader = {"qkv": act_V, "Y": dve_x1, "rotT": dve_rot}[was[0]]
                        pe.wait_ge(*done(reader, b, *was))

                def t_bank_free(b, stage):
                    was = T_BEFORE[stage]
                    if was:
                        pe.wait_ge(*done(dve_T if was[0] == "T" else act_hf, b, *was))

                with pe.Fori(0, B) as b:
                    pe.wait_ge(s_batch, b * 4 + 4)
                    for stage in PLAN:
                        kind, t, g = stage
                        if kind == "scores":
                            if g == 0:
                                pe.wait_ge(*done(act_rot, b, "rotT", t, 0, 2))
                                pe.wait_ge(*done(dve_rot, b, "rotT", t))
                            if (t, g) != (0, 0):
                                pe.wait_ge(*done(act_exp, b, "softmax", *((t, 0) if g else (t - 1, 1))))
                            L = (t + 1) * P
                            q1, q2 = (q[:, t % 2, g * P:(g + 1) * P] for q in (q_hi, q_lo))
                            for c0 in range(0, L, 512):
                                w = min(512, L - c0)
                                o = score_ps[:, c0 // 512, 0:w]
                                diag = c0 + w == L
                                nc.tensor.matmul(o, q1, k_hi[:, c0:c0 + w], start=True, stop=False)
                                nc.tensor.matmul(o, q1, k_lo[:, c0:c0 + w], start=False, stop=False)
                                last = nc.tensor.matmul(o, q2, k_hi[:, c0:c0 + w], start=False, stop=not diag)
                                if diag:
                                    last = nc.tensor.matmul(score_ps[:, c0 // 512, w - P:w], ident_r[:],
                                                            mask_r[:], start=False, stop=True)
                            last.then_inc(pe_scores, 1)
                        elif kind == "T":
                            if g == 0:
                                pe.wait_ge(*done(act_exp, b, "softmax", t, 1))
                            t_bank_free(b, stage)
                            for j in blocks_of(t, g):
                                for h in range(NH):
                                    c0 = ((j % 2) * NH + h) * P
                                    last = nc.tensor.transpose(tr_ps[:, T_BANK[stage], c0:c0 + P],
                                                               probs[:, t % 2, h, j * P:(j + 1) * P], ident_sb[:])
                            last.then_inc(pe_T, 1)
                        elif kind == "PV":
                            slot = AT["T", t, g] % 2
                            pe.wait_ge(*done(dve_T, b, "T", t, g))
                            if g == 0:
                                if t > 0:
                                    pe.wait_ge(*done(dve_O, b, "O", t - 1))
                                if ok(t - 3):
                                    pe.wait_ge(*done(dve_logits, b, "gate", t - 3))
                                pe.wait_ge(*done(act_V, b, "qkv", t))
                                pe.wait_ge(*done(pool_V, b, "qkv", t))
                            o = o_ps[:, 0:NH * P]
                            for j in blocks_of(t, g):
                                r = slice((j % 2) * NH * P, (j % 2 + 1) * NH * P)
                                nc.tensor.matmul(o, v_hi[:, j, :], pT_hi[:, slot, r], start=(j == 0), stop=False)
                                nc.tensor.matmul(o, v_hi[:, j, :], pT_lo[:, slot, r], start=False, stop=False)
                                last = nc.tensor.matmul(o, v_lo[:, j, :], pT_hi[:, slot, r], start=False,
                                                        stop=(j == t))
                            last.then_inc(pe_PV, 1)
                        elif kind == "gate":
                            if ok(t + 2):
                                pe.wait_ge(*done(dve_O, b, "O", t + 2))
                            elif ok(t - 1):
                                pe.wait_ge(*done(dve_logits, b, "gate", t - 1))
                            pe.wait_ge(*done(act_hf, b, "normT", t + 3))
                            for k in range(KD):
                                last = nc.tensor.matmul(o_ps[:, NH * P:NH * P + NG], hf[:, 1, k, :],
                                                        wgt_sb[:, k, :], start=(k == 0), stop=(k == KD - 1))
                            last.then_inc(pe_gate, 1)
                        elif kind == "qkv":
                            pe.wait_ge(*done(act_hT, b, "hT", t))
                            pe.wait_ge(*done(pool_hT, b, "hT", t))
                            m_bank_free(b, stage)
                            n = 0
                            for k in range(KD):
                                for a, w in ((hT_hi, wqkv_hi), (hT_hi, wqkv_lo), (hT_lo, wqkv_hi)):
                                    last = nc.tensor.matmul(m_ps[:], a[:, k, :], w[:, k, :], start=(n == 0),
                                                            stop=(n == 3 * KD - 1))
                                    n += 1
                            last.then_inc(pe_qkv, 1)
                        elif kind == "Y":
                            pe.wait_ge(*done(dve_O, b, "O", t))
                            m_bank_free(b, stage)
                            for h in range(NH):
                                for n, (a, w) in enumerate(((o_hi, wo_hi), (o_hi, wo_lo), (o_lo, wo_hi))):
                                    last = nc.tensor.matmul(m_ps[:, h * D:(h + 1) * D], a[:, h * P:(h + 1) * P],
                                                            w[:, h, :], start=(n == 0), stop=(n == 2))
                            last.then_inc(pe_Y, 1)
                        elif kind == "rotT":
                            pe.wait_ge(*done(dve_even, b, "rope", t))
                            pe.wait_ge(*done(dve_odd, b, "rope", t))
                            m_bank_free(b, stage)
                            for h in range(NH + 1):
                                last = nc.tensor.transpose(m_ps[:, h * P:(h + 1) * P], rot[:, h * P:(h + 1) * P],
                                                           ident_sb[:])
                            last.then_inc(pe_rotT, 1)
                        elif kind == "normT":
                            pe.wait_ge(*done(dve_xn, b, "xn", t - 1))
                            t_bank_free(b, stage)
                            for i, tile in enumerate((t + 2, t - 3)):
                                if ok(tile):
                                    for k in range(KD):
                                        c0 = (i * KD + k) * P
                                        last = nc.tensor.transpose(tr_ps[:, T_BANK[stage], c0:c0 + P],
                                                                   xn[:, i, k * P:(k + 1) * P], ident_sb[:])
                            last.then_inc(pe_normT, 1)
                    batch_end(pe, b)

            @block.scalar
            def _(act):
                act.preload_act_table_set("natural_log_exp_and_others")
                act.wait_ge(l_c, 16)
                nc.scalar.activation(c_exp[:], c_cols[:], ACT.Exp, scale=-1.0).then_inc(s_pre_a, 1)
                with act.Fori(0, B) as b:
                    for kind, t, g in PLAN:
                        if kind == "softmax":
                            act.wait_ge(*done(dve_negmax, b, "softmax", t, g))
                            if ok(t - 2):
                                act.wait_ge(*done(pe_PV, b, "PV", t - 2, groups_of(t - 2) - 1))
                            elif t == 0 and g == 0:
                                act.wait_ge(s_batch, b * 4 + 4)
                            L = (t + 1) * P
                            nc.scalar.activation(probs[:, t % 2, g, 0:L],
                                                 score_ps[:].rearrange("p c n -> p (c n)")[:, 0:L], ACT.Exp,
                                                 bias=neg[:, g:g + 1], scale=SCALE,
                                                 accum_out=sums[:, t % 4, g:g + 1]).then_inc(act_exp, 1)
                        elif kind == "T":
                            n = len(blocks_of(t, g)) * NH * P
                            slot = AT["T", t, g] % 2
                            act.wait_ge(*done(pe_T, b, "T", t, g))
                            before = AT["T", t, g] - 2
                            if before >= 1:
                                act.wait_ge(pe_PV, b * TOTAL["PV"] + before)
                            nc.scalar.activation(pT_hi[:, slot, 0:n], tr_ps[:, T_BANK[kind, t, g], 0:n],
                                                 ACT.Copy).then_inc(act_T, 1)
                        elif kind == "O":
                            act.wait_ge(*done(pe_PV, b, "PV", t, groups_of(t) - 1))
                            if t > 0:
                                act.wait_ge(*done(pe_Y, b, "Y", t - 1))
                            nc.scalar.activation(o_hi[:], o_ps[:, 0:NH * P], ACT.Copy).then_inc(act_O, 1)
                        elif kind == "hT":
                            act.wait_ge(*done(act_hf, b, "normT", t - 2))
                            if t > 0:
                                act.wait_ge(*done(pe_qkv, b, "qkv", t - 1))
                            nc.scalar.activation(hT_hi[:], hf[:, 0, :, :], ACT.Copy).then_inc(act_hT, 1)
                        elif kind == "qkv":
                            act.wait_ge(*done(pe_qkv, b, "qkv", t))
                            if t > 0:
                                act.wait_ge(*done(pool_cos, b, "rope", t - 1))
                                act.wait_ge(*done(pool_sin, b, "rope", t - 1))
                                act.wait_ge(*done(pool_V, b, "qkv", t - 1))
                            nc.scalar.activation(qkv[:], m_ps[:], ACT.Copy).then_inc(act_qkv, 1)
                            nc.scalar.activation(v_hi[:, t, :], m_ps[:, ROT:QKV], ACT.Copy).then_inc(act_V, 1)
                        elif kind == "norm":
                            act.wait_ge(*done(pool_ln, b, "norm", t, 0, 5, 4))
                            nc.scalar.activation(ln_v[:], var_eps[:], ACT.Ln).then_inc(act_ln, 1)
                            act.wait_ge(*done(act_ln, b, "norm", t))
                            nc.scalar.activation(rs0[:], ln_v[:], ACT.Exp, scale=-0.5).then_inc(act_rstd, 1)
                        elif kind == "rotT":
                            act.wait_ge(*done(pe_rotT, b, "rotT", t))
                            if ok(t - 2):
                                act.wait_ge(*done(pe_scores, b, "scores", t - 2, 1))
                            nc.scalar.activation(q_hi[:, t % 2, :], m_ps[:, 0:NH * P],
                                                 ACT.Copy).then_inc(act_rot, 1)
                            nc.scalar.activation(k_hi[:, t * P:(t + 1) * P], m_ps[:, NH * P:ROT],
                                                 ACT.Copy).then_inc(act_rot, 1)
                        elif kind == "normT":
                            act.wait_ge(*done(pe_normT, b, "normT", t))
                            if ok(t + 1):
                                act.wait_ge(*done(pool_hT, b, "hT", t + 1))
                            if ok(t - 4):
                                act.wait_ge(*done(pool_h2, b, "h2", t - 4))
                                act.wait_ge(*done(pe_gate, b, "gate", t - 4))
                            if t == -2:
                                act.wait_ge(s_batch, b * 4 + 4)
                            for i, tile in enumerate((t + 2, t - 3)):
                                if ok(tile):
                                    for k in range(KD):
                                        c0 = (i * KD + k) * P
                                        last = nc.scalar.activation(
                                            hf[:, i, k, :], tr_ps[:, T_BANK[kind, t, g], c0:c0 + P], ACT.Identity,
                                            scale=mod_b[:, 2 * i, k:k + 1], bias=mod_b[:, 2 * i + 1, k:k + 1])
                            last.then_inc(act_hf, 1)
                        elif kind == "h2":
                            wait_alone(act, done(act_hf, b, "normT", t + 3))
                            nc.scalar.activation(h2_hi[:, :, bass.ds(b * T + t * P, P)], hf[:, 1, :, :],
                                                 ACT.Copy).then_inc(act_h2, 1)
                    batch_end(act, b)

            @block.vector
            def _(dve):
                made = [0]

                def step(ins):
                    made[0] += 1
                    ins.then_inc(s_pre_d, 1)
                    dve.wait_ge(s_pre_d, made[0])

                dve.wait_ge(s_pre_a, 1)
                step(nc.vector.tensor_scalar_add(c_sig[:], c_exp[:], 1.0))
                step(nc.vector.reciprocal(c_rec[:], c_sig[:]))
                step(nc.vector.tensor_tensor(s_cols[:], c_cols[:], c_rec[:], ALU.mult))
                step(nc.vector.tensor_copy(s_rows, s_cols[:].unsqueeze(3).broadcast_to([P, KD, B, P])))
                dve.wait_ge(l_ident, 16)
                step(nc.vector.tensor_copy(ident_r[:], ident_sb[:]))
                dve.wait_ge(l_mask, 16)
                step(nc.vector.tensor_copy(mask_r[:], mask_raw[:]))
                step(nc.vector.memset(mv[:], 0.0))
                dve.wait_ge(s_pre_e, 1)
                step(nc.vector.tensor_copy(mod_cols[:].rearrange("p b m j -> p (m j) b"),
                                           m_ps[:, 0:4 * KD * B].rearrange("p (n b) -> p n b", b=B)))
                step(nc.vector.tensor_scalar_add(mod_cols[:, :, 0, :], mod_cols[:, :, 0, :], 1.0))
                step(nc.vector.tensor_scalar_add(mod_cols[:, :, 2, :], mod_cols[:, :, 2, :], 1.0))
                dve.wait_ge(s_pre_e, 2)
                step(nc.vector.tensor_copy(gates_raw, score_ps[:, 0:B, :]))
                step(nc.vector.scalar_tensor_tensor(gates_abs, gates_raw, -1.0, gates_raw, ALU.mult, ALU.max))
                step(nc.vector.tensor_scalar(gates_abs, gates_abs, 0.25, None, ALU.max))
                step(nc.vector.tensor_scalar(gates_raw, gates_raw, 0.0, 2.0, ALU.is_ge, ALU.mult))
                step(nc.vector.scalar_tensor_tensor(ga_rows[:], gates_raw[:, :, 0:D], 1.0, gates_abs[:, :, 0:D],
                                                    ALU.subtract, ALU.mult))
                step(nc.vector.scalar_tensor_tensor(gb_rows[:], gates_raw[:, :, D:2 * D], 1.0,
                                                    gates_abs[:, :, D:2 * D], ALU.subtract, ALU.mult))
                dve.wait_ge(l_wo, 16)
                with dve.Fori(0, B) as b:
                    nc.vector.tensor_copy(mod_b[:].unsqueeze(1), mod_cols[:, bass.ds(b, 1), :, :]).then_inc(s_batch, 1)
                    nc.vector.tensor_tensor(wo_ga[:], wo_raw[:],
                                            ga_rows[:, bass.ds(b, 1), :].broadcast_to([P, NH, D]),
                                            ALU.mult).then_inc(s_batch, 1)
                    dve.wait_ge(s_batch, b * 4 + 2)
                    nc.vector.tensor_copy(wo_hi[:], wo_ga[:]).then_inc(s_batch, 1)
                    dve.wait_ge(s_batch, b * 4 + 3)
                    nc.vector.tensor_tensor(wo_lo[:], wo_ga[:], wo_hi[:].bitcast(F32),
                                            ALU.subtract).then_inc(s_batch, 1)
                    dve.wait_ge(s_batch, b * 4 + 4)
                    for kind, t, g in PLAN:
                        if kind == "softmax":
                            dve.wait_ge(*done(pe_scores, b, "scores", t, g))
                            L = (t + 1) * P
                            nc.vector.reduce_max(top[:, g:g + 1],
                                                 score_ps[:].rearrange("p c n -> p (c n)")[:, 0:L],
                                                 axis=AX_X).then_inc(dve_max, 1)
                            dve.wait_ge(*done(dve_max, b, "softmax", t, g))
                            nc.vector.tensor_scalar(neg[:, g:g + 1], top[:, g:g + 1], -SCALE, None,
                                                    ALU.mult).then_inc(dve_negmax, 1)
                        elif kind == "T":
                            n = len(blocks_of(t, g)) * NH * P
                            slot = AT["T", t, g] % 2
                            dve.wait_ge(*done(act_T, b, "T", t, g))
                            nc.vector.tensor_tensor(pT_lo[:, slot, 0:n], tr_ps[:, T_BANK[kind, t, g], 0:n],
                                                    pT_hi[:, slot, 0:n].bitcast(F32),
                                                    ALU.subtract).then_inc(dve_T, 1)
                        elif kind == "O":
                            dve.wait_ge(*done(act_O, b, "O", t))
                            nc.vector.tensor_tensor(o_lo[:], o_ps[:, 0:NH * P], o_hi[:].bitcast(F32),
                                                    ALU.subtract).then_inc(dve_O, 1)
                        elif kind == "gate":
                            dve.wait_ge(*done(pe_gate, b, "gate", t))
                            nc.vector.tensor_copy(logits[:, bass.ds(b * NT + t, 1), :],
                                                  o_ps[:, NH * P:NH * P + NG].unsqueeze(1)).then_inc(dve_logits, 1)
                        elif kind == "rope":
                            turned = lambda a, eo: a[:, 0:ROT].rearrange("p (h e i) -> p h e i", e=2,
                                                                         i=HS // 2)[:, :, eo, :]
                            dve.wait_ge(*done(pool_cos, b, "rope", t))
                            dve.wait_ge(*done(pool_sin, b, "rope", t))
                            if t > 0:
                                dve.wait_ge(*done(pe_rotT, b, "rotT", t - 1))
                            nc.vector.tensor_tensor(turned(rot, 0), turned(rot_c, 0), turned(rot_s, 1),
                                                    ALU.subtract).then_inc(dve_even, 1)
                            nc.vector.tensor_tensor(turned(rot, 1), turned(rot_c, 1), turned(rot_s, 0),
                                                    ALU.add).then_inc(dve_odd, 1)
                        elif kind == "rotT":
                            dve.wait_ge(*done(act_rot, b, "rotT", t, 0, 2))
                            nc.vector.tensor_tensor(q_lo[:, t % 2, :], m_ps[:, 0:NH * P],
                                                    q_hi[:, t % 2, :].bitcast(F32), ALU.subtract)
                            nc.vector.tensor_tensor(k_lo[:, t * P:(t + 1) * P], m_ps[:, NH * P:ROT],
                                                    k_hi[:, t * P:(t + 1) * P].bitcast(F32),
                                                    ALU.subtract).then_inc(dve_rot, 1)
                        elif kind == "Y":
                            if t > 0:
                                dve.wait_ge(*done(dve_x1, b, "Y", t - 1))
                            nc.vector.reciprocal(rsums[:], sums[:, t % 4, :]).then_inc(dve_recip, 1)
                            dve.wait_ge(*done(dve_recip, b, "Y", t))
                            dve.wait_ge(*done(pe_Y, b, "Y", t))
                            nc.vector.scalar_tensor_tensor(y0_sb[:], m_ps[:, 0:D], rsums[:, 0:1], x_sb[:, t % XS, :],
                                                           ALU.mult, ALU.add).then_inc(dve_y0, 1)
                            dve.wait_ge(*done(dve_y0, b, "Y", t))
                            if t >= 2:
                                dve.wait_ge(*done(dve_xn, b, "xn", t))
                                dve.wait_ge(s_st[t % 2], b * (NT // 2 * 16) + t // 2 * 16)
                            nc.vector.scalar_tensor_tensor(x1_sb[:, t % 2, :], m_ps[:, D:2 * D], rsums[:, 1:2],
                                                           y0_sb[:], ALU.mult, ALU.add).then_inc(dve_x1, 1)
                        elif kind == "norm":
                            s = t
                            if s > -3:
                                dve.wait_ge(*done(dve_xn, b, "xn", s - 1))
                            if ok(s + 3):
                                dve.wait_ge(*x_loaded(b, s + 3))
                                last = nc.vector.bn_stats(stats[:, 0, :], x_sb[:, (s + 3) % XS, :])
                            if ok(s - 2):
                                dve.wait_ge(*done(dve_x1, b, "Y", s - 2))
                                last = nc.vector.bn_stats(stats[:, 1, :], x1_sb[:, s % 2, :])
                            last.then_inc(dve_stats, 1)
                            wait_alone(dve, done(dve_stats, b, "norm", s))
                            for i, tile in enumerate((s + 3, s - 2)):
                                if ok(tile):
                                    last = nc.vector.bn_aggr(mv[:, i, :], stats[:, i, :])
                            last.then_inc(dve_norm, 1)
                        elif kind == "xn":
                            dve.wait_ge(*done(pool_ln, b, "norm", t, 0, 5))
                            if t > -3:
                                dve.wait_ge(*done(pe_normT, b, "normT", t))
                            if ok(t + 3):
                                last = nc.vector.tensor_scalar(xn[:, 0, :], x_sb[:, (t + 3) % XS, :], mv[:, 0, 0:1],
                                                               rstd[:, 0:1], ALU.subtract, ALU.mult)
                            if ok(t - 2):
                                last = nc.vector.tensor_scalar(xn[:, 1, :], x1_sb[:, t % 2, :], mv[:, 1, 0:1],
                                                               rstd[:, 1:2], ALU.subtract, ALU.mult)
                            last.then_inc(dve_xn, 1)
                    batch_end(dve, b)

            @block.gpsimd
            def _(pool):
                pool.wait_ge(l_wqkv, 16)
                nc.gpsimd.tensor_copy(wqkv_hi[:], wqkv_raw).then_inc(s_pre_p, 1)
                pool.wait_ge(s_pre_p, 1)
                nc.gpsimd.tensor_tensor(wqkv_lo[:], wqkv_raw, wqkv_hi[:].bitcast(F32),
                                        ALU.subtract).then_inc(s_pre_p, 1)
                pool.wait_ge(s_pre_p, 2)
                pool.wait_ge(l_cos, 16)
                pool.wait_ge(l_sin, 16)
                with pool.Fori(0, B) as b:
                    for kind, t, g in PLAN:
                        if kind == "hT":
                            pool.wait_ge(*done(act_hT, b, "hT", t))
                            nc.gpsimd.tensor_tensor(hT_lo[:], hf[:, 0, :, :], hT_hi[:].bitcast(F32),
                                                    ALU.subtract).then_inc(pool_hT, 1)
                        elif kind == "qkv":
                            pool.wait_ge(*done(act_V, b, "qkv", t))
                            nc.gpsimd.tensor_tensor(v_lo[:, t, :], qkv[:, ROT:QKV], v_hi[:, t, :].bitcast(F32),
                                                    ALU.subtract).then_inc(pool_V, 1)
                        elif kind == "rope":
                            half = lambda a: a[:, 0:ROT].rearrange("p (n i) -> p n i", i=HS // 2)
                            if t > 0:
                                pool.wait_ge(*done(dve_odd, b, "rope", t - 1))
                            for to, table, made in ((rot_c, cos_sb, pool_cos), (rot_s, sin_sb, pool_sin)):
                                nc.gpsimd.tensor_tensor(half(to), half(qkv),
                                                        table[:, t:t + 1, :].broadcast_to(
                                                            [P, 2 * (NH + 1), HS // 2]),
                                                        ALU.mult).then_inc(made, 1)
                        elif kind == "norm":
                            chain = lambda n: pool.wait_ge(*done(pool_ln, b, "norm", t, 0, 5, 5 - n))
                            chain_alone = lambda n: wait_alone(pool, done(pool_ln, b, "norm", t, 0, 5, 5 - n))
                            wait_alone(pool, done(dve_norm, b, "norm", t))
                            nc.gpsimd.tensor_scalar(var_eps[:], mv[:, :, 1], EPS, None, ALU.add).then_inc(pool_ln, 1)
                            pool.wait_ge(*done(act_rstd, b, "norm", t))
                            nc.gpsimd.tensor_tensor(rs1[:], rs0[:], rs0[:], ALU.mult).then_inc(pool_ln, 1)
                            chain(2)
                            nc.gpsimd.tensor_tensor(rs2[:], rs1[:], var_eps[:], ALU.mult).then_inc(pool_ln, 1)
                            chain_alone(3)
                            nc.gpsimd.tensor_scalar(rs3[:], rs2[:], -0.5, 1.5, ALU.mult, ALU.add).then_inc(pool_ln, 1)
                            chain(4)
                            if t > -3:
                                pool.wait_ge(*done(dve_xn, b, "xn", t - 1))
                            nc.gpsimd.tensor_tensor(rstd[:], rs0[:], rs3[:], ALU.mult).then_inc(pool_ln, 1)
                        elif kind == "h2":
                            wait_alone(pool, done(act_h2, b, "h2", t))
                            tok = bass.ds(b * T + t * P, P)
                            nc.gpsimd.tensor_tensor(h2_lo[:, :, tok], hf[:, 1, :, :], h2_hi[:, :, tok].bitcast(F32),
                                                    ALU.subtract).then_inc(pool_h2, 1)
                    batch_end(pool, b)

            attention_block.close()

        mixture = ExitStack()
        with mixture:
            def mx(name, shape, dt=F32, ctx=mixture):
                return ctx.enter_context(nc.sbuf_tensor(name, shape, dt))

            w1_hi = [mx(f"w1_hi{i}", [P, KD, FF], F32R) for i in range(2)]
            w1_lo = [mx(f"w1_lo{i}", [P, KD, FF], F32R) for i in range(2)]
            w2_raw = mx("w2_raw", [P, FT, D])
            acc = mx("acc", [P, TILES, D])
            h_hi, h_lo = mx("h_hi", [P, 4, UTOK], F32R), mx("h_lo", [P, 4, UTOK], F32R)
            g_sb = mx("g_sb", [P, 2, UTOK])
            y_sb = mx("y_sb", [P, 2, 2 * D])
            w2_both = [mx("w2_both0", [P, FT, 2, D], F32R)]

            start = ExitStack()
            with start:
                b2_raw, b2_low = (mx(n, [P, UNIT * D], F32, start) for n in ("b2_raw", "b2_low"))
                b2_all = mx("b2_all", [P, UNIT * D], F32R, start)
                lo_cols = mx("lo_cols", [P, 2], F32, start)
                bgt_sb = mx("bgt_sb", [P, NG], F32, start)
                ge0, ge1 = mx("ge0", [P, TILES, E], F32, start), mx("ge1", [P, TILES, E], F32, start)
                gt = [mx(f"gt{i}", [P, TILES], F32, start) for i in range(5)]
                w_hi, w_lo = mx("w_hi", [P, TILES, E], F32R, start), mx("w_lo", [P, TILES, E], F32R, start)
                w_stack = mx("w_stack", [P, UNIT, 4, E], F32, start)
                w_T = mx("w_T", [P, P], F32R, start)

                with nc.Block() as block:
                    @block.sync
                    def _(sp):
                        sp.dma_start(w2_raw[:], w2[0].rearrange("(f p) n -> p f n", p=P)).then_inc(l_w2, 16)
                        sp.dma_start(bgt_sb[:], bgt.partition_broadcast(P)).then_inc(l_bgt, 16)
                        sp.dma_start(lo_cols[:], lo_rows).then_inc(l_lor, 16)
                        sp.wait_ge(s_b2, 1)
                        for j in range(UNIT):
                            for r in range(3):
                                p0 = j * 4 * E + r * E
                                sp.dma_start(b2_raw[p0:p0 + E, j * D:(j + 1) * D], b2).then_inc(l_b2, 16)
                        sp.wait_ge(s_first1, 2)
                        sp.dma_start(w1_raw[:], w1[1].rearrange("(k p) n -> p k n", p=P)).then_inc(l_w1, 16)
                        sp.wait_ge(s_first2, 2)
                        sp.dma_start(w2_raw[:], w2[1].rearrange("(f p) n -> p f n", p=P)).then_inc(l_w2, 16)
                        sp.wait_ge(l_w1, 32)
                        sp.wait_ge(l_w2, 32)

                    @block.gpsimd
                    def _(pool):
                        nc.gpsimd.memset(b2_raw[:], 0.0).then_inc(s_b2, 1)
                        pool.wait_ge(l_w2, 16)
                        nc.gpsimd.tensor_copy(w2_both[0][:, :, 0, :], w2_raw[:]).then_inc(s_first2, 1)
                        pool.wait_ge(s_first2, 1)
                        nc.gpsimd.tensor_tensor(w2_both[0][:, :, 1, :], w2_raw[:],
                                                w2_both[0][:, :, 0, :].bitcast(F32),
                                                ALU.subtract).then_inc(s_first2, 1)

                    @block.scalar
                    def _(act):
                        act.wait_ge(l_w1, 16)
                        nc.scalar.activation(w1_hi[0][:], w1_raw[:], ACT.Copy).then_inc(s_first1, 1)
                        act.wait_ge(s_gate, 3)
                        nc.scalar.activation(ge1[:], ge0[:], ACT.Exp).then_inc(s_gexp, 1)
                        nc.scalar.activation(gt[1][:], logits[:, :, E], ACT.Exp, scale=-1.0).then_inc(s_gexp, 1)
                        for q in range(UNITS):
                            act.wait_ge(s_wtr, q + 1)
                            if q:
                                act.wait_ge(s_init, q)
                            nc.scalar.activation(w_T[:], tr_ps[:, 0, 0:P], ACT.Copy).then_inc(s_wtc, 1)

                    @block.vector
                    def _(dve):
                        made = [0]

                        def step(ins):
                            made[0] += 1
                            ins.then_inc(s_gate, 1)
                            dve.wait_ge(s_gate, made[0])

                        wide = lambda a: a[:].unsqueeze(2).broadcast_to([P, TILES, E])
                        dve.wait_ge(l_bgt, 16)
                        step(nc.vector.tensor_tensor(logits[:], logits[:],
                                                     bgt_sb[:].unsqueeze(1).broadcast_to([P, TILES, NG]), ALU.add))
                        step(nc.vector.reduce_max(gt[0][:], logits[:, :, 0:E], axis=AX_X))
                        step(nc.vector.tensor_tensor(ge0[:], logits[:, :, 0:E], wide(gt[0]), ALU.subtract))
                        dve.wait_ge(s_gexp, 2)
                        step(nc.vector.reduce_sum(gt[2][:], ge1[:], axis=AX_X))
                        step(nc.vector.reciprocal(gt[3][:], gt[2][:]))
                        step(nc.vector.tensor_tensor(ge0[:], ge1[:], wide(gt[3]), ALU.mult))
                        step(nc.vector.tensor_scalar_add(gt[2][:], gt[1][:], 1.0))
                        step(nc.vector.reciprocal(gt[3][:], gt[2][:]))
                        step(nc.vector.tensor_scalar(gt[4][:], gt[3][:], MAX_THRESHOLD, None, ALU.mult))
                        step(nc.vector.tensor_tensor(ge1[:], ge0[:], wide(gt[4]), ALU.subtract))
                        step(nc.vector.scalar_tensor_tensor(ge0[:], ge1[:], 0.0, ge1[:], ALU.is_ge, ALU.mult))
                        step(nc.vector.reduce_sum(gt[0][:], ge0[:], axis=AX_X))
                        step(nc.vector.scalar_tensor_tensor(gt[2][:], gt[0][:], 0.0, gt[0][:], ALU.is_equal, ALU.add))
                        step(nc.vector.reciprocal(gt[3][:], gt[2][:]))
                        step(nc.vector.tensor_tensor(gates[:], ge0[:], wide(gt[3]), ALU.mult))
                        step(nc.vector.tensor_copy(w_hi[:], gates[:]))
                        step(nc.vector.tensor_tensor(w_lo[:], gates[:], w_hi[:].bitcast(F32), ALU.subtract))
                        step(nc.vector.memset(w_stack[:], 0.0))
                        dve.wait_ge(l_b2, 16 * 3 * UNIT)
                        dve.wait_ge(l_lor, 16)
                        step(nc.vector.tensor_copy(b2_all[:], b2_raw[:]))
                        step(nc.vector.tensor_tensor(b2_low[:], b2_raw[:], b2_all[:].bitcast(F32), ALU.subtract))
                        step(nc.vector.tensor_scalar(b2_low[:], b2_low[:], lo_cols[:, 0:1], None, ALU.mult))
                        step(nc.vector.scalar_tensor_tensor(b2_all[:], b2_all[:].bitcast(F32), lo_cols[:, 1:2],
                                                            b2_low[:], ALU.mult, ALU.add))
                        for q in range(UNITS):
                            if q:
                                dve.wait_ge(s_wtr, q)
                            four = slice(q * UNIT, (q + 1) * UNIT)
                            nc.vector.tensor_copy(w_stack[:, :, 0, :], w_hi[:, four, :].bitcast(F32))
                            nc.vector.tensor_copy(w_stack[:, :, 1, :], w_hi[:, four, :].bitcast(F32))
                            nc.vector.tensor_copy(w_stack[:, :, 2, :],
                                                  w_lo[:, four, :].bitcast(F32)).then_inc(s_wst, 1)
                            dve.wait_ge(s_init, q + 1)
                            nc.vector.tensor_copy(acc[:, four, :].rearrange("p (a t) d -> p a (t d)", a=2),
                                                  score_ps[:, 0:2, :]).then_inc(s_acc, 1)
                        dve.wait_ge(s_first1, 1)
                        nc.vector.tensor_tensor(w1_lo[0][:], w1_raw[:], w1_hi[0][:].bitcast(F32),
                                                ALU.subtract).then_inc(s_first1, 1)

                    @block.tensor
                    def _(pe):
                        pe.wait_ge(s_gate, 22)
                        for q in range(UNITS):
                            pe.wait_ge(s_wst, q + 1)
                            if q:
                                pe.wait_ge(s_wtc, q)
                            nc.tensor.transpose(tr_ps[:, 0, 0:P], w_stack[:].rearrange("p a b c -> p (a b c)"),
                                                ident_sb[:]).then_inc(s_wtr, 1)
                            pe.wait_ge(s_wtc, q + 1)
                            if q:
                                pe.wait_ge(s_acc, q)
                            for i in range(2):
                                last = nc.tensor.matmul(score_ps[:, i, :], w_T[:], b2_all[:, i * 512:(i + 1) * 512],
                                                        start=True, stop=True)
                            last.then_inc(s_init, 1)

            w2_both.append(mx("w2_both1", [P, FT, 2, D], F32R))
            up_ps = [score_ps[:, i, :] for i in range(4)]
            down_ps = [tr_ps[:, 0, :], tr_ps[:, 1, :], o_ps[:], m_ps[:]]
            slabs = [w1_raw[:].rearrange("p k n -> p (k n)")[:, i * UNIT * D:(i + 1) * UNIT * D].rearrange(
                "p (t d) -> p t d", t=UNIT) for i in range(2)]

            def experts(eng, unit):
                def expert(e, par, last):
                    with eng.Fori(0, UNITS - 1) as t:
                        unit(e, par, t, (e, par, t + 1), last)
                    unit(e, par, UNITS - 1, None if last else (e + 1, 1 - par, 0), last)

                with eng.Fori(0, E // 2 - 1) as pair:
                    expert(pair * 2, 0, False)
                    expert(pair * 2 + 1, 1, False)
                expert(E - 2, 0, False)
                expert(E - 1, 1, True)

            def hidden(e, t, f):
                return e * (UNITS * FT) + t * FT + f

            AHEAD = 2

            def gate_of(e, t, j):
                return gates[:].rearrange("p t e -> p (t e)")[:, bass.ds(t * (UNIT * E) + (j * E + e), 1)]

            def wait_slot(eng, e, t, f):
                u = e * UNITS + t
                if f >= 4:
                    wait_alone(eng, (h_free, u * (FT - 1) + (f - 4) + 1 + 3))
                elif f == 3:
                    wait_alone(eng, (down_done, u * UNIT + 1))
                else:
                    wait_alone(eng, (h_free, u * (FT - 1) + f + 1))

            with nc.Block() as block:
                @block.sync
                def _(sp):
                    with sp.Fori(0, E - 2) as e:
                        sp.wait_ge(w_split, (e + 1) * (2 * UNITS))
                        sp.dma_start(w1_raw[:].unsqueeze(1), w1[bass.ds(e + 2, 1)].rearrange(
                            "e (k p) n -> p e k n", p=P)).then_inc(l_w1, 16)
                        sp.dma_start(w2_raw[:].unsqueeze(1), w2[bass.ds(e + 2, 1)].rearrange(
                            "e (f p) n -> p e f n", p=P)).then_inc(l_w2, 16)
                    sp.wait_ge(w_split, (E - 1) * (2 * UNITS))
                    for t in range(UNITS + 1):
                        if t > 0:
                            sp.wait_ge(pool_out, t)
                            sp.dma_start(of[:, (t - 1) * UNIT:t * UNIT, :],
                                         acc[:, (t - 1) * UNIT:t * UNIT, :]).then_inc(s_out[t % 2], 16)
                        if t < UNITS:
                            if t >= 2:
                                sp.wait_ge(pool_out, t - 1)
                            sp.dma_start(slabs[t % 2], x1_dram[:, t * UNIT:(t + 1) * UNIT, :]).then_inc(l_x1[t % 2], 16)
                    for s in s_out:
                        sp.wait_ge(s, UNITS // 2 * 16)

                @block.tensor
                def _(pe):
                    pe.sem_inc(h_free, 3)
                    pe.sem_inc(down_done, 1)

                    def up(e, par, t, f):
                        n = hidden(e, t, f)
                        pe.wait_ge(up_free, n + 1)
                        tok = bass.ds(t * UTOK, UTOK)
                        i = 0
                        for k in range(KD):
                            for w, h in ((w1_hi, h2_hi), (w1_hi, h2_lo), (w1_lo, h2_hi)):
                                last = nc.tensor.matmul(up_ps[f % 4], w[par][:, k, f * P:(f + 1) * P], h[:, k, tok],
                                                        start=(i == 0), stop=(i == 3 * KD - 1))
                                i += 1
                        last.then_inc(up_done, 1)

                    def down(e, par, t, f):
                        n = hidden(e, t, f)
                        pe.wait_ge(lo_done, n + 2 + 1)
                        for j in range(UNIT):
                            if f == 0:
                                u = e * UNITS + t
                                pe.wait_ge(*((dve_evict, 2 * u + j + 1) if j < 2 else (act_evict, 2 * u + j - 1)))
                            tok = slice(j * P, (j + 1) * P)
                            nc.tensor.matmul(down_ps[j], h_hi[:, f % 4, tok],
                                             w2_both[par][:, f, :, :].rearrange("p a d -> p (a d)"),
                                             start=(f == 0), stop=False)
                            last = nc.tensor.matmul(down_ps[j][:, 0:D], h_lo[:, f % 4, tok],
                                                    w2_both[par][:, f, 0, :], start=False, stop=(f == FT - 1))
                            if f == FT - 1:
                                last.then_inc(down_done, 1)
                        if f < FT - 1:
                            last.then_inc(h_free, 1)

                    def unit(e, par, t, following, last):
                        for f in range(FT):
                            if f + AHEAD < FT:
                                up(e, par, t, f + AHEAD)
                            elif following:
                                if following[1] != par and f + AHEAD == FT:
                                    pe.wait_ge(w_split, (e + 1) * (2 * UNITS))
                                up(*following, f + AHEAD - FT)
                            down(e, par, t, f)

                    for f in range(AHEAD):
                        up(0, 0, 0, f)
                    experts(pe, unit)

                @block.scalar
                def _(act):
                    act.sem_inc(up_free, 4)
                    act.sem_inc(act_evict, 2)

                    def gelu(e, par, t, f):
                        n = hidden(e, t, f)
                        wait_alone(act, (up_done, n + 1), (lo_done, n + 1))
                        bias = b1_cols[:, bass.ds(e * FT + f, 1)]
                        nc.scalar.activation(g_sb[:, f % 2, :], up_ps[f % 4], ACT.Gelu_apprx_tanh,
                                             bias=bias).then_inc(g_done, 1)
                        wait_slot(act, e, t, f)
                        nc.scalar.activation(h_hi[:, f % 4, :], up_ps[f % 4], ACT.Gelu_apprx_tanh,
                                             bias=bias).then_inc(up_free, 1)

                    def unit(e, par, t, following, last):
                        for f in range(AHEAD, FT):
                            gelu(e, par, t, f)
                        if following:
                            for f in range(AHEAD):
                                gelu(*following, f)
                        u = e * UNITS + t
                        for j in (2, 3):
                            wait_alone(act, (down_done, u * UNIT + j + 2), (pool_evict, 2 * u + j - 1))
                            nc.scalar.activation(y_sb[:, j - 2, :], down_ps[j], ACT.Copy,
                                                 scale=gate_of(e, t, j)).then_inc(act_evict, 1)

                    for f in range(AHEAD):
                        gelu(0, 0, 0, f)
                    experts(act, unit)

                @block.vector
                def _(dve):
                    dve.sem_inc(lo_done, 2)
                    dve.sem_inc(dve_evict, 2)

                    def low(e, par, t, f):
                        n = hidden(e, t, f)
                        dve.wait_ge(g_done, n + 1)
                        dve.wait_ge(up_free, n + 4 + 1)
                        nc.vector.tensor_tensor(h_lo[:, f % 4, :], g_sb[:, f % 2, :], h_hi[:, f % 4, :].bitcast(F32),
                                                ALU.subtract).then_inc(lo_done, 1)

                    def unit(e, par, t, following, last):
                        for f in range(AHEAD, FT):
                            low(e, par, t, f)
                        if following:
                            for f in range(AHEAD):
                                low(*following, f)
                        u = e * UNITS + t
                        tile = lambda j: acc[:, bass.ds(t * UNIT + j, 1), :]
                        for j in (0, 1):
                            dve.wait_ge(down_done, u * UNIT + j + 2)
                            nc.vector.scalar_tensor_tensor(tile(j), down_ps[j][:, 0:D].unsqueeze(1), gate_of(e, t, j),
                                                           tile(j), ALU.mult, ALU.add).then_inc(dve_first, 1)
                        for j in (0, 1):
                            dve.wait_ge(dve_first, 2 * u + j + 1)
                            nc.vector.scalar_tensor_tensor(tile(j), down_ps[j][:, D:2 * D].unsqueeze(1),
                                                           gate_of(e, t, j), tile(j),
                                                           ALU.mult, ALU.add).then_inc(dve_evict, 1)

                    for f in range(AHEAD):
                        low(0, 0, 0, f)
                    experts(dve, unit)

                @block.gpsimd
                def _(pool):
                    pool.sem_inc(pool_evict, 2)

                    def add(e, t):
                        u = e * UNITS + t
                        tile = lambda j: acc[:, bass.ds(t * UNIT + j, 1), :]
                        for n, sem_, before in ((0, pool_first, act_evict), (1, pool_evict, pool_first)):
                            for j in (2, 3):
                                wait_alone(pool, (before, 2 * u + j - 1 + (2 if n == 0 else 0)))
                                nc.gpsimd.tensor_tensor(tile(j), tile(j),
                                                        y_sb[:, j - 2:j - 1, n * D:(n + 1) * D],
                                                        ALU.add).then_inc(sem_, 1)

                    def split(e, par, t):
                        to = 1 - par
                        cols = bass.ds(t * P, P)
                        row = bass.ds(t, 1)
                        done_ = e * (2 * UNITS) + t * 2
                        nc.gpsimd.tensor_copy(w1_hi[to][:, :, cols], w1_raw[:, :, cols]).then_inc(split_chain, 1)
                        nc.gpsimd.tensor_copy(w2_both[to][:, row, 0, :], w2_raw[:, row, :]).then_inc(split_chain, 1)
                        wait_alone(pool, (split_chain, done_ + 1))
                        nc.gpsimd.tensor_tensor(w1_lo[to][:, :, cols], w1_raw[:, :, cols],
                                                w1_hi[to][:, :, cols].bitcast(F32), ALU.subtract).then_inc(w_split, 1)
                        wait_alone(pool, (split_chain, done_ + 2))
                        nc.gpsimd.tensor_tensor(w2_both[to][:, row, 1, :], w2_raw[:, row, :],
                                                w2_both[to][:, row, 0, :].bitcast(F32),
                                                ALU.subtract).then_inc(w_split, 1)

                    def expert(e, par):
                        wait_alone(pool, (down_done, e * (UNITS * UNIT) + 1), (l_w1, e * 16 + 32), (l_w2, e * 16 + 32))
                        with pool.Fori(0, UNITS) as t:
                            split(e, par, t)
                            add(e, t)

                    with pool.Fori(0, E // 2 - 1) as pair:
                        expert(pair * 2, 0)
                        expert(pair * 2 + 1, 1)
                    expert(E - 2, 0)
                    for b in range(B):
                        with pool.Fori(0, UNITS // B // 2) as half:
                            for i in range(2):
                                t = half * 2 + (b * (UNITS // B) + i)
                                add(E - 1, t)
                                u = (E - 1) * UNITS + t
                                wait_alone(pool, (dve_evict, 2 * u + 2 + 2), (pool_evict, 2 * u + 2 + 2))
                                unit_acc = acc[:, bass.ds(t * UNIT, UNIT), :]
                                nc.gpsimd.tensor_tensor(unit_acc, unit_acc,
                                                        gb_rows[:, b:b + 1, :].broadcast_to([P, UNIT, D]),
                                                        ALU.mult).then_inc(pool_scaled, 1)
                                wait_alone(pool, (pool_scaled, t + 1), (l_x1[i], half * 16 + (b * (UNITS // B // 2) + 1) * 16))
                                nc.gpsimd.tensor_tensor(unit_acc, unit_acc, slabs[i],
                                                        ALU.add).then_inc(pool_out, 1)


def kernel(L0_attn_x, L0_attn_Wq, L0_attn_Wk, L0_attn_Wv, L0_attn_Wo, L0_ffn_Wg, L0_ffn_bg, L0_ffn_Wt, L0_ffn_bt,
           L0_ffn_W1, L0_ffn_b1, L0_ffn_W2, L0_ffn_b2, L0_c, L0_wmod):
    import numpy as np
    import concourse.bacc as bacc
    from concourse.bass_utils import run_bass_kernel_spmd

    A = np.asarray
    order = np.r_[0:HS:2, 1:HS:2]
    heads = [A(L0_attn_Wq)[0][order], A(L0_attn_Wq)[1][order], A(L0_attn_Wk)[order], A(L0_attn_Wv)]
    theta = np.float32(10000.0) ** (np.float32(-2.0) * np.arange(0, HS, 2, dtype=np.float32) / np.float32(HS))
    angles = np.arange(T, dtype=np.float32)[:, None] * theta.astype(np.float32)[None, :]
    rows = np.arange(P)
    mask = np.where(rows[None, :] > rows[:, None], np.float32(-2.0 ** 127), np.float32(0))
    low = (rows % (4 * E) // E == 1).astype(np.float32)
    arrays = {
        "x": A(L0_attn_x),
        "wqkvT": np.concatenate(heads, axis=0).T,
        "woT": A(L0_attn_Wo).T,
        "wgt": np.concatenate([A(L0_ffn_Wg), A(L0_ffn_Wt)], axis=1),
        "bgt": np.concatenate([A(L0_ffn_bg), A(L0_ffn_bt)]),
        "w1": A(L0_ffn_W1),
        "b1": A(L0_ffn_b1).reshape(E * FT, P).T,
        "w2": A(L0_ffn_W2),
        "b2": A(L0_ffn_b2),
        "c": A(L0_c).reshape(B, KD, P).transpose(2, 1, 0),
        "wmod": A(L0_wmod),
        "cos": np.cos(angles.astype(np.float64)).astype(np.float32),
        "sin": np.sin(angles.astype(np.float64)).astype(np.float32),
        "ident": np.eye(P, dtype=np.float32),
        "mask": mask.astype(np.float32),
        "lo_rows": np.stack([low, 1 - low], axis=1),
    }
    arrays = {f"{n}_dram": np.ascontiguousarray(a) for n, a in arrays.items()}
    nc = bacc.Bacc("TRN2", target_bir_lowering=False, num_devices=1)
    args = [nc.dram_tensor(n, a.shape, mybir.dt.from_np(a.dtype), kind="ExternalInput").ap()
            for n, a in arrays.items()]
    args.append(nc.dram_tensor("out_dram", (B, T, D), F32, kind="ExternalOutput").ap())
    adaln_block(nc, *args)
    r = run_bass_kernel_spmd(nc, [arrays], core_ids=[0])
    return r.results[0]["out_dram"]
```

```python
from contextlib import ExitStack

import concourse.bass as bass
from concourse import mybir

F32 = mybir.dt.float32
F32R = mybir.dt.float32r
ALU = mybir.AluOpType
ACT = mybir.ActivationFunctionType
AX_X = mybir.AxisListType.X

P = 128
B, T, D = 2, 2048, 256
HS, NH = 128, 2
E, FF = 8, 1024
KD = D // P
NT = T // P
TILES = B * NT
FT = FF // P
UNIT = 4
UTOK = UNIT * P
UNITS = TILES // UNIT
QKV = (NH + 2) * HS
ROT = (NH + 1) * HS
SCALE = float(HS) ** -0.5
EPS = 1e-5
XS = 6
NG = E + 1
MAX_THRESHOLD = 0.125


def ok(t):
    return 0 <= t < NT


def groups_of(t):
    return (t + 2) // 2


def blocks_of(t, g):
    return range(2 * g, min(2 * g + 2, t + 1))


def chunks_of(t):
    return t // 4 + 1


def stages_by_kind():
    kinds = {k: [(k, t, 0) for t in range(NT)] for k in ("hT", "qkv", "rope", "rotT", "O", "Y", "gate", "h2")}
    kinds.update({k: [(k, s, 0) for s in range(-3, NT + 2)] for k in ("norm", "rstd", "xn")})
    kinds["normT"] = [("normT", s, 0) for s in range(-2, NT + 3)]
    for k in ("S", "M", "E"):
        kinds[k] = [(k, t, 4 * h + c) for t in range(NT) for h in range(NH) for c in range(chunks_of(t))]
    kinds["N"] = [("N", t, h) for t in range(NT) for h in range(NH)]
    for k in ("T", "PV"):
        kinds[k] = [(k, t, g) for t in range(NT) for g in range(groups_of(t))]
    return kinds


STAGES = stages_by_kind()
AT = {stage: n + 1 for stages in STAGES.values() for n, stage in enumerate(stages)}
TOTAL = {kind: len(stages) for kind, stages in STAGES.items()}


def parts_of(stage):
    kind, t, g = stage
    head, chunk = divmod(g, 4)
    w = min(512, (t + 1) * P - chunk * 512)
    if kind == "S":
        was = t if head else t - 1
        after = [("rotT", t, 0, "DVE")]
        if ok(was) and chunk < chunks_of(was):
            after.append(("E", was, (1 - head) * 4 + chunk, "ACT"))
        return [("PE", 1.25 * w + 53 * (chunk == chunks_of(t) - 1), after)]
    if kind == "M":
        return [("DVE", 65 + 1.04 * w, [("S", t, g, "PE")])]
    if kind == "N":
        return [("DVE", 330, [("M", t, g * 4 + chunks_of(t) - 1, "DVE")])]
    if kind == "E":
        return [("ACT", 230 + 0.83 * w, [("N", t, head, "DVE"), ("T", t - 2, groups_of(t - 2) - 1, "PE"),
                                         ("Y", t - 4, 0, "DVE")])]
    if kind == "T":
        n = len(blocks_of(t, g))
        return [("PE", 214 * n, [("E", t, 4 + g // 2, "ACT")]),
                ("ACT", 60 + 210 * n, [("T", t, g, "PE")]),
                ("DVE", 70 + 266 * n, [("T", t, g, "ACT")])]
    if kind == "PV":
        first = [("O", t - 1, 0, "DVE"), ("gate", t - 3, 0, "DVE"), ("qkv", t, 0, "POOL")]
        return [("PE", 320 * len(blocks_of(t, g)), [("T", t, g, "DVE")] + first * (g == 0))]
    if kind == "O":
        return [("ACT", 270, [("PV", t, groups_of(t) - 1, "PE"), ("Y", t - 1, 0, "PE")]),
                ("DVE", 330, [("O", t, 0, "ACT")])]
    if kind == "Y":
        return [("PE", 640, [("O", t, 0, "DVE"), ("xn", t, 0, "DVE")] if t >= 2 else [("O", t, 0, "DVE")]),
                ("DVE", 1350, [("Y", t, 0, "PE")])]
    if kind == "gate":
        return [("PE", 430, [("normT", t + 3, 0, "ACT"), ("O", t + 2, 0, "DVE"), ("gate", t - 1, 0, "DVE")]),
                ("DVE", 80, [("gate", t, 0, "PE")])]
    if kind == "qkv":
        return [("PE", 1280, [("hT", t, 0, "POOL"), ("rope", t - 1, 0, "POOL")]),
                ("ACT", 640, [("qkv", t, 0, "PE"), ("rope", t - 1, 0, "POOL"), ("qkv", t - 1, 0, "POOL")]),
                ("POOL", 420, [("qkv", t, 0, "ACT")])]
    if kind == "rope":
        return [("POOL", 1900, [("qkv", t, 0, "ACT"), ("rope", t - 1, 0, "DVE")]),
                ("DVE", 540, [("rope", t, 0, "POOL"), ("rotT", t - 1, 0, "PE")])]
    if kind == "rotT":
        return [("PE", 320, [("rope", t, 0, "DVE"), ("S", t - 2, 4 + chunks_of(t - 2) - 1, "PE")]),
                ("ACT", 420, [("rotT", t, 0, "PE"), ("S", t - 2, 4 + chunks_of(t - 2) - 1, "PE")]),
                ("DVE", 540, [("rotT", t, 0, "ACT")])]
    n = ok(t + 3) + ok(t - 2)
    if kind == "norm":
        return [("DVE", 410 * n + 200, [("xn", t - 1, 0, "DVE"), ("Y", t - 2, 0, "DVE")]),
                ("POOL", 180, [("norm", t, 0, "DVE")]),
                ("ACT", 330, [("norm", t, 0, "POOL")])]
    if kind == "rstd":
        return [("POOL", 1000, [("norm", t, 0, "ACT"), ("xn", t - 1, 0, "DVE")])]
    if kind == "xn":
        return [("DVE", 330 * n, [("rstd", t, 0, "POOL"), ("normT", t, 0, "PE")])]
    n = ok(t + 2) + ok(t - 3)
    if kind == "normT":
        before = [("hT", t + 1, 0, "POOL"), ("h2", t - 4, 0, "POOL"), ("gate", t - 4, 0, "PE")]
        return [("PE", 214 * n, [("xn", t - 1, 0, "DVE")] + before),
                ("ACT", 685 * n, [("normT", t, 0, "PE")] + before)]
    if kind == "hT":
        return [("ACT", 310, [("normT", t - 2, 0, "ACT"), ("qkv", t - 1, 0, "PE")]),
                ("POOL", 690, [("hT", t, 0, "ACT")])]
    return [("ACT", 310, [("normT", t + 3, 0, "ACT")]), ("POOL", 690, [("h2", t, 0, "ACT")])]


PATIENCE = {'E': 100, 'h2': -200, 'gate': -400, 'qkv': -200, 'normT': -100, 'hT': -300, 'rstd': -1600, 'PV': 300, 'norm': -400, 'rope': 100, 'O': -300, 'xn': 300}
PASS_ON = 150


def order_stages(patience):
    queues, ends, free, orders = {}, {}, {}, {}
    for stages in STAGES.values():
        for stage in stages:
            for engine, length, after in parts_of(stage):
                queues.setdefault((engine, stage[0]), []).append(
                    (stage, length, [x for x in after if x[:3] in AT]))
                free[engine], orders[engine] = 0.0, []
    heads = {q: 0 for q in queues}
    last_in = {"T0": None, "T1": None, "M": None}
    turn = 0
    reader = {"T": "DVE", "normT": "ACT", "qkv": "ACT", "Y": "DVE", "rotT": "DVE"}
    while heads:
        best = None
        for (engine, kind), i in heads.items():
            stage, length, after = queues[engine, kind][i]
            if engine == "PE" and kind in ("T", "normT"):
                bank = f"T{turn % 2}"
            elif engine == "PE" and kind in ("qkv", "Y", "rotT"):
                bank = "M"
            else:
                bank = None
            if bank and last_in[bank]:
                after = after + [(*last_in[bank], reader[last_in[bank][0]])]
            if kind == "T" and engine in ("PE", "ACT") and i >= 2:
                after = after + [(*STAGES["PV"][i - 2], "PE")]
            if any(x not in ends for x in after):
                continue
            start = max([free[engine]] + [ends[x] + (PASS_ON if x[3] != engine else 60) for x in after
                                          if not (engine == "PE" and kind == "T" and x[0] == "PV")])
            rank = (start + patience.get(kind, 0), start)
            if best is None or rank < best[0]:
                best = (rank, engine, kind, stage, start, length, bank)
        _, engine, kind, stage, start, length, bank = best
        ends[(*stage, engine)] = free[engine] = start + length
        orders[engine].append(stage)
        if bank:
            last_in[bank] = stage
            turn += bank != "M"
        heads[engine, kind] += 1
        if heads[engine, kind] == len(queues[engine, kind]):
            del heads[engine, kind]
    return orders, max(free.values())


ORDER, _ = order_stages(PATIENCE)


def turns(kinds, banks):
    bank, before, last = {}, {}, [None] * banks
    for n, stage in enumerate(stage for stage in ORDER["PE"] if stage[0] in kinds):
        bank[stage], before[stage] = n % banks, last[n % banks]
        last[n % banks] = stage
    return bank, before


T_BANK, T_BEFORE = turns(("T", "normT"), 2)
_, M_BEFORE = turns(("qkv", "Y", "rotT"), 1)


def adaln_block(nc, x, wqkvT, woT, wgt, bgt, w1, b1, w2, b2, c, wmod, cos, sin, ident, mask, lo_rows, out):
    xf = x.rearrange("b (t p) d -> p (b t) d", p=P)
    of = out.rearrange("b (t p) d -> p (b t) d", p=P)
    x1_dram = nc.dram_tensor("x1_scratch", [P, TILES, D], F32).ap()

    outer = ExitStack()
    with outer:
        def sem(name):
            return outer.enter_context(nc.semaphore(name))

        def psum(name, shape):
            return outer.enter_context(nc.psum_tensor(name, shape, F32))

        def keep(name, shape, dt=F32):
            return outer.enter_context(nc.sbuf_tensor(name, shape, dt))

        score_ps = psum("score_ps", [P, 4, 512])
        tr_ps = psum("tr_ps", [P, 2, 512])
        o_ps = psum("o_ps", [P, 512])
        m_ps = psum("m_ps", [P, 512])

        h2_hi = keep("h2_hi", [P, KD, TILES * P], F32R)
        h2_lo = keep("h2_lo", [P, KD, TILES * P], F32R)
        w1_raw = keep("w1_raw", [P, KD, FF])
        ident_sb = keep("ident_sb", [P, P])
        logits = keep("logits", [P, TILES, NG])
        gates = keep("gates", [P, TILES, E])
        gb_rows = keep("gb_rows", [P, B, D])
        b1_cols = keep("b1_cols", [P, E * FT])

        s_ld = [sem(f"s_ld{i}") for i in range(14)]
        (l_ident, l_c, l_wmod, l_wqkv, l_wo, l_cos, l_sin, l_mask, l_wgt, l_bgt, l_b1, l_w1, l_b2, l_lor) = s_ld
        s_x = [sem(f"s_x{i}") for i in range(XS)]
        s_st = [sem(f"s_st{i}") for i in range(2)]
        s_pre_e = sem("s_pre_e")
        s_pre_a = sem("s_pre_a")
        s_pre_d = sem("s_pre_d")
        s_pre_p = sem("s_pre_p")
        s_batch = sem("s_batch")
        pe_S, pe_T, pe_PV = sem("pe_S"), sem("pe_T"), sem("pe_PV")
        pe_qkv, pe_rotT, pe_Y, pe_gate = sem("pe_qkv"), sem("pe_rotT"), sem("pe_Y"), sem("pe_gate")
        pe_normT = sem("pe_normT")
        act_E, act_T, act_O = sem("act_E"), sem("act_T"), sem("act_O")
        act_hT, act_qkv, act_V = sem("act_hT"), sem("act_qkv"), sem("act_V")
        act_rot, act_h2, act_ln, act_rstd = sem("act_rot"), sem("act_h2"), sem("act_ln"), sem("act_rstd")
        dve_M, dve_top, dve_N = sem("dve_M"), sem("dve_top"), sem("dve_N")
        dve_sum = sem("dve_sum")
        dve_T, dve_O, dve_rot = sem("dve_T"), sem("dve_O"), sem("dve_rot")
        dve_logits, act_hf = sem("dve_logits"), sem("act_hf")
        dve_recip, dve_y0, dve_x1 = sem("dve_recip"), sem("dve_y0"), sem("dve_x1")
        dve_stats, dve_norm = sem("dve_stats"), sem("dve_norm")
        pool_sin, dve_even = sem("pool_sin"), sem("dve_even")
        pool_cos, dve_odd = sem("pool_cos"), sem("dve_odd")
        pool_hT, pool_V, pool_h2 = sem("pool_hT"), sem("pool_V"), sem("pool_h2")
        pool_var, pool_ln, dve_xn = sem("pool_var"), sem("pool_ln"), sem("dve_xn")
        s_gate = sem("s_gate")
        s_gexp = sem("s_gexp")
        s_b2 = sem("s_b2")
        s_wst, s_wtr, s_wtc, s_init, s_acc = (sem("s_wst"), sem("s_wtr"), sem("s_wtc"),
                                              sem("s_init"), sem("s_acc"))
        s_first1, s_first2 = sem("s_first1"), sem("s_first2")
        l_w2 = sem("l_w2")
        split_chain, w_split = sem("split_chain"), sem("w_split")
        up_done, up_free, lo_done, h_free = sem("up_done"), sem("up_free"), sem("lo_done"), sem("h_free")
        g_done = sem("g_done")
        down_done, dve_first, dve_evict = sem("down_done"), sem("dve_first"), sem("dve_evict")
        act_evict, pool_first, pool_evict = sem("act_evict"), sem("pool_first"), sem("pool_evict")
        pool_scaled, pool_out = sem("pool_scaled"), sem("pool_out")
        l_x1 = [sem(f"l_x1_{i}") for i in range(2)]
        s_out = [sem(f"s_out{i}") for i in range(2)]

        def wait_alone(eng, *waits):
            waits = [(w, v if isinstance(v, int) else eng.to_reg(v)) for w, v in waits]
            eng.wait_ge(l_ident, 16)
            for w in waits:
                eng.wait_ge(*w)

        attention = ExitStack()
        with attention:
            def sb(name, shape, dt=F32):
                return attention.enter_context(nc.sbuf_tensor(name, shape, dt))

            k_hi, k_lo = sb("k_hi", [P, T], F32R), sb("k_lo", [P, T], F32R)
            v_hi, v_lo = sb("v_hi", [P, NT, HS], F32R), sb("v_lo", [P, NT, HS], F32R)
            probs = sb("probs", [P, 2, NH, T])
            wmod_raw = probs[:, 0, :, :].rearrange("p h t -> p (h t)")[:, 0:KD * 6 * D].rearrange(
                "p (k n) -> p k n", k=KD)
            wqkv_raw = probs[:, 1, 0, 0:KD * QKV].rearrange("p (k n) -> p k n", k=KD)
            s_rows = probs[:, 1, 1, 0:KD * B * P].rearrange("p (k b n) -> p k b n", k=KD, b=B)
            gates_raw = probs[:, 1, 1, 1024:2048].rearrange("p (b n) -> p b n", b=B)
            gates_abs = probs[:, 1, 0, 1024:2048].rearrange("p (b n) -> p b n", b=B)
            pT_hi, pT_lo = sb("pT_hi", [P, 2, 512], F32R), sb("pT_lo", [P, 2, 512], F32R)
            cos_sb, sin_sb = sb("cos_sb", [P, NT, HS // 2]), sb("sin_sb", [P, NT, HS // 2])
            wqkv_hi, wqkv_lo = sb("wqkv_hi", [P, KD, QKV], F32R), sb("wqkv_lo", [P, KD, QKV], F32R)
            wo_raw, wo_ga = sb("wo_raw", [P, NH, D]), sb("wo_ga", [P, NH, D])
            wo_hi, wo_lo = sb("wo_hi", [P, NH, D], F32R), sb("wo_lo", [P, NH, D], F32R)
            ga_rows = sb("ga_rows", [P, B, D])
            mask_raw, mask_r, ident_r = sb("mask_raw", [P, P]), sb("mask_r", [P, P], F32R), sb("ident_r", [P, P], F32R)
            wgt_sb = sb("wgt_sb", [P, KD, NG])
            c_cols = sb("c_cols", [P, KD, B])
            c_exp, c_sig, c_rec, s_cols = (sb(n, [P, KD, B]) for n in ("c_exp", "c_sig", "c_rec", "s_cols"))
            mod_cols = sb("mod_cols", [P, B, 4, KD])
            mod_b = sb("mod_b", [P, 4, KD])
            x_sb = sb("x_sb", [P, XS, D])
            x1_sb, y0_sb = sb("x1_sb", [P, 2, D]), sb("y0_sb", [P, D])
            xn = sb("xn", [P, 2, D])
            hf = sb("hf", [P, 2, KD, P])
            hT_hi, hT_lo = sb("hT_hi", [P, KD, P], F32R), sb("hT_lo", [P, KD, P], F32R)
            qkv = sb("qkv", [P, QKV])
            rot_c, rot_s, rot = sb("rot_c", [P, ROT]), sb("rot_s", [P, ROT]), sb("rot", [P, ROT])
            q_hi, q_lo = sb("q_hi", [P, 2, NH * P], F32R), sb("q_lo", [P, 2, NH * P], F32R)
            o_hi, o_lo = sb("o_hi", [P, NH * P], F32R), sb("o_lo", [P, NH * P], F32R)
            top, neg = sb("top", [P, NH, 5]), sb("neg", [P, NH])
            sums, sum_sb, rsums = sb("sums", [P, 4, NH, 4]), sb("sum_sb", [P, NH]), sb("rsums", [P, NH])
            stats, mv = sb("stats", [P, 2, 6]), sb("mv", [P, 2, 2])
            var_eps, ln_v, rs0, rs1, rs2, rs3, rstd = (sb(n, [P, 2]) for n in (
                "var_eps", "ln_v", "rs0", "rs1", "rs2", "rs3", "rstd"))


            def done(sem_, b, kind, t, g=0, times=1, minus=0):
                return (sem_, b * (TOTAL[kind] * times) + AT[kind, t, g] * times - minus)

            def batch_end(eng, b):
                wait_alone(eng, (act_h2, b * NT + NT), (pool_h2, b * NT + NT), (dve_logits, b * NT + NT),
                           (s_st[0], b * (NT // 2 * 16) + NT // 2 * 16), (s_st[1], b * (NT // 2 * 16) + NT // 2 * 16))

            attention_block = ExitStack()
            block = attention_block.enter_context(nc.Block())

            @block.sync
            def _(sp):
                sp.dma_start(ident_sb[:], ident).then_inc(l_ident, 16)
                sp.dma_start(c_cols[:], c).then_inc(l_c, 16)
                sp.dma_start(wmod_raw, wmod.rearrange("(k p) n -> p k n", p=P)).then_inc(l_wmod, 16)
                sp.dma_start(wqkv_raw, wqkvT.rearrange("(k p) n -> p k n", p=P)).then_inc(l_wqkv, 16)
                sp.dma_start(wo_raw[:], woT.rearrange("(h p) n -> p h n", p=P)).then_inc(l_wo, 16)
                sp.dma_start(cos_sb[:], cos.rearrange("(t p) n -> p t n", p=P)).then_inc(l_cos, 16)
                sp.dma_start(sin_sb[:], sin.rearrange("(t p) n -> p t n", p=P)).then_inc(l_sin, 16)
                sp.dma_start(mask_raw[:], mask).then_inc(l_mask, 16)
                sp.dma_start(wgt_sb[:], wgt.rearrange("(k p) n -> p k n", p=P)).then_inc(l_wgt, 16)
                sp.dma_start(b1_cols[:], b1).then_inc(l_b1, 16)
                sp.dma_start(w1_raw[:], w1[0].rearrange("(k p) n -> p k n", p=P)).then_inc(l_w1, 16)
                with sp.Fori(0, B) as b:
                    for t in range(NT + XS):
                        if t >= XS:
                            sp.wait_ge(*done(dve_x1, b, "Y", t - XS))
                            sp.dma_start(x1_dram[:, bass.ds(b * NT + (t - XS), 1), :],
                                         x1_sb[:, (t - XS) % 2:(t - XS) % 2 + 1, :]).then_inc(s_st[t % 2], 16)
                        if t < NT:
                            sp.dma_start(x_sb[:, t % XS:t % XS + 1, :],
                                         xf[:, bass.ds(b * NT + t, 1), :]).then_inc(s_x[t % XS], 16)
                    batch_end(sp, b)

            def x_loaded(b, t):
                per = len(range(t % XS, NT, XS))
                return s_x[t % XS], b * (per * 16) + (t // XS + 1) * 16

            @block.tensor
            def _(pe):
                pe.wait_ge(l_wmod, 16)
                pe.wait_ge(s_pre_d, 4)
                for m, part in enumerate((1, 0, 4, 3)):
                    for j in range(KD):
                        for k in range(KD):
                            last = nc.tensor.matmul(m_ps[:, (m * KD + j) * B:(m * KD + j + 1) * B],
                                                    wmod_raw[:, k, part * D + j * P:part * D + (j + 1) * P],
                                                    s_cols[:, k, :], start=(k == 0), stop=(k == KD - 1))
                last.then_inc(s_pre_e, 1)
                for b in range(B):
                    for n, part in enumerate((2, 5)):
                        for k in range(KD):
                            last = nc.tensor.matmul(score_ps[:, b, n * D:(n + 1) * D], s_rows[:, k, b, :],
                                                    wmod_raw[:, k, part * D:(part + 1) * D],
                                                    start=(k == 0), stop=(k == KD - 1))
                last.then_inc(s_pre_e, 1)
                pe.wait_ge(s_pre_p, 2)
                pe.wait_ge(l_wgt, 16)

                def m_bank_free(b, stage):
                    was = M_BEFORE[stage]
                    if was:
                        reader = {"qkv": act_V, "Y": dve_x1, "rotT": dve_rot}[was[0]]
                        pe.wait_ge(*done(reader, b, *was))

                def t_bank_free(b, stage):
                    was = T_BEFORE[stage]
                    if was:
                        pe.wait_ge(*done(dve_T if was[0] == "T" else act_hf, b, *was))

                with pe.Fori(0, B) as b:
                    pe.wait_ge(s_batch, b * 4 + 4)
                    for stage in ORDER["PE"]:
                        kind, t, g = stage
                        if kind == "S":
                            h, chunk = g // 4, g % 4
                            if g == 0:
                                pe.wait_ge(*done(act_rot, b, "rotT", t, 0, 2))
                                pe.wait_ge(*done(dve_rot, b, "rotT", t))
                            was = t if h else t - 1
                            if ok(was) and chunk < chunks_of(was):
                                pe.wait_ge(*done(act_E, b, "E", was, (1 - h) * 4 + chunk))
                            w = min(512, (t + 1) * P - chunk * 512)
                            keys = slice(chunk * 512, chunk * 512 + w)
                            diag = chunk == chunks_of(t) - 1
                            q1, q2 = (q[:, t % 2, h * P:(h + 1) * P] for q in (q_hi, q_lo))
                            o = score_ps[:, chunk, 0:w]
                            nc.tensor.matmul(o, q1, k_hi[:, keys], start=True, stop=False)
                            nc.tensor.matmul(o, q1, k_lo[:, keys], start=False, stop=False)
                            last = nc.tensor.matmul(o, q2, k_hi[:, keys], start=False, stop=not diag)
                            if diag:
                                last = nc.tensor.matmul(score_ps[:, chunk, w - P:w], ident_r[:], mask_r[:],
                                                        start=False, stop=True)
                            last.then_inc(pe_S, 1)
                        elif kind == "T":
                            pe.wait_ge(*done(act_E, b, "E", t, 4 + g // 2))
                            t_bank_free(b, stage)
                            for j in blocks_of(t, g):
                                for h in range(NH):
                                    c0 = ((j % 2) * NH + h) * P
                                    last = nc.tensor.transpose(tr_ps[:, T_BANK[stage], c0:c0 + P],
                                                               probs[:, t % 2, h, j * P:(j + 1) * P], ident_sb[:])
                            last.then_inc(pe_T, 1)
                        elif kind == "PV":
                            slot = AT["T", t, g] % 2
                            pe.wait_ge(*done(dve_T, b, "T", t, g))
                            if g == 0:
                                if t > 0:
                                    pe.wait_ge(*done(dve_O, b, "O", t - 1))
                                if ok(t - 3):
                                    pe.wait_ge(*done(dve_logits, b, "gate", t - 3))
                                pe.wait_ge(*done(act_V, b, "qkv", t))
                                pe.wait_ge(*done(pool_V, b, "qkv", t))
                            o = o_ps[:, 0:NH * P]
                            for j in blocks_of(t, g):
                                r = slice((j % 2) * NH * P, (j % 2 + 1) * NH * P)
                                nc.tensor.matmul(o, v_hi[:, j, :], pT_hi[:, slot, r], start=(j == 0), stop=False)
                                nc.tensor.matmul(o, v_hi[:, j, :], pT_lo[:, slot, r], start=False, stop=False)
                                last = nc.tensor.matmul(o, v_lo[:, j, :], pT_hi[:, slot, r], start=False,
                                                        stop=(j == t))
                            last.then_inc(pe_PV, 1)
                        elif kind == "gate":
                            if ok(t + 2):
                                pe.wait_ge(*done(dve_O, b, "O", t + 2))
                            elif ok(t - 1):
                                pe.wait_ge(*done(dve_logits, b, "gate", t - 1))
                            pe.wait_ge(*done(act_hf, b, "normT", t + 3))
                            for k in range(KD):
                                last = nc.tensor.matmul(o_ps[:, NH * P:NH * P + NG], hf[:, 1, k, :],
                                                        wgt_sb[:, k, :], start=(k == 0), stop=(k == KD - 1))
                            last.then_inc(pe_gate, 1)
                        elif kind == "qkv":
                            pe.wait_ge(*done(act_hT, b, "hT", t))
                            pe.wait_ge(*done(pool_hT, b, "hT", t))
                            m_bank_free(b, stage)
                            n = 0
                            for k in range(KD):
                                for a, w in ((hT_hi, wqkv_hi), (hT_hi, wqkv_lo), (hT_lo, wqkv_hi)):
                                    last = nc.tensor.matmul(m_ps[:], a[:, k, :], w[:, k, :], start=(n == 0),
                                                            stop=(n == 3 * KD - 1))
                                    n += 1
                            last.then_inc(pe_qkv, 1)
                        elif kind == "Y":
                            pe.wait_ge(*done(dve_O, b, "O", t))
                            m_bank_free(b, stage)
                            for h in range(NH):
                                for n, (a, w) in enumerate(((o_hi, wo_hi), (o_hi, wo_lo), (o_lo, wo_hi))):
                                    last = nc.tensor.matmul(m_ps[:, h * D:(h + 1) * D], a[:, h * P:(h + 1) * P],
                                                            w[:, h, :], start=(n == 0), stop=(n == 2))
                            last.then_inc(pe_Y, 1)
                        elif kind == "rotT":
                            pe.wait_ge(*done(dve_even, b, "rope", t))
                            pe.wait_ge(*done(dve_odd, b, "rope", t))
                            m_bank_free(b, stage)
                            for h in range(NH + 1):
                                last = nc.tensor.transpose(m_ps[:, h * P:(h + 1) * P], rot[:, h * P:(h + 1) * P],
                                                           ident_sb[:])
                            last.then_inc(pe_rotT, 1)
                        elif kind == "normT":
                            pe.wait_ge(*done(dve_xn, b, "xn", t - 1))
                            t_bank_free(b, stage)
                            for i, tile in enumerate((t + 2, t - 3)):
                                if ok(tile):
                                    for k in range(KD):
                                        c0 = (i * KD + k) * P
                                        last = nc.tensor.transpose(tr_ps[:, T_BANK[stage], c0:c0 + P],
                                                                   xn[:, i, k * P:(k + 1) * P], ident_sb[:])
                            last.then_inc(pe_normT, 1)
                    batch_end(pe, b)

            @block.scalar
            def _(act):
                act.preload_act_table_set("natural_log_exp_and_others")
                act.wait_ge(l_c, 16)
                nc.scalar.activation(c_exp[:], c_cols[:], ACT.Exp, scale=-1.0).then_inc(s_pre_a, 1)
                with act.Fori(0, B) as b:
                    for kind, t, g in ORDER["ACT"]:
                        if kind == "E":
                            h, chunk = g // 4, g % 4
                            act.wait_ge(*done(dve_N, b, "N", t, h))
                            if ok(t - 2):
                                act.wait_ge(*done(pe_T, b, "T", t - 2, groups_of(t - 2) - 1))
                            if ok(t - 4):
                                act.wait_ge(*done(dve_x1, b, "Y", t - 4))
                            if t == 0 and g == 0:
                                act.wait_ge(s_batch, b * 4 + 4)
                            w = min(512, (t + 1) * P - chunk * 512)
                            nc.scalar.activation(probs[:, t % 2, h, chunk * 512:chunk * 512 + w],
                                                 score_ps[:, chunk, 0:w], ACT.Exp,
                                                 bias=neg[:, h:h + 1], scale=SCALE,
                                                 accum_out=sums[:, t % 4, h, chunk:chunk + 1]).then_inc(act_E, 1)
                        elif kind == "T":
                            n = len(blocks_of(t, g)) * NH * P
                            slot = AT["T", t, g] % 2
                            act.wait_ge(*done(pe_T, b, "T", t, g))
                            before = AT["T", t, g] - 2
                            if before >= 1:
                                act.wait_ge(pe_PV, b * TOTAL["PV"] + before)
                            nc.scalar.activation(pT_hi[:, slot, 0:n], tr_ps[:, T_BANK[kind, t, g], 0:n],
                                                 ACT.Copy).then_inc(act_T, 1)
                        elif kind == "O":
                            act.wait_ge(*done(pe_PV, b, "PV", t, groups_of(t) - 1))
                            if t > 0:
                                act.wait_ge(*done(pe_Y, b, "Y", t - 1))
                            nc.scalar.activation(o_hi[:], o_ps[:, 0:NH * P], ACT.Copy).then_inc(act_O, 1)
                        elif kind == "hT":
                            act.wait_ge(*done(act_hf, b, "normT", t - 2))
                            if t > 0:
                                act.wait_ge(*done(pe_qkv, b, "qkv", t - 1))
                            nc.scalar.activation(hT_hi[:], hf[:, 0, :, :], ACT.Copy).then_inc(act_hT, 1)
                        elif kind == "qkv":
                            act.wait_ge(*done(pe_qkv, b, "qkv", t))
                            if t > 0:
                                act.wait_ge(*done(pool_cos, b, "rope", t - 1))
                                act.wait_ge(*done(pool_sin, b, "rope", t - 1))
                                act.wait_ge(*done(pool_V, b, "qkv", t - 1))
                            nc.scalar.activation(qkv[:], m_ps[:], ACT.Copy).then_inc(act_qkv, 1)
                            nc.scalar.activation(v_hi[:, t, :], m_ps[:, ROT:QKV], ACT.Copy).then_inc(act_V, 1)
                        elif kind == "norm":
                            act.wait_ge(*done(pool_var, b, "norm", t))
                            nc.scalar.activation(ln_v[:], var_eps[:], ACT.Ln).then_inc(act_ln, 1)
                            act.wait_ge(*done(act_ln, b, "norm", t))
                            nc.scalar.activation(rs0[:], ln_v[:], ACT.Exp, scale=-0.5).then_inc(act_rstd, 1)
                        elif kind == "rotT":
                            act.wait_ge(*done(pe_rotT, b, "rotT", t))
                            if ok(t - 2):
                                act.wait_ge(*done(pe_S, b, "S", t - 2, 4 + chunks_of(t - 2) - 1))
                            nc.scalar.activation(q_hi[:, t % 2, :], m_ps[:, 0:NH * P],
                                                 ACT.Copy).then_inc(act_rot, 1)
                            nc.scalar.activation(k_hi[:, t * P:(t + 1) * P], m_ps[:, NH * P:ROT],
                                                 ACT.Copy).then_inc(act_rot, 1)
                        elif kind == "normT":
                            act.wait_ge(*done(pe_normT, b, "normT", t))
                            if ok(t + 1):
                                act.wait_ge(*done(pool_hT, b, "hT", t + 1))
                            if ok(t - 4):
                                act.wait_ge(*done(pool_h2, b, "h2", t - 4))
                                act.wait_ge(*done(pe_gate, b, "gate", t - 4))
                            if t == -2:
                                act.wait_ge(s_batch, b * 4 + 4)
                            for i, tile in enumerate((t + 2, t - 3)):
                                if ok(tile):
                                    for k in range(KD):
                                        c0 = (i * KD + k) * P
                                        last = nc.scalar.activation(
                                            hf[:, i, k, :], tr_ps[:, T_BANK[kind, t, g], c0:c0 + P], ACT.Identity,
                                            scale=mod_b[:, 2 * i, k:k + 1], bias=mod_b[:, 2 * i + 1, k:k + 1])
                            last.then_inc(act_hf, 1)
                        elif kind == "h2":
                            wait_alone(act, done(act_hf, b, "normT", t + 3))
                            nc.scalar.activation(h2_hi[:, :, bass.ds(b * T + t * P, P)], hf[:, 1, :, :],
                                                 ACT.Copy).then_inc(act_h2, 1)
                    batch_end(act, b)

            @block.vector
            def _(dve):
                made = [0]

                def step(ins):
                    made[0] += 1
                    ins.then_inc(s_pre_d, 1)
                    dve.wait_ge(s_pre_d, made[0])

                dve.wait_ge(s_pre_a, 1)
                step(nc.vector.tensor_scalar_add(c_sig[:], c_exp[:], 1.0))
                step(nc.vector.reciprocal(c_rec[:], c_sig[:]))
                step(nc.vector.tensor_tensor(s_cols[:], c_cols[:], c_rec[:], ALU.mult))
                step(nc.vector.tensor_copy(s_rows, s_cols[:].unsqueeze(3).broadcast_to([P, KD, B, P])))
                dve.wait_ge(l_ident, 16)
                step(nc.vector.tensor_copy(ident_r[:], ident_sb[:]))
                dve.wait_ge(l_mask, 16)
                step(nc.vector.tensor_copy(mask_r[:], mask_raw[:]))
                step(nc.vector.memset(mv[:], 0.0))
                dve.wait_ge(s_pre_e, 1)
                step(nc.vector.tensor_copy(mod_cols[:].rearrange("p b m j -> p (m j) b"),
                                           m_ps[:, 0:4 * KD * B].rearrange("p (n b) -> p n b", b=B)))
                step(nc.vector.tensor_scalar_add(mod_cols[:, :, 0, :], mod_cols[:, :, 0, :], 1.0))
                step(nc.vector.tensor_scalar_add(mod_cols[:, :, 2, :], mod_cols[:, :, 2, :], 1.0))
                dve.wait_ge(s_pre_e, 2)
                step(nc.vector.tensor_copy(gates_raw, score_ps[:, 0:B, :]))
                step(nc.vector.scalar_tensor_tensor(gates_abs, gates_raw, -1.0, gates_raw, ALU.mult, ALU.max))
                step(nc.vector.tensor_scalar(gates_abs, gates_abs, 0.25, None, ALU.max))
                step(nc.vector.tensor_scalar(gates_raw, gates_raw, 0.0, 2.0, ALU.is_ge, ALU.mult))
                step(nc.vector.scalar_tensor_tensor(ga_rows[:], gates_raw[:, :, 0:D], 1.0, gates_abs[:, :, 0:D],
                                                    ALU.subtract, ALU.mult))
                step(nc.vector.scalar_tensor_tensor(gb_rows[:], gates_raw[:, :, D:2 * D], 1.0,
                                                    gates_abs[:, :, D:2 * D], ALU.subtract, ALU.mult))
                dve.wait_ge(l_wo, 16)
                with dve.Fori(0, B) as b:
                    nc.vector.tensor_copy(mod_b[:].unsqueeze(1), mod_cols[:, bass.ds(b, 1), :, :]).then_inc(s_batch, 1)
                    nc.vector.tensor_tensor(wo_ga[:], wo_raw[:],
                                            ga_rows[:, bass.ds(b, 1), :].broadcast_to([P, NH, D]),
                                            ALU.mult).then_inc(s_batch, 1)
                    dve.wait_ge(s_batch, b * 4 + 2)
                    nc.vector.tensor_copy(wo_hi[:], wo_ga[:]).then_inc(s_batch, 1)
                    dve.wait_ge(s_batch, b * 4 + 3)
                    nc.vector.tensor_tensor(wo_lo[:], wo_ga[:], wo_hi[:].bitcast(F32),
                                            ALU.subtract).then_inc(s_batch, 1)
                    dve.wait_ge(s_batch, b * 4 + 4)
                    for kind, t, g in ORDER["DVE"]:
                        if kind == "M":
                            h, chunk = g // 4, g % 4
                            dve.wait_ge(*done(pe_S, b, "S", t, g))
                            w = min(512, (t + 1) * P - chunk * 512)
                            nc.vector.reduce_max(top[:, h, chunk:chunk + 1], score_ps[:, chunk, 0:w],
                                                 axis=AX_X).then_inc(dve_M, 1)
                        elif kind == "N":
                            n = chunks_of(t)
                            dve.wait_ge(*done(dve_M, b, "M", t, g * 4 + n - 1))
                            nc.vector.reduce_max(top[:, g, 4:5], top[:, g, 0:n], axis=AX_X).then_inc(dve_top, 1)
                            dve.wait_ge(*done(dve_top, b, "N", t, g))
                            nc.vector.tensor_scalar(neg[:, g:g + 1], top[:, g, 4:5], -SCALE, None,
                                                    ALU.mult).then_inc(dve_N, 1)
                        elif kind == "T":
                            n = len(blocks_of(t, g)) * NH * P
                            slot = AT["T", t, g] % 2
                            dve.wait_ge(*done(act_T, b, "T", t, g))
                            nc.vector.tensor_tensor(pT_lo[:, slot, 0:n], tr_ps[:, T_BANK[kind, t, g], 0:n],
                                                    pT_hi[:, slot, 0:n].bitcast(F32),
                                                    ALU.subtract).then_inc(dve_T, 1)
                        elif kind == "O":
                            dve.wait_ge(*done(act_O, b, "O", t))
                            nc.vector.tensor_tensor(o_lo[:], o_ps[:, 0:NH * P], o_hi[:].bitcast(F32),
                                                    ALU.subtract).then_inc(dve_O, 1)
                        elif kind == "gate":
                            dve.wait_ge(*done(pe_gate, b, "gate", t))
                            nc.vector.tensor_copy(logits[:, bass.ds(b * NT + t, 1), :],
                                                  o_ps[:, NH * P:NH * P + NG].unsqueeze(1)).then_inc(dve_logits, 1)
                        elif kind == "rope":
                            turned = lambda a, eo: a[:, 0:ROT].rearrange("p (h e i) -> p h e i", e=2,
                                                                         i=HS // 2)[:, :, eo, :]
                            dve.wait_ge(*done(pool_cos, b, "rope", t))
                            dve.wait_ge(*done(pool_sin, b, "rope", t))
                            if t > 0:
                                dve.wait_ge(*done(pe_rotT, b, "rotT", t - 1))
                            nc.vector.tensor_tensor(turned(rot, 0), turned(rot_c, 0), turned(rot_s, 1),
                                                    ALU.subtract).then_inc(dve_even, 1)
                            nc.vector.tensor_tensor(turned(rot, 1), turned(rot_c, 1), turned(rot_s, 0),
                                                    ALU.add).then_inc(dve_odd, 1)
                        elif kind == "rotT":
                            dve.wait_ge(*done(act_rot, b, "rotT", t, 0, 2))
                            nc.vector.tensor_tensor(q_lo[:, t % 2, :], m_ps[:, 0:NH * P],
                                                    q_hi[:, t % 2, :].bitcast(F32), ALU.subtract)
                            nc.vector.tensor_tensor(k_lo[:, t * P:(t + 1) * P], m_ps[:, NH * P:ROT],
                                                    k_hi[:, t * P:(t + 1) * P].bitcast(F32),
                                                    ALU.subtract).then_inc(dve_rot, 1)
                        elif kind == "Y":
                            if t > 0:
                                dve.wait_ge(*done(dve_x1, b, "Y", t - 1))
                            nc.vector.reduce_sum(sum_sb[:], sums[:, t % 4, :, 0:chunks_of(t)],
                                                 axis=AX_X).then_inc(dve_sum, 1)
                            dve.wait_ge(*done(dve_sum, b, "Y", t))
                            nc.vector.reciprocal(rsums[:], sum_sb[:]).then_inc(dve_recip, 1)
                            dve.wait_ge(*done(dve_recip, b, "Y", t))
                            dve.wait_ge(*done(pe_Y, b, "Y", t))
                            nc.vector.scalar_tensor_tensor(y0_sb[:], m_ps[:, 0:D], rsums[:, 0:1], x_sb[:, t % XS, :],
                                                           ALU.mult, ALU.add).then_inc(dve_y0, 1)
                            dve.wait_ge(*done(dve_y0, b, "Y", t))
                            if t >= 2:
                                dve.wait_ge(*done(dve_xn, b, "xn", t))
                                dve.wait_ge(s_st[t % 2], b * (NT // 2 * 16) + t // 2 * 16)
                            nc.vector.scalar_tensor_tensor(x1_sb[:, t % 2, :], m_ps[:, D:2 * D], rsums[:, 1:2],
                                                           y0_sb[:], ALU.mult, ALU.add).then_inc(dve_x1, 1)
                        elif kind == "norm":
                            s = t
                            if s > -3:
                                dve.wait_ge(*done(dve_xn, b, "xn", s - 1))
                            if ok(s + 3):
                                dve.wait_ge(*x_loaded(b, s + 3))
                                last = nc.vector.bn_stats(stats[:, 0, :], x_sb[:, (s + 3) % XS, :])
                            if ok(s - 2):
                                dve.wait_ge(*done(dve_x1, b, "Y", s - 2))
                                last = nc.vector.bn_stats(stats[:, 1, :], x1_sb[:, s % 2, :])
                            last.then_inc(dve_stats, 1)
                            wait_alone(dve, done(dve_stats, b, "norm", s))
                            for i, tile in enumerate((s + 3, s - 2)):
                                if ok(tile):
                                    last = nc.vector.bn_aggr(mv[:, i, :], stats[:, i, :])
                            last.then_inc(dve_norm, 1)
                        elif kind == "xn":
                            dve.wait_ge(*done(pool_ln, b, "rstd", t, 0, 4))
                            if t > -3:
                                dve.wait_ge(*done(pe_normT, b, "normT", t))
                            if ok(t + 3):
                                last = nc.vector.tensor_scalar(xn[:, 0, :], x_sb[:, (t + 3) % XS, :], mv[:, 0, 0:1],
                                                               rstd[:, 0:1], ALU.subtract, ALU.mult)
                            if ok(t - 2):
                                last = nc.vector.tensor_scalar(xn[:, 1, :], x1_sb[:, t % 2, :], mv[:, 1, 0:1],
                                                               rstd[:, 1:2], ALU.subtract, ALU.mult)
                            last.then_inc(dve_xn, 1)
                    batch_end(dve, b)

            @block.gpsimd
            def _(pool):
                pool.wait_ge(l_wqkv, 16)
                nc.gpsimd.tensor_copy(wqkv_hi[:], wqkv_raw).then_inc(s_pre_p, 1)
                pool.wait_ge(s_pre_p, 1)
                nc.gpsimd.tensor_tensor(wqkv_lo[:], wqkv_raw, wqkv_hi[:].bitcast(F32),
                                        ALU.subtract).then_inc(s_pre_p, 1)
                pool.wait_ge(s_pre_p, 2)
                pool.wait_ge(l_cos, 16)
                pool.wait_ge(l_sin, 16)
                with pool.Fori(0, B) as b:
                    for kind, t, g in ORDER["POOL"]:
                        if kind == "hT":
                            pool.wait_ge(*done(act_hT, b, "hT", t))
                            nc.gpsimd.tensor_tensor(hT_lo[:], hf[:, 0, :, :], hT_hi[:].bitcast(F32),
                                                    ALU.subtract).then_inc(pool_hT, 1)
                        elif kind == "qkv":
                            pool.wait_ge(*done(act_V, b, "qkv", t))
                            nc.gpsimd.tensor_tensor(v_lo[:, t, :], qkv[:, ROT:QKV], v_hi[:, t, :].bitcast(F32),
                                                    ALU.subtract).then_inc(pool_V, 1)
                        elif kind == "rope":
                            half = lambda a: a[:, 0:ROT].rearrange("p (n i) -> p n i", i=HS // 2)
                            pool.wait_ge(*done(act_qkv, b, "qkv", t))
                            if t > 0:
                                pool.wait_ge(*done(dve_odd, b, "rope", t - 1))
                            for to, table, made in ((rot_c, cos_sb, pool_cos), (rot_s, sin_sb, pool_sin)):
                                nc.gpsimd.tensor_tensor(half(to), half(qkv),
                                                        table[:, t:t + 1, :].broadcast_to(
                                                            [P, 2 * (NH + 1), HS // 2]),
                                                        ALU.mult).then_inc(made, 1)
                        elif kind == "norm":
                            wait_alone(pool, done(dve_norm, b, "norm", t))
                            nc.gpsimd.tensor_scalar(var_eps[:], mv[:, :, 1], EPS, None, ALU.add).then_inc(pool_var, 1)
                        elif kind == "rstd":
                            made = lambda n: done(pool_ln, b, "rstd", t, 0, 4, 4 - n)
                            pool.wait_ge(*done(act_rstd, b, "norm", t))
                            nc.gpsimd.tensor_tensor(rs1[:], rs0[:], rs0[:], ALU.mult).then_inc(pool_ln, 1)
                            pool.wait_ge(*made(1))
                            nc.gpsimd.tensor_tensor(rs2[:], rs1[:], var_eps[:], ALU.mult).then_inc(pool_ln, 1)
                            wait_alone(pool, made(2))
                            nc.gpsimd.tensor_scalar(rs3[:], rs2[:], -0.5, 1.5, ALU.mult, ALU.add).then_inc(pool_ln, 1)
                            pool.wait_ge(*made(3))
                            if t > -3:
                                pool.wait_ge(*done(dve_xn, b, "xn", t - 1))
                            nc.gpsimd.tensor_tensor(rstd[:], rs0[:], rs3[:], ALU.mult).then_inc(pool_ln, 1)
                        elif kind == "h2":
                            wait_alone(pool, done(act_h2, b, "h2", t))
                            tok = bass.ds(b * T + t * P, P)
                            nc.gpsimd.tensor_tensor(h2_lo[:, :, tok], hf[:, 1, :, :], h2_hi[:, :, tok].bitcast(F32),
                                                    ALU.subtract).then_inc(pool_h2, 1)
                    batch_end(pool, b)

            attention_block.close()

        mixture = ExitStack()
        with mixture:
            def mx(name, shape, dt=F32, ctx=mixture):
                return ctx.enter_context(nc.sbuf_tensor(name, shape, dt))

            w1_hi = [mx(f"w1_hi{i}", [P, KD, FF], F32R) for i in range(2)]
            w1_lo = [mx(f"w1_lo{i}", [P, KD, FF], F32R) for i in range(2)]
            w2_raw = mx("w2_raw", [P, FT, D])
            acc = mx("acc", [P, TILES, D])
            h_hi, h_lo = mx("h_hi", [P, 4, UTOK], F32R), mx("h_lo", [P, 4, UTOK], F32R)
            g_sb = mx("g_sb", [P, 2, UTOK])
            y_sb = mx("y_sb", [P, 2, 2 * D])
            w2_both = [mx("w2_both0", [P, FT, 2, D], F32R)]

            start = ExitStack()
            with start:
                b2_raw, b2_low = (mx(n, [P, UNIT * D], F32, start) for n in ("b2_raw", "b2_low"))
                b2_all = mx("b2_all", [P, UNIT * D], F32R, start)
                lo_cols = mx("lo_cols", [P, 2], F32, start)
                bgt_sb = mx("bgt_sb", [P, NG], F32, start)
                ge0, ge1 = mx("ge0", [P, TILES, E], F32, start), mx("ge1", [P, TILES, E], F32, start)
                gt = [mx(f"gt{i}", [P, TILES], F32, start) for i in range(5)]
                w_hi, w_lo = mx("w_hi", [P, TILES, E], F32R, start), mx("w_lo", [P, TILES, E], F32R, start)
                w_stack = mx("w_stack", [P, UNIT, 4, E], F32, start)
                w_T = mx("w_T", [P, P], F32R, start)

                with nc.Block() as block:
                    @block.sync
                    def _(sp):
                        sp.dma_start(w2_raw[:], w2[0].rearrange("(f p) n -> p f n", p=P)).then_inc(l_w2, 16)
                        sp.dma_start(bgt_sb[:], bgt.partition_broadcast(P)).then_inc(l_bgt, 16)
                        sp.dma_start(lo_cols[:], lo_rows).then_inc(l_lor, 16)
                        sp.wait_ge(s_b2, 1)
                        for j in range(UNIT):
                            for r in range(3):
                                p0 = j * 4 * E + r * E
                                sp.dma_start(b2_raw[p0:p0 + E, j * D:(j + 1) * D], b2).then_inc(l_b2, 16)
                        sp.wait_ge(s_first1, 2)
                        sp.dma_start(w1_raw[:], w1[1].rearrange("(k p) n -> p k n", p=P)).then_inc(l_w1, 16)
                        sp.wait_ge(s_first2, 2)
                        sp.dma_start(w2_raw[:], w2[1].rearrange("(f p) n -> p f n", p=P)).then_inc(l_w2, 16)
                        sp.wait_ge(l_w1, 32)
                        sp.wait_ge(l_w2, 32)

                    @block.gpsimd
                    def _(pool):
                        nc.gpsimd.memset(b2_raw[:], 0.0).then_inc(s_b2, 1)
                        pool.wait_ge(l_w2, 16)
                        nc.gpsimd.tensor_copy(w2_both[0][:, :, 0, :], w2_raw[:]).then_inc(s_first2, 1)
                        pool.wait_ge(s_first2, 1)
                        nc.gpsimd.tensor_tensor(w2_both[0][:, :, 1, :], w2_raw[:],
                                                w2_both[0][:, :, 0, :].bitcast(F32),
                                                ALU.subtract).then_inc(s_first2, 1)

                    @block.scalar
                    def _(act):
                        act.wait_ge(l_w1, 16)
                        nc.scalar.activation(w1_hi[0][:], w1_raw[:], ACT.Copy).then_inc(s_first1, 1)
                        act.wait_ge(s_gate, 3)
                        nc.scalar.activation(ge1[:], ge0[:], ACT.Exp).then_inc(s_gexp, 1)
                        nc.scalar.activation(gt[1][:], logits[:, :, E], ACT.Exp, scale=-1.0).then_inc(s_gexp, 1)
                        for q in range(UNITS):
                            act.wait_ge(s_wtr, q + 1)
                            if q:
                                act.wait_ge(s_init, q)
                            nc.scalar.activation(w_T[:], tr_ps[:, 0, 0:P], ACT.Copy).then_inc(s_wtc, 1)

                    @block.vector
                    def _(dve):
                        made = [0]

                        def step(ins):
                            made[0] += 1
                            ins.then_inc(s_gate, 1)
                            dve.wait_ge(s_gate, made[0])

                        wide = lambda a: a[:].unsqueeze(2).broadcast_to([P, TILES, E])
                        dve.wait_ge(l_bgt, 16)
                        step(nc.vector.tensor_tensor(logits[:], logits[:],
                                                     bgt_sb[:].unsqueeze(1).broadcast_to([P, TILES, NG]), ALU.add))
                        step(nc.vector.reduce_max(gt[0][:], logits[:, :, 0:E], axis=AX_X))
                        step(nc.vector.tensor_tensor(ge0[:], logits[:, :, 0:E], wide(gt[0]), ALU.subtract))
                        dve.wait_ge(s_gexp, 2)
                        step(nc.vector.reduce_sum(gt[2][:], ge1[:], axis=AX_X))
                        step(nc.vector.reciprocal(gt[3][:], gt[2][:]))
                        step(nc.vector.tensor_tensor(ge0[:], ge1[:], wide(gt[3]), ALU.mult))
                        step(nc.vector.tensor_scalar_add(gt[2][:], gt[1][:], 1.0))
                        step(nc.vector.reciprocal(gt[3][:], gt[2][:]))
                        step(nc.vector.tensor_scalar(gt[4][:], gt[3][:], MAX_THRESHOLD, None, ALU.mult))
                        step(nc.vector.tensor_tensor(ge1[:], ge0[:], wide(gt[4]), ALU.subtract))
                        step(nc.vector.scalar_tensor_tensor(ge0[:], ge1[:], 0.0, ge1[:], ALU.is_ge, ALU.mult))
                        step(nc.vector.reduce_sum(gt[0][:], ge0[:], axis=AX_X))
                        step(nc.vector.scalar_tensor_tensor(gt[2][:], gt[0][:], 0.0, gt[0][:], ALU.is_equal, ALU.add))
                        step(nc.vector.reciprocal(gt[3][:], gt[2][:]))
                        step(nc.vector.tensor_tensor(gates[:], ge0[:], wide(gt[3]), ALU.mult))
                        step(nc.vector.tensor_copy(w_hi[:], gates[:]))
                        step(nc.vector.tensor_tensor(w_lo[:], gates[:], w_hi[:].bitcast(F32), ALU.subtract))
                        step(nc.vector.memset(w_stack[:], 0.0))
                        dve.wait_ge(l_b2, 16 * 3 * UNIT)
                        dve.wait_ge(l_lor, 16)
                        step(nc.vector.tensor_copy(b2_all[:], b2_raw[:]))
                        step(nc.vector.tensor_tensor(b2_low[:], b2_raw[:], b2_all[:].bitcast(F32), ALU.subtract))
                        step(nc.vector.tensor_scalar(b2_low[:], b2_low[:], lo_cols[:, 0:1], None, ALU.mult))
                        step(nc.vector.scalar_tensor_tensor(b2_all[:], b2_all[:].bitcast(F32), lo_cols[:, 1:2],
                                                            b2_low[:], ALU.mult, ALU.add))
                        for q in range(UNITS):
                            if q:
                                dve.wait_ge(s_wtr, q)
                            four = slice(q * UNIT, (q + 1) * UNIT)
                            nc.vector.tensor_copy(w_stack[:, :, 0, :], w_hi[:, four, :].bitcast(F32))
                            nc.vector.tensor_copy(w_stack[:, :, 1, :], w_hi[:, four, :].bitcast(F32))
                            nc.vector.tensor_copy(w_stack[:, :, 2, :],
                                                  w_lo[:, four, :].bitcast(F32)).then_inc(s_wst, 1)
                            dve.wait_ge(s_init, q + 1)
                            nc.vector.tensor_copy(acc[:, four, :].rearrange("p (a t) d -> p a (t d)", a=2),
                                                  score_ps[:, 0:2, :]).then_inc(s_acc, 1)
                        dve.wait_ge(s_first1, 1)
                        nc.vector.tensor_tensor(w1_lo[0][:], w1_raw[:], w1_hi[0][:].bitcast(F32),
                                                ALU.subtract).then_inc(s_first1, 1)

                    @block.tensor
                    def _(pe):
                        pe.wait_ge(s_gate, 22)
                        for q in range(UNITS):
                            pe.wait_ge(s_wst, q + 1)
                            if q:
                                pe.wait_ge(s_wtc, q)
                            nc.tensor.transpose(tr_ps[:, 0, 0:P], w_stack[:].rearrange("p a b c -> p (a b c)"),
                                                ident_sb[:]).then_inc(s_wtr, 1)
                            pe.wait_ge(s_wtc, q + 1)
                            if q:
                                pe.wait_ge(s_acc, q)
                            for i in range(2):
                                last = nc.tensor.matmul(score_ps[:, i, :], w_T[:], b2_all[:, i * 512:(i + 1) * 512],
                                                        start=True, stop=True)
                            last.then_inc(s_init, 1)

            w2_both.append(mx("w2_both1", [P, FT, 2, D], F32R))
            up_ps = [score_ps[:, i, :] for i in range(4)]
            down_ps = [tr_ps[:, 0, :], tr_ps[:, 1, :], o_ps[:], m_ps[:]]
            slabs = [w1_raw[:].rearrange("p k n -> p (k n)")[:, i * UNIT * D:(i + 1) * UNIT * D].rearrange(
                "p (t d) -> p t d", t=UNIT) for i in range(2)]

            def experts(eng, unit):
                def expert(e, par, last):
                    with eng.Fori(0, UNITS - 1) as t:
                        unit(e, par, t, (e, par, t + 1), last)
                    unit(e, par, UNITS - 1, None if last else (e + 1, 1 - par, 0), last)

                with eng.Fori(0, E // 2 - 1) as pair:
                    expert(pair * 2, 0, False)
                    expert(pair * 2 + 1, 1, False)
                expert(E - 2, 0, False)
                expert(E - 1, 1, True)

            def hidden(e, t, f):
                return e * (UNITS * FT) + t * FT + f

            AHEAD = 2

            def gate_of(e, t, j):
                return gates[:].rearrange("p t e -> p (t e)")[:, bass.ds(t * (UNIT * E) + (j * E + e), 1)]

            def wait_slot(eng, e, t, f):
                u = e * UNITS + t
                if f >= 4:
                    wait_alone(eng, (h_free, u * (FT - 1) + (f - 4) + 1 + 3))
                elif f == 3:
                    wait_alone(eng, (down_done, u * UNIT + 1))
                else:
                    wait_alone(eng, (h_free, u * (FT - 1) + f + 1))

            with nc.Block() as block:
                @block.sync
                def _(sp):
                    with sp.Fori(0, E - 2) as e:
                        sp.wait_ge(w_split, (e + 1) * (2 * UNITS))
                        sp.dma_start(w1_raw[:].unsqueeze(1), w1[bass.ds(e + 2, 1)].rearrange(
                            "e (k p) n -> p e k n", p=P)).then_inc(l_w1, 16)
                        sp.dma_start(w2_raw[:].unsqueeze(1), w2[bass.ds(e + 2, 1)].rearrange(
                            "e (f p) n -> p e f n", p=P)).then_inc(l_w2, 16)
                    sp.wait_ge(w_split, (E - 1) * (2 * UNITS))
                    for t in range(UNITS + 1):
                        if t > 0:
                            sp.wait_ge(pool_out, t)
                            sp.dma_start(of[:, (t - 1) * UNIT:t * UNIT, :],
                                         acc[:, (t - 1) * UNIT:t * UNIT, :]).then_inc(s_out[t % 2], 16)
                        if t < UNITS:
                            if t >= 2:
                                sp.wait_ge(pool_out, t - 1)
                            sp.dma_start(slabs[t % 2], x1_dram[:, t * UNIT:(t + 1) * UNIT, :]).then_inc(l_x1[t % 2], 16)
                    for s in s_out:
                        sp.wait_ge(s, UNITS // 2 * 16)

                @block.tensor
                def _(pe):
                    pe.sem_inc(h_free, 3)
                    pe.sem_inc(down_done, 1)

                    def up(e, par, t, f):
                        n = hidden(e, t, f)
                        pe.wait_ge(up_free, n + 1)
                        tok = bass.ds(t * UTOK, UTOK)
                        i = 0
                        for k in range(KD):
                            for w, h in ((w1_hi, h2_hi), (w1_hi, h2_lo), (w1_lo, h2_hi)):
                                last = nc.tensor.matmul(up_ps[f % 4], w[par][:, k, f * P:(f + 1) * P], h[:, k, tok],
                                                        start=(i == 0), stop=(i == 3 * KD - 1))
                                i += 1
                        last.then_inc(up_done, 1)

                    def down(e, par, t, f):
                        n = hidden(e, t, f)
                        pe.wait_ge(lo_done, n + 2 + 1)
                        for j in range(UNIT):
                            if f == 0:
                                u = e * UNITS + t
                                pe.wait_ge(*((dve_evict, 2 * u + j + 1) if j < 2 else (act_evict, 2 * u + j - 1)))
                            tok = slice(j * P, (j + 1) * P)
                            nc.tensor.matmul(down_ps[j], h_hi[:, f % 4, tok],
                                             w2_both[par][:, f, :, :].rearrange("p a d -> p (a d)"),
                                             start=(f == 0), stop=False)
                            last = nc.tensor.matmul(down_ps[j][:, 0:D], h_lo[:, f % 4, tok],
                                                    w2_both[par][:, f, 0, :], start=False, stop=(f == FT - 1))
                            if f == FT - 1:
                                last.then_inc(down_done, 1)
                        if f < FT - 1:
                            last.then_inc(h_free, 1)

                    def unit(e, par, t, following, last):
                        for f in range(FT):
                            if f + AHEAD < FT:
                                up(e, par, t, f + AHEAD)
                            elif following:
                                if following[1] != par and f + AHEAD == FT:
                                    pe.wait_ge(w_split, (e + 1) * (2 * UNITS))
                                up(*following, f + AHEAD - FT)
                            down(e, par, t, f)

                    for f in range(AHEAD):
                        up(0, 0, 0, f)
                    experts(pe, unit)

                @block.scalar
                def _(act):
                    act.sem_inc(up_free, 4)
                    act.sem_inc(act_evict, 2)

                    def gelu(e, par, t, f):
                        n = hidden(e, t, f)
                        wait_alone(act, (up_done, n + 1), (lo_done, n + 1))
                        bias = b1_cols[:, bass.ds(e * FT + f, 1)]
                        nc.scalar.activation(g_sb[:, f % 2, :], up_ps[f % 4], ACT.Gelu_apprx_tanh,
                                             bias=bias).then_inc(g_done, 1)
                        wait_slot(act, e, t, f)
                        nc.scalar.activation(h_hi[:, f % 4, :], up_ps[f % 4], ACT.Gelu_apprx_tanh,
                                             bias=bias).then_inc(up_free, 1)

                    def unit(e, par, t, following, last):
                        for f in range(AHEAD, FT):
                            gelu(e, par, t, f)
                        if following:
                            for f in range(AHEAD):
                                gelu(*following, f)
                        u = e * UNITS + t
                        for j in (2, 3):
                            wait_alone(act, (down_done, u * UNIT + j + 2), (pool_evict, 2 * u + j - 1))
                            nc.scalar.activation(y_sb[:, j - 2, :], down_ps[j], ACT.Copy,
                                                 scale=gate_of(e, t, j)).then_inc(act_evict, 1)

                    for f in range(AHEAD):
                        gelu(0, 0, 0, f)
                    experts(act, unit)

                @block.vector
                def _(dve):
                    dve.sem_inc(lo_done, 2)
                    dve.sem_inc(dve_evict, 2)

                    def low(e, par, t, f):
                        n = hidden(e, t, f)
                        dve.wait_ge(g_done, n + 1)
                        dve.wait_ge(up_free, n + 4 + 1)
                        nc.vector.tensor_tensor(h_lo[:, f % 4, :], g_sb[:, f % 2, :], h_hi[:, f % 4, :].bitcast(F32),
                                                ALU.subtract).then_inc(lo_done, 1)

                    def unit(e, par, t, following, last):
                        for f in range(AHEAD, FT):
                            low(e, par, t, f)
                        if following:
                            for f in range(AHEAD):
                                low(*following, f)
                        u = e * UNITS + t
                        tile = lambda j: acc[:, bass.ds(t * UNIT + j, 1), :]
                        for j in (0, 1):
                            dve.wait_ge(down_done, u * UNIT + j + 2)
                            nc.vector.scalar_tensor_tensor(tile(j), down_ps[j][:, 0:D].unsqueeze(1), gate_of(e, t, j),
                                                           tile(j), ALU.mult, ALU.add).then_inc(dve_first, 1)
                        for j in (0, 1):
                            dve.wait_ge(dve_first, 2 * u + j + 1)
                            nc.vector.scalar_tensor_tensor(tile(j), down_ps[j][:, D:2 * D].unsqueeze(1),
                                                           gate_of(e, t, j), tile(j),
                                                           ALU.mult, ALU.add).then_inc(dve_evict, 1)

                    for f in range(AHEAD):
                        low(0, 0, 0, f)
                    experts(dve, unit)

                @block.gpsimd
                def _(pool):
                    pool.sem_inc(pool_evict, 2)

                    def add(e, t):
                        u = e * UNITS + t
                        tile = lambda j: acc[:, bass.ds(t * UNIT + j, 1), :]
                        for n, sem_, before in ((0, pool_first, act_evict), (1, pool_evict, pool_first)):
                            for j in (2, 3):
                                wait_alone(pool, (before, 2 * u + j - 1 + (2 if n == 0 else 0)))
                                nc.gpsimd.tensor_tensor(tile(j), tile(j),
                                                        y_sb[:, j - 2:j - 1, n * D:(n + 1) * D],
                                                        ALU.add).then_inc(sem_, 1)

                    def split(e, par, t):
                        to = 1 - par
                        cols = bass.ds(t * P, P)
                        row = bass.ds(t, 1)
                        done_ = e * (2 * UNITS) + t * 2
                        nc.gpsimd.tensor_copy(w1_hi[to][:, :, cols], w1_raw[:, :, cols]).then_inc(split_chain, 1)
                        nc.gpsimd.tensor_copy(w2_both[to][:, row, 0, :], w2_raw[:, row, :]).then_inc(split_chain, 1)
                        wait_alone(pool, (split_chain, done_ + 1))
                        nc.gpsimd.tensor_tensor(w1_lo[to][:, :, cols], w1_raw[:, :, cols],
                                                w1_hi[to][:, :, cols].bitcast(F32), ALU.subtract).then_inc(w_split, 1)
                        wait_alone(pool, (split_chain, done_ + 2))
                        nc.gpsimd.tensor_tensor(w2_both[to][:, row, 1, :], w2_raw[:, row, :],
                                                w2_both[to][:, row, 0, :].bitcast(F32),
                                                ALU.subtract).then_inc(w_split, 1)

                    def expert(e, par):
                        wait_alone(pool, (down_done, e * (UNITS * UNIT) + 1), (l_w1, e * 16 + 32), (l_w2, e * 16 + 32))
                        with pool.Fori(0, UNITS) as t:
                            split(e, par, t)
                            add(e, t)

                    with pool.Fori(0, E // 2 - 1) as pair:
                        expert(pair * 2, 0)
                        expert(pair * 2 + 1, 1)
                    expert(E - 2, 0)
                    for b in range(B):
                        with pool.Fori(0, UNITS // B // 2) as half:
                            for i in range(2):
                                t = half * 2 + (b * (UNITS // B) + i)
                                add(E - 1, t)
                                u = (E - 1) * UNITS + t
                                wait_alone(pool, (dve_evict, 2 * u + 2 + 2), (pool_evict, 2 * u + 2 + 2))
                                unit_acc = acc[:, bass.ds(t * UNIT, UNIT), :]
                                nc.gpsimd.tensor_tensor(unit_acc, unit_acc,
                                                        gb_rows[:, b:b + 1, :].broadcast_to([P, UNIT, D]),
                                                        ALU.mult).then_inc(pool_scaled, 1)
                                wait_alone(pool, (pool_scaled, t + 1), (l_x1[i], half * 16 + (b * (UNITS // B // 2) + 1) * 16))
                                nc.gpsimd.tensor_tensor(unit_acc, unit_acc, slabs[i],
                                                        ALU.add).then_inc(pool_out, 1)


def kernel(L0_attn_x, L0_attn_Wq, L0_attn_Wk, L0_attn_Wv, L0_attn_Wo, L0_ffn_Wg, L0_ffn_bg, L0_ffn_Wt, L0_ffn_bt,
           L0_ffn_W1, L0_ffn_b1, L0_ffn_W2, L0_ffn_b2, L0_c, L0_wmod):
    import numpy as np
    import concourse.bacc as bacc
    from concourse.bass_utils import run_bass_kernel_spmd

    A = np.asarray
    order = np.r_[0:HS:2, 1:HS:2]
    heads = [A(L0_attn_Wq)[0][order], A(L0_attn_Wq)[1][order], A(L0_attn_Wk)[order], A(L0_attn_Wv)]
    theta = np.float32(10000.0) ** (np.float32(-2.0) * np.arange(0, HS, 2, dtype=np.float32) / np.float32(HS))
    angles = np.arange(T, dtype=np.float32)[:, None] * theta.astype(np.float32)[None, :]
    rows = np.arange(P)
    mask = np.where(rows[None, :] > rows[:, None], np.float32(-2.0 ** 127), np.float32(0))
    low = (rows % (4 * E) // E == 1).astype(np.float32)
    arrays = {
        "x": A(L0_attn_x),
        "wqkvT": np.concatenate(heads, axis=0).T,
        "woT": A(L0_attn_Wo).T,
        "wgt": np.concatenate([A(L0_ffn_Wg), A(L0_ffn_Wt)], axis=1),
        "bgt": np.concatenate([A(L0_ffn_bg), A(L0_ffn_bt)]),
        "w1": A(L0_ffn_W1),
        "b1": A(L0_ffn_b1).reshape(E * FT, P).T,
        "w2": A(L0_ffn_W2),
        "b2": A(L0_ffn_b2),
        "c": A(L0_c).reshape(B, KD, P).transpose(2, 1, 0),
        "wmod": A(L0_wmod),
        "cos": np.cos(angles.astype(np.float64)).astype(np.float32),
        "sin": np.sin(angles.astype(np.float64)).astype(np.float32),
        "ident": np.eye(P, dtype=np.float32),
        "mask": mask.astype(np.float32),
        "lo_rows": np.stack([low, 1 - low], axis=1),
    }
    arrays = {f"{n}_dram": np.ascontiguousarray(a) for n, a in arrays.items()}
    nc = bacc.Bacc("TRN2", target_bir_lowering=False, num_devices=1)
    args = [nc.dram_tensor(n, a.shape, mybir.dt.from_np(a.dtype), kind="ExternalInput").ap()
            for n, a in arrays.items()]
    args.append(nc.dram_tensor("out_dram", (B, T, D), F32, kind="ExternalOutput").ap())
    adaln_block(nc, *args)
    r = run_bass_kernel_spmd(nc, [arrays], core_ids=[0])
    return r.results[0]["out_dram"]
```

```python
from contextlib import ExitStack

import concourse.bass as bass
from concourse import mybir

F32 = mybir.dt.float32
F32R = mybir.dt.float32r
ALU = mybir.AluOpType
ACT = mybir.ActivationFunctionType
AX_X = mybir.AxisListType.X

P = 128
B, T, D = 2, 2048, 256
HS, NH = 128, 2
E, FF = 8, 1024
KD = D // P
NT = T // P
TILES = B * NT
FT = FF // P
UNIT = 4
UTOK = UNIT * P
UNITS = TILES // UNIT
QKV = (NH + 2) * HS
ROT = (NH + 1) * HS
SCALE = float(HS) ** -0.5
EPS = 1e-5
XS = 6
PT_SLOTS = 3
NG = E + 1
MAX_THRESHOLD = 0.125
GT = NT // 2
WO_STEPS = 7
G1_STEPS, G2_STEPS = 2, 12


def ok(t):
    return 0 <= t < NT


def groups_of(t):
    return (t + 2) // 2


def blocks_of(t, g):
    return range(2 * g, min(2 * g + 2, t + 1))


def chunks_of(t):
    return t // 4 + 1


def stages_by_kind():
    kinds = {k: [(k, t, 0) for t in range(NT)] for k in ("hT", "qkv", "rope", "rotT", "O", "Y", "gate", "h2")}
    kinds.update({k: [(k, s, 0) for s in range(-3, NT + 2)] for k in ("norm", "rstd", "xn")})
    kinds["wo"] = [("wo", 0, 0)]
    kinds.update({k: [(k, half, 0) for half in range(NT // GT)] for k in ("G1", "G2")})
    kinds["normT"] = [("normT", s, 0) for s in range(-2, NT + 3)]
    for k in ("S", "M", "E"):
        kinds[k] = [(k, t, 4 * h + c) for t in range(NT) for h in range(NH) for c in range(chunks_of(t))]
    kinds["N"] = [("N", t, h) for t in range(NT) for h in range(NH)]
    for k in ("T", "PV"):
        kinds[k] = [(k, t, g) for t in range(NT) for g in range(groups_of(t))]
    return kinds


STAGES = stages_by_kind()
AT = {stage: n + 1 for stages in STAGES.values() for n, stage in enumerate(stages)}
TOTAL = {kind: len(stages) for kind, stages in STAGES.items()}


def parts_of(stage):
    kind, t, g = stage
    head, chunk = divmod(g, 4)
    w = min(512, (t + 1) * P - chunk * 512)
    if kind == "S":
        was = t if head else t - 1
        after = [("rotT", t, 0, "DVE")]
        if ok(was) and chunk < chunks_of(was):
            after.append(("E", was, (1 - head) * 4 + chunk, "ACT"))
        return [("PE", 1.25 * w + 53 * (chunk == chunks_of(t) - 1), after)]
    if kind == "M":
        return [("DVE", 65 + 1.04 * w, [("S", t, g, "PE")])]
    if kind == "N":
        return [("DVE", 270, [("M", t, g * 4 + chunks_of(t) - 1, "DVE")])]
    if kind == "E":
        return [("ACT", 230 + 0.83 * w, [("N", t, head, "DVE"), ("T", t - 2, groups_of(t - 2) - 1, "PE"),
                                         ("Y", t - 4, 0, "DVE")])]
    if kind == "T":
        n = len(blocks_of(t, g))
        return [("PE", 214 * n, [("E", t, 4 + g // 2, "ACT")]),
                ("ACT", 60 + 210 * n, [("T", t, g, "PE")]),
                ("DVE", 70 + 266 * n, [("T", t, g, "ACT")])]
    if kind == "PV":
        first = [("O", t - 1, 0, "DVE"), ("gate", t - 3, 0, "DVE"), ("qkv", t, 0, "POOL")]
        return [("PE", 320 * len(blocks_of(t, g)), [("T", t, g, "DVE")] + first * (g == 0))]
    if kind == "O":
        return [("ACT", 270, [("PV", t, groups_of(t) - 1, "PE"), ("Y", t - 1, 0, "PE")]),
                ("DVE", 330, [("O", t, 0, "ACT")])]
    if kind == "Y":
        return [("PE", 640, [("O", t, 0, "DVE"), ("xn", t, 0, "DVE") if t >= 2 else ("wo", 0, 0, "DVE")]),
                ("DVE", 1350, [("Y", t, 0, "PE")])]
    if kind == "gate":
        return [("PE", 430, [("normT", t + 3, 0, "ACT"), ("O", t + 2, 0, "DVE"), ("gate", t - 1, 0, "DVE")]),
                ("DVE", 80, [("gate", t, 0, "PE")])]
    if kind == "qkv":
        return [("PE", 1280, [("hT", t, 0, "POOL"), ("rope", t - 1, 0, "POOL")]),
                ("ACT", 640, [("qkv", t, 0, "PE"), ("rope", t - 1, 0, "POOL"), ("qkv", t - 1, 0, "POOL")]),
                ("POOL", 420, [("qkv", t, 0, "ACT")])]
    if kind == "rope":
        return [("POOL", 1900, [("qkv", t, 0, "ACT"), ("rope", t - 1, 0, "DVE")]),
                ("DVE", 540, [("rope", t, 0, "POOL"), ("rotT", t - 1, 0, "PE")])]
    if kind == "rotT":
        return [("PE", 320, [("rope", t, 0, "DVE"), ("S", t - 2, 4 + chunks_of(t - 2) - 1, "PE")]),
                ("ACT", 420, [("rotT", t, 0, "PE"), ("S", t - 2, 4 + chunks_of(t - 2) - 1, "PE")]),
                ("DVE", 540, [("rotT", t, 0, "ACT")])]
    if kind == "wo":
        return [("DVE", 4500, [("norm", 1, 0, "DVE")])]
    if kind == "G1":
        return [("DVE", 350, [("gate", t * GT + GT - 1, 0, "DVE"), ("G2", t - 1, 0, "DVE")]),
                ("ACT", 560, [("G1", t, 0, "DVE")])]
    if kind == "G2":
        return [("DVE", 1700, [("G1", t, 0, "ACT")])]
    n = ok(t + 3) + ok(t - 2)
    if kind == "norm":
        return [("DVE", 410 * n + 200, [("xn", t - 1, 0, "DVE"), ("Y", t - 2, 0, "DVE")]),
                ("POOL", 180, [("norm", t, 0, "DVE")]),
                ("ACT", 330, [("norm", t, 0, "POOL")])]
    if kind == "rstd":
        return [("POOL", 1000, [("norm", t, 0, "ACT"), ("xn", t - 1, 0, "DVE")])]
    if kind == "xn":
        return [("DVE", 330 * n, [("rstd", t, 0, "POOL"), ("normT", t, 0, "PE")])]
    n = ok(t + 2) + ok(t - 3)
    if kind == "normT":
        before = [("hT", t + 1, 0, "POOL"), ("h2", t - 4, 0, "POOL"), ("gate", t - 4, 0, "PE")]
        return [("PE", 214 * n, [("xn", t - 1, 0, "DVE")] + before),
                ("ACT", 685 * n, [("normT", t, 0, "PE")] + before)]
    if kind == "hT":
        return [("ACT", 310, [("normT", t - 2, 0, "ACT"), ("qkv", t - 1, 0, "PE")]),
                ("POOL", 690, [("hT", t, 0, "ACT")])]
    return [("ACT", 310, [("normT", t + 3, 0, "ACT")]), ("POOL", 690, [("h2", t, 0, "ACT")])]


PATIENCE = {
    "PE": {"qkv": 510, "rotT": -30, "Y": 260, "gate": 220, "normT": -10, "S": 280, "T": 90, "PV": 380},
    "ACT": {"hT": -72160, "qkv": -71370, "rotT": -35320, "O": -92220, "h2": -29710, "norm": -840, "G1": 3240,
        "normT": 990, "E": -460, "T": -41540},
    "DVE": {"rope": -460, "rotT": 20, "O": -780, "Y": -105530, "gate": -44320, "norm": 160, "xn": -190,
        "wo": -233350, "G1": -72790, "G2": -144560, "M": -440, "N": -16550, "T": -250},
    "POOL": {"hT": -175000, "qkv": -36740, "rope": -43800, "h2": -125100, "norm": -128250, "rstd": -73670},
}
PASS_ON = 220


def order_stages(patience):
    queues, ends, free, orders = {}, {}, {}, {}
    for stages in STAGES.values():
        for stage in stages:
            for engine, length, after in parts_of(stage):
                queues.setdefault((engine, stage[0]), []).append(
                    (stage, length, [x for x in after if x[:3] in AT]))
                free[engine], orders[engine] = 0.0, []
    heads = {q: 0 for q in queues}
    last_in = {"T0": None, "T1": None, "M": None}
    turn = 0
    reader = {"T": "DVE", "normT": "ACT", "qkv": "ACT", "Y": "DVE", "rotT": "DVE"}
    while heads:
        best = None
        for (engine, kind), i in heads.items():
            stage, length, after = queues[engine, kind][i]
            if engine == "PE" and kind in ("T", "normT"):
                bank = f"T{turn % 2}"
            elif engine == "PE" and kind in ("qkv", "Y", "rotT"):
                bank = "M"
            else:
                bank = None
            if bank and last_in[bank]:
                after = after + [(*last_in[bank], reader[last_in[bank][0]])]
            if kind == "T" and engine in ("PE", "ACT") and i >= PT_SLOTS:
                after = after + [(*STAGES["PV"][i - PT_SLOTS], "PE")]
            if any(x not in ends for x in after):
                continue
            start = max([free[engine]] + [ends[x] + (PASS_ON if x[3] != engine else 60) for x in after
                                          if not (engine == "PE" and kind == "T" and x[0] == "PV")])
            rank = (start + patience[engine].get(kind, 0), start)
            if best is None or rank < best[0]:
                best = (rank, engine, kind, stage, start, length, bank)
        _, engine, kind, stage, start, length, bank = best
        ends[(*stage, engine)] = free[engine] = start + length
        orders[engine].append(stage)
        if bank:
            last_in[bank] = stage
            turn += bank != "M"
        heads[engine, kind] += 1
        if heads[engine, kind] == len(queues[engine, kind]):
            del heads[engine, kind]
    return orders, max(free.values())


ORDER, _ = order_stages(PATIENCE)


def turns(kinds, banks):
    bank, before, last = {}, {}, [None] * banks
    for n, stage in enumerate(stage for stage in ORDER["PE"] if stage[0] in kinds):
        bank[stage], before[stage] = n % banks, last[n % banks]
        last[n % banks] = stage
    return bank, before


T_BANK, T_BEFORE = turns(("T", "normT"), 2)
_, M_BEFORE = turns(("qkv", "Y", "rotT"), 1)


def adaln_block(nc, x, wqkvT, woT, wgt, bgt, w1, b1, w2, b2, c, wmod, cos, sin, ident, mask, out):
    xf = x.rearrange("b (t p) d -> p (b t) d", p=P)
    of = out.rearrange("b (t p) d -> p (b t) d", p=P)
    x1_dram = nc.dram_tensor("x1_scratch", [P, TILES, D], F32).ap()

    outer = ExitStack()
    with outer:
        def sem(name):
            return outer.enter_context(nc.semaphore(name))

        def psum(name, shape):
            return outer.enter_context(nc.psum_tensor(name, shape, F32))

        def keep(name, shape, dt=F32):
            return outer.enter_context(nc.sbuf_tensor(name, shape, dt))

        score_ps = psum("score_ps", [P, 4, 512])
        tr_ps = psum("tr_ps", [P, 2, 512])
        o_ps = psum("o_ps", [P, 512])
        m_ps = psum("m_ps", [P, 512])

        h2_hi = keep("h2_hi", [P, KD, TILES * P], F32R)
        h2_lo = keep("h2_lo", [P, KD, TILES * P], F32R)
        w1_raw = keep("w1_raw", [P, KD, FF])
        ident_sb = keep("ident_sb", [P, P])
        gates = keep("gates", [P, TILES, E])
        out_gates = keep("out_gates", [P, B, 2 * D])
        b1_cols = keep("b1_cols", [P, E * FT])
        probs_even = keep("probs_even", [P, NH, T])
        w2_raw = probs_even[:, 0, :].rearrange("p (f d) -> p f d", f=FT)

        s_ld = [sem(f"s_ld{i}") for i in range(13)]
        (l_ident, l_c, l_wmod, l_wqkv, l_wo, l_cos, l_sin, l_mask, l_wgt, l_bgt, l_b1, l_w1, l_wgates) = s_ld
        s_x = [sem(f"s_x{i}") for i in range(XS)]
        s_st = [sem(f"s_st{i}") for i in range(2)]
        s_pre_e = sem("s_pre_e")
        s_pre_a = sem("s_pre_a")
        s_pre_d = sem("s_pre_d")
        s_pre_p = sem("s_pre_p")
        s_batch = sem("s_batch")
        dve_wo = sem("dve_wo")
        pe_S, pe_T, pe_PV = sem("pe_S"), sem("pe_T"), sem("pe_PV")
        pe_qkv, pe_rotT, pe_Y, pe_gate = sem("pe_qkv"), sem("pe_rotT"), sem("pe_Y"), sem("pe_gate")
        pe_normT = sem("pe_normT")
        act_E, act_T, act_O = sem("act_E"), sem("act_T"), sem("act_O")
        act_hT, act_qkv, act_V = sem("act_hT"), sem("act_qkv"), sem("act_V")
        act_rot, act_h2, act_ln, act_rstd = sem("act_rot"), sem("act_h2"), sem("act_ln"), sem("act_rstd")
        dve_M, dve_top, dve_N = sem("dve_M"), sem("dve_top"), sem("dve_N")
        dve_sum = sem("dve_sum")
        dve_T, dve_O, dve_rot = sem("dve_T"), sem("dve_O"), sem("dve_rot")
        dve_logits, act_hf = sem("dve_logits"), sem("act_hf")
        dve_recip, dve_y0, dve_x1 = sem("dve_recip"), sem("dve_y0"), sem("dve_x1")
        dve_stats, dve_norm = sem("dve_stats"), sem("dve_norm")
        pool_sin, dve_even = sem("pool_sin"), sem("dve_even")
        pool_cos, dve_odd = sem("pool_cos"), sem("dve_odd")
        dve_G1, act_G1, dve_G2 = sem("dve_G1"), sem("act_G1"), sem("dve_G2")
        pool_hT, pool_V, pool_h2 = sem("pool_hT"), sem("pool_V"), sem("pool_h2")
        pool_var, pool_ln, dve_xn = sem("pool_var"), sem("pool_ln"), sem("dve_xn")
        first_w1, first_w2, acc_zero = sem("first_w1"), sem("first_w2"), sem("acc_zero")
        dve_bias, l_b2 = sem("dve_bias"), [sem(f"l_b2_{i}") for i in range(2)]
        l_w2 = sem("l_w2")
        split_chain, w_split = sem("split_chain"), sem("w_split")
        up_done, up_free, lo_done, h_free = sem("up_done"), sem("up_free"), sem("lo_done"), sem("h_free")
        g_done = sem("g_done")
        down_done, dve_first, dve_evict = sem("down_done"), sem("dve_first"), sem("dve_evict")
        act_evict, pool_first, pool_evict = sem("act_evict"), sem("pool_first"), sem("pool_evict")
        pool_scaled, pool_out, dve_out = sem("pool_scaled"), sem("pool_out"), sem("dve_out")
        l_x1 = [sem(f"l_x1_{i}") for i in range(2)]
        s_out = [sem(f"s_out{i}") for i in range(2)]

        def wait_alone(eng, *waits):
            waits = [(w, v if isinstance(v, int) else eng.to_reg(v)) for w, v in waits]
            eng.wait_ge(l_ident, 16)
            for w in waits:
                eng.wait_ge(*w)

        attention = ExitStack()
        with attention:
            def sb(name, shape, dt=F32):
                return attention.enter_context(nc.sbuf_tensor(name, shape, dt))

            k_hi, k_lo = sb("k_hi", [P, T], F32R), sb("k_lo", [P, T], F32R)
            v_hi, v_lo = sb("v_hi", [P, NT, HS], F32R), sb("v_lo", [P, NT, HS], F32R)
            probs = [probs_even, sb("probs_odd", [P, NH, T])]
            wmod_raw = probs[0][:].rearrange("p h t -> p (h t)")[:, 0:KD * 6 * D].rearrange(
                "p (k n) -> p k n", k=KD)
            wqkv_raw = probs[1][:, 0, 0:KD * QKV].rearrange("p (k n) -> p k n", k=KD)
            s_rows = probs[1][:, 1, 0:KD * B * P].rearrange("p (k b n) -> p k b n", k=KD, b=B)
            pT_hi, pT_lo = sb("pT_hi", [P, PT_SLOTS, 512], F32R), sb("pT_lo", [P, PT_SLOTS, 512], F32R)
            cos_sb, sin_sb = (w1_raw[:, i, :].rearrange("p (t i) -> p t i", t=NT) for i in range(2))
            wqkv_hi, wqkv_lo = sb("wqkv_hi", [P, KD, QKV], F32R), sb("wqkv_lo", [P, KD, QKV], F32R)
            wo_raw, wo_ga = sb("wo_raw", [P, NH, D]), sb("wo_ga", [P, NH, D])
            wo_hi, wo_lo = sb("wo_hi", [P, NH, D], F32R), sb("wo_lo", [P, NH, D], F32R)
            mask_raw, mask_r, ident_r = sb("mask_raw", [P, P]), sb("mask_r", [P, P], F32R), sb("ident_r", [P, P], F32R)
            wgt_sb, bgt_sb, logits = sb("wgt_sb", [P, KD, NG]), sb("bgt_sb", [P, NG]), sb("logits", [P, NT, NG])
            less_max, exps, weights = (sb(n, [P, GT, E]) for n in ("less_max", "exps", "weights"))
            exp_z, row_a, row_b, thr_a, thr_b = (sb(n, [P, GT]) for n in ("exp_z", "row_a", "row_b", "thr_a", "thr_b"))
            c_cols = sb("c_cols", [P, KD, B])
            c_exp, c_sig, c_rec, s_cols = (sb(n, [P, KD, B]) for n in ("c_exp", "c_sig", "c_rec", "s_cols"))
            mod_cols = sb("mod_cols", [P, B, 4, KD])
            mod_b = sb("mod_b", [P, 4, KD])
            x_sb = sb("x_sb", [P, XS, D])
            x1_sb, y0_sb = sb("x1_sb", [P, 2, D]), sb("y0_sb", [P, D])
            xn = sb("xn", [P, 2, D])
            hf = sb("hf", [P, 2, KD, P])
            hT_hi, hT_lo = sb("hT_hi", [P, KD, P], F32R), sb("hT_lo", [P, KD, P], F32R)
            qkv = sb("qkv", [P, QKV])
            rot_c, rot_s, rot = sb("rot_c", [P, ROT]), sb("rot_s", [P, ROT]), sb("rot", [P, ROT])
            q_hi, q_lo = sb("q_hi", [P, 2, NH * P], F32R), sb("q_lo", [P, 2, NH * P], F32R)
            o_hi, o_lo = sb("o_hi", [P, NH * P], F32R), sb("o_lo", [P, NH * P], F32R)
            top, neg = sb("top", [P, NH, 5]), sb("neg", [P, NH])
            sums, sum_sb, rsums = sb("sums", [P, 4, NH, 4]), sb("sum_sb", [P, NH]), sb("rsums", [P, NH])
            stats, mv = sb("stats", [P, 2, 6]), sb("mv", [P, 2, 2])
            var_eps, ln_v, rs0, rs1, rs2, rs3, rstd = (sb(n, [P, 2]) for n in (
                "var_eps", "ln_v", "rs0", "rs1", "rs2", "rs3", "rstd"))


            def done(sem_, b, kind, t, g=0, times=1, minus=0):
                return (sem_, b * (TOTAL[kind] * times) + AT[kind, t, g] * times - minus)

            def batch_end(eng, b):
                wait_alone(eng, (act_h2, b * NT + NT), (pool_h2, b * NT + NT),
                           (dve_G2, b * (NT // GT * G2_STEPS) + NT // GT * G2_STEPS),
                           (dve_x1, b * NT + NT))

            attention_block = ExitStack()
            block = attention_block.enter_context(nc.Block())

            def free_after(n):
                return max(t for t in range(NT) if t % XS == n % XS)

            @block.sync
            def _(sp):
                sp.dma_start(ident_sb[:], ident).then_inc(l_ident, 16)
                sp.dma_start(c_cols[:], c).then_inc(l_c, 16)
                for k in range(KD):
                    for g in range(2):
                        sp.dma_start(wmod_raw[:, k, (3 * g + 2) * D:(3 * g + 3) * D],
                                     wmod[k * P:(k + 1) * P, (3 * g + 2) * D:(3 * g + 3) * D]).then_inc(l_wgates, 16)
                sp.dma_start(x_sb[:, 0:1, :], xf[:, 0:1, :]).then_inc(s_x[0], 16)
                for k in range(KD):
                    for g in range(2):
                        sp.dma_start(wmod_raw[:, k, 3 * g * D:(3 * g + 2) * D],
                                     wmod[k * P:(k + 1) * P, 3 * g * D:(3 * g + 2) * D]).then_inc(l_wmod, 16)
                sp.dma_start(wqkv_raw, wqkvT.rearrange("(k p) n -> p k n", p=P)).then_inc(l_wqkv, 16)
                sp.dma_start(mask_raw[:], mask).then_inc(l_mask, 16)
                for t in range(1, XS):
                    sp.dma_start(x_sb[:, t:t + 1, :], xf[:, t:t + 1, :]).then_inc(s_x[t], 16)
                sp.dma_start(cos_sb[:], cos.rearrange("(t p) n -> p t n", p=P)).then_inc(l_cos, 16)
                sp.dma_start(sin_sb[:], sin.rearrange("(t p) n -> p t n", p=P)).then_inc(l_sin, 16)
                sp.dma_start(wo_raw[:], woT.rearrange("(h p) n -> p h n", p=P)).then_inc(l_wo, 16)
                sp.dma_start(bgt_sb[:], bgt.partition_broadcast(P)).then_inc(l_bgt, 16)
                sp.dma_start(wgt_sb[:], wgt.rearrange("(k p) n -> p k n", p=P)).then_inc(l_wgt, 16)
                sp.dma_start(b1_cols[:], b1).then_inc(l_b1, 16)
                for b in range(B):
                    for t in range(NT):
                        if b == B - 1 and t == NT - 1:
                            sp.wait_ge(*done(pool_cos, b, "rope", t))
                            sp.wait_ge(*done(pool_sin, b, "rope", t))
                            sp.dma_start(w1_raw[:], w1[0].rearrange("(k p) n -> p k n", p=P)).then_inc(l_w1, 16)
                            sp.wait_ge(*done(pe_T, b, "T", NT - 2, groups_of(NT - 2) - 1))
                            sp.dma_start(w2_raw, w2[0].rearrange("(f p) n -> p f n", p=P)).then_inc(l_w2, 16)
                        sp.wait_ge(*done(dve_x1, b, "Y", t))
                        sp.dma_start(x1_dram[:, b * NT + t:b * NT + t + 1, :],
                                     x1_sb[:, t % 2:t % 2 + 1, :]).then_inc(s_st[t % 2], 16)
                        new = [(b, t + XS)] if t + XS < NT else [(b + 1, n) for n in range(XS) if free_after(n) == t]
                        for to, n in new:
                            if to < B:
                                sp.dma_start(x_sb[:, n % XS:n % XS + 1, :],
                                             xf[:, to * NT + n:to * NT + n + 1, :]).then_inc(s_x[n % XS], 16)
                for s in s_st:
                    sp.wait_ge(s, B * (NT // 2) * 16 + 16)

            def x_loaded(b, t):
                per = len(range(t % XS, NT, XS))
                return s_x[t % XS], b * (per * 16) + (t // XS + 1) * 16

            @block.tensor
            def _(pe):
                pe.wait_ge(s_pre_d, 4)
                pe.wait_ge(l_wgates, 16 * 2 * KD)
                for b in range(B):
                    for n, part in enumerate((2, 5)):
                        for k in range(KD):
                            last = nc.tensor.matmul(score_ps[:, b, n * D:(n + 1) * D], s_rows[:, k, b, :],
                                                    wmod_raw[:, k, part * D:(part + 1) * D],
                                                    start=(k == 0), stop=(k == KD - 1))
                last.then_inc(s_pre_e, 1)
                pe.wait_ge(l_wmod, 16 * 2 * KD)
                for m, part in enumerate((1, 0, 4, 3)):
                    for j in range(KD):
                        for k in range(KD):
                            last = nc.tensor.matmul(m_ps[:, (m * KD + j) * B:(m * KD + j + 1) * B],
                                                    wmod_raw[:, k, part * D + j * P:part * D + (j + 1) * P],
                                                    s_cols[:, k, :], start=(k == 0), stop=(k == KD - 1))
                last.then_inc(s_pre_e, 1)
                pe.wait_ge(s_pre_p, 2)

                def m_bank_free(b, stage):
                    was = M_BEFORE[stage]
                    if was:
                        reader = {"qkv": act_V, "Y": dve_x1, "rotT": dve_rot}[was[0]]
                        pe.wait_ge(*done(reader, b, *was))

                def t_bank_free(b, stage):
                    was = T_BEFORE[stage]
                    if was:
                        pe.wait_ge(*done(dve_T if was[0] == "T" else act_hf, b, *was))

                with pe.Fori(0, B) as b:
                    for stage in ORDER["PE"]:
                        kind, t, g = stage
                        if kind == "S":
                            h, chunk = g // 4, g % 4
                            if g == 0:
                                pe.wait_ge(*done(act_rot, b, "rotT", t, 0, 2))
                                pe.wait_ge(*done(dve_rot, b, "rotT", t))
                            was = t if h else t - 1
                            if ok(was) and chunk < chunks_of(was):
                                pe.wait_ge(*done(act_E, b, "E", was, (1 - h) * 4 + chunk))
                            w = min(512, (t + 1) * P - chunk * 512)
                            keys = slice(chunk * 512, chunk * 512 + w)
                            diag = chunk == chunks_of(t) - 1
                            q1, q2 = (q[:, t % 2, h * P:(h + 1) * P] for q in (q_hi, q_lo))
                            o = score_ps[:, chunk, 0:w]
                            nc.tensor.matmul(o, q1, k_hi[:, keys], start=True, stop=False)
                            nc.tensor.matmul(o, q1, k_lo[:, keys], start=False, stop=False)
                            last = nc.tensor.matmul(o, q2, k_hi[:, keys], start=False, stop=not diag)
                            if diag:
                                last = nc.tensor.matmul(score_ps[:, chunk, w - P:w], ident_r[:], mask_r[:],
                                                        start=False, stop=True)
                            last.then_inc(pe_S, 1)
                        elif kind == "T":
                            pe.wait_ge(*done(act_E, b, "E", t, 4 + g // 2))
                            t_bank_free(b, stage)
                            for j in blocks_of(t, g):
                                for h in range(NH):
                                    c0 = ((j % 2) * NH + h) * P
                                    last = nc.tensor.transpose(tr_ps[:, T_BANK[stage], c0:c0 + P],
                                                               probs[t % 2][:, h, j * P:(j + 1) * P], ident_sb[:])
                            last.then_inc(pe_T, 1)
                        elif kind == "PV":
                            slot = AT["T", t, g] % PT_SLOTS
                            pe.wait_ge(*done(dve_T, b, "T", t, g))
                            if g == 0:
                                if t > 0:
                                    pe.wait_ge(*done(dve_O, b, "O", t - 1))
                                if ok(t - 3):
                                    pe.wait_ge(*done(dve_logits, b, "gate", t - 3))
                                pe.wait_ge(*done(act_V, b, "qkv", t))
                                pe.wait_ge(*done(pool_V, b, "qkv", t))
                            o = o_ps[:, 0:NH * P]
                            for j in blocks_of(t, g):
                                r = slice((j % 2) * NH * P, (j % 2 + 1) * NH * P)
                                nc.tensor.matmul(o, v_hi[:, j, :], pT_hi[:, slot, r], start=(j == 0), stop=False)
                                nc.tensor.matmul(o, v_hi[:, j, :], pT_lo[:, slot, r], start=False, stop=False)
                                last = nc.tensor.matmul(o, v_lo[:, j, :], pT_hi[:, slot, r], start=False,
                                                        stop=(j == t))
                            last.then_inc(pe_PV, 1)
                        elif kind == "gate":
                            if ok(t + 2):
                                pe.wait_ge(*done(dve_O, b, "O", t + 2))
                            elif ok(t - 1):
                                pe.wait_ge(*done(dve_logits, b, "gate", t - 1))
                            if t == 0:
                                pe.wait_ge(l_wgt, 16)
                            pe.wait_ge(*done(act_hf, b, "normT", t + 3))
                            for k in range(KD):
                                last = nc.tensor.matmul(o_ps[:, NH * P:NH * P + NG], hf[:, 1, k, :],
                                                        wgt_sb[:, k, :], start=(k == 0), stop=(k == KD - 1))
                            last.then_inc(pe_gate, 1)
                        elif kind == "qkv":
                            pe.wait_ge(*done(act_hT, b, "hT", t))
                            pe.wait_ge(*done(pool_hT, b, "hT", t))
                            m_bank_free(b, stage)
                            n = 0
                            for k in range(KD):
                                for a, w in ((hT_hi, wqkv_hi), (hT_hi, wqkv_lo), (hT_lo, wqkv_hi)):
                                    last = nc.tensor.matmul(m_ps[:], a[:, k, :], w[:, k, :], start=(n == 0),
                                                            stop=(n == 3 * KD - 1))
                                    n += 1
                            last.then_inc(pe_qkv, 1)
                        elif kind == "Y":
                            pe.wait_ge(*done(dve_O, b, "O", t))
                            if t == 0:
                                pe.wait_ge(*done(dve_wo, b, "wo", 0, 0, WO_STEPS))
                            m_bank_free(b, stage)
                            for h in range(NH):
                                for n, (a, w) in enumerate(((o_hi, wo_hi), (o_hi, wo_lo), (o_lo, wo_hi))):
                                    last = nc.tensor.matmul(m_ps[:, h * D:(h + 1) * D], a[:, h * P:(h + 1) * P],
                                                            w[:, h, :], start=(n == 0), stop=(n == 2))
                            last.then_inc(pe_Y, 1)
                        elif kind == "rotT":
                            pe.wait_ge(*done(dve_even, b, "rope", t))
                            pe.wait_ge(*done(dve_odd, b, "rope", t))
                            m_bank_free(b, stage)
                            for h in range(NH + 1):
                                last = nc.tensor.transpose(m_ps[:, h * P:(h + 1) * P], rot[:, h * P:(h + 1) * P],
                                                           ident_sb[:])
                            last.then_inc(pe_rotT, 1)
                        elif kind == "normT":
                            pe.wait_ge(*done(dve_xn, b, "xn", t - 1))
                            t_bank_free(b, stage)
                            for i, tile in enumerate((t + 2, t - 3)):
                                if ok(tile):
                                    for k in range(KD):
                                        c0 = (i * KD + k) * P
                                        last = nc.tensor.transpose(tr_ps[:, T_BANK[stage], c0:c0 + P],
                                                                   xn[:, i, k * P:(k + 1) * P], ident_sb[:])
                            last.then_inc(pe_normT, 1)
                    batch_end(pe, b)

            @block.scalar
            def _(act):
                act.preload_act_table_set("natural_log_exp_and_others")
                act.wait_ge(l_c, 16)
                nc.scalar.activation(c_exp[:], c_cols[:], ACT.Exp, scale=-1.0).then_inc(s_pre_a, 1)
                act.wait_ge(s_pre_e, 1)
                nc.scalar.activation(out_gates[:], score_ps[:, 0:B, :], ACT.Copy).then_inc(s_pre_a, 1)
                with act.Fori(0, B) as b:
                    for kind, t, g in ORDER["ACT"]:
                        if kind == "E":
                            h, chunk = g // 4, g % 4
                            act.wait_ge(*done(dve_N, b, "N", t, h))
                            if ok(t - 2):
                                act.wait_ge(*done(pe_T, b, "T", t - 2, groups_of(t - 2) - 1))
                            if ok(t - 4):
                                act.wait_ge(*done(dve_x1, b, "Y", t - 4))
                            w = min(512, (t + 1) * P - chunk * 512)
                            nc.scalar.activation(probs[t % 2][:, h, chunk * 512:chunk * 512 + w],
                                                 score_ps[:, chunk, 0:w], ACT.Exp,
                                                 bias=neg[:, h:h + 1], scale=SCALE,
                                                 accum_out=sums[:, t % 4, h, chunk:chunk + 1]).then_inc(act_E, 1)
                        elif kind == "T":
                            n = len(blocks_of(t, g)) * NH * P
                            slot = AT["T", t, g] % PT_SLOTS
                            act.wait_ge(*done(pe_T, b, "T", t, g))
                            before = AT["T", t, g] - PT_SLOTS
                            if before >= 1:
                                act.wait_ge(pe_PV, b * TOTAL["PV"] + before)
                            nc.scalar.activation(pT_hi[:, slot, 0:n], tr_ps[:, T_BANK[kind, t, g], 0:n],
                                                 ACT.Copy).then_inc(act_T, 1)
                        elif kind == "O":
                            act.wait_ge(*done(pe_PV, b, "PV", t, groups_of(t) - 1))
                            if t > 0:
                                act.wait_ge(*done(pe_Y, b, "Y", t - 1))
                            nc.scalar.activation(o_hi[:], o_ps[:, 0:NH * P], ACT.Copy).then_inc(act_O, 1)
                        elif kind == "hT":
                            act.wait_ge(*done(act_hf, b, "normT", t - 2))
                            if t > 0:
                                act.wait_ge(*done(pe_qkv, b, "qkv", t - 1))
                            nc.scalar.activation(hT_hi[:], hf[:, 0, :, :], ACT.Copy).then_inc(act_hT, 1)
                        elif kind == "qkv":
                            act.wait_ge(*done(pe_qkv, b, "qkv", t))
                            if t > 0:
                                act.wait_ge(*done(pool_cos, b, "rope", t - 1))
                                act.wait_ge(*done(pool_sin, b, "rope", t - 1))
                                act.wait_ge(*done(pool_V, b, "qkv", t - 1))
                            nc.scalar.activation(qkv[:], m_ps[:], ACT.Copy).then_inc(act_qkv, 1)
                            nc.scalar.activation(v_hi[:, t, :], m_ps[:, ROT:QKV], ACT.Copy).then_inc(act_V, 1)
                        elif kind == "norm":
                            act.wait_ge(*done(pool_var, b, "norm", t))
                            nc.scalar.activation(ln_v[:], var_eps[:], ACT.Ln).then_inc(act_ln, 1)
                            act.wait_ge(*done(act_ln, b, "norm", t))
                            nc.scalar.activation(rs0[:], ln_v[:], ACT.Exp, scale=-0.5).then_inc(act_rstd, 1)
                        elif kind == "rotT":
                            act.wait_ge(*done(pe_rotT, b, "rotT", t))
                            if ok(t - 2):
                                act.wait_ge(*done(pe_S, b, "S", t - 2, 4 + chunks_of(t - 2) - 1))
                            nc.scalar.activation(q_hi[:, t % 2, :], m_ps[:, 0:NH * P],
                                                 ACT.Copy).then_inc(act_rot, 1)
                            nc.scalar.activation(k_hi[:, t * P:(t + 1) * P], m_ps[:, NH * P:ROT],
                                                 ACT.Copy).then_inc(act_rot, 1)
                        elif kind == "normT":
                            act.wait_ge(*done(pe_normT, b, "normT", t))
                            if ok(t + 1):
                                act.wait_ge(*done(pool_hT, b, "hT", t + 1))
                            if ok(t - 4):
                                act.wait_ge(*done(pool_h2, b, "h2", t - 4))
                                act.wait_ge(*done(pe_gate, b, "gate", t - 4))
                            if t == -2:
                                act.wait_ge(s_batch, b + 1)
                            for i, tile in enumerate((t + 2, t - 3)):
                                if ok(tile):
                                    for k in range(KD):
                                        c0 = (i * KD + k) * P
                                        last = nc.scalar.activation(
                                            hf[:, i, k, :], tr_ps[:, T_BANK[kind, t, g], c0:c0 + P], ACT.Identity,
                                            scale=mod_b[:, 2 * i, k:k + 1], bias=mod_b[:, 2 * i + 1, k:k + 1])
                            last.then_inc(act_hf, 1)
                        elif kind == "G1":
                            act.wait_ge(*done(dve_G1, b, "G1", t, 0, G1_STEPS))
                            nc.scalar.activation(exps[:], less_max[:], ACT.Exp).then_inc(act_G1, 1)
                            nc.scalar.activation(exp_z[:], logits[:, t * GT:(t + 1) * GT, E], ACT.Exp,
                                                 scale=-1.0).then_inc(act_G1, 1)
                        elif kind == "h2":
                            wait_alone(act, done(act_hf, b, "normT", t + 3))
                            nc.scalar.activation(h2_hi[:, :, bass.ds(b * T + t * P, P)], hf[:, 1, :, :],
                                                 ACT.Copy).then_inc(act_h2, 1)
                    batch_end(act, b)

            @block.vector
            def _(dve):
                made = [0]

                def step(ins):
                    made[0] += 1
                    ins.then_inc(s_pre_d, 1)
                    dve.wait_ge(s_pre_d, made[0])

                dve.wait_ge(s_pre_a, 1)
                step(nc.vector.tensor_scalar_add(c_sig[:], c_exp[:], 1.0))
                step(nc.vector.reciprocal(c_rec[:], c_sig[:]))
                step(nc.vector.tensor_tensor(s_cols[:], c_cols[:], c_rec[:], ALU.mult))
                step(nc.vector.tensor_copy(s_rows, s_cols[:].unsqueeze(3).broadcast_to([P, KD, B, P])))
                dve.wait_ge(l_ident, 16)
                step(nc.vector.tensor_copy(ident_r[:], ident_sb[:]))
                step(nc.vector.memset(mv[:], 0.0))
                dve.wait_ge(s_pre_e, 2)
                step(nc.vector.tensor_copy(mod_cols[:].rearrange("p b m j -> p (m j) b"),
                                           m_ps[:, 0:4 * KD * B].rearrange("p (n b) -> p n b", b=B)))
                step(nc.vector.tensor_scalar_add(mod_cols[:, :, 0, :], mod_cols[:, :, 0, :], 1.0))
                step(nc.vector.tensor_scalar_add(mod_cols[:, :, 2, :], mod_cols[:, :, 2, :], 1.0))
                dve.wait_ge(l_mask, 16)
                step(nc.vector.tensor_copy(mask_r[:], mask_raw[:]))
                for s in s_st:
                    dve.sem_inc(s, 16)
                wide = lambda a: a[:].unsqueeze(2).broadcast_to([P, GT, E])
                with dve.Fori(0, B) as b:
                    nc.vector.tensor_copy(mod_b[:].unsqueeze(1), mod_cols[:, bass.ds(b, 1), :, :]).then_inc(s_batch, 1)
                    for kind, t, g in ORDER["DVE"]:
                        if kind == "M":
                            h, chunk = g // 4, g % 4
                            dve.wait_ge(*done(pe_S, b, "S", t, g))
                            w = min(512, (t + 1) * P - chunk * 512)
                            nc.vector.reduce_max(top[:, h, chunk:chunk + 1], score_ps[:, chunk, 0:w],
                                                 axis=AX_X).then_inc(dve_M, 1)
                        elif kind == "N":
                            n = chunks_of(t)
                            dve.wait_ge(*done(dve_M, b, "M", t, g * 4 + n - 1))
                            nc.vector.reduce_max(top[:, g, 4:5], top[:, g, 0:n], axis=AX_X).then_inc(dve_top, 1)
                            dve.wait_ge(*done(dve_top, b, "N", t, g))
                            nc.vector.tensor_scalar(neg[:, g:g + 1], top[:, g, 4:5], -SCALE, None,
                                                    ALU.mult).then_inc(dve_N, 1)
                        elif kind == "T":
                            n = len(blocks_of(t, g)) * NH * P
                            slot = AT["T", t, g] % PT_SLOTS
                            dve.wait_ge(*done(act_T, b, "T", t, g))
                            nc.vector.tensor_tensor(pT_lo[:, slot, 0:n], tr_ps[:, T_BANK[kind, t, g], 0:n],
                                                    pT_hi[:, slot, 0:n].bitcast(F32),
                                                    ALU.subtract).then_inc(dve_T, 1)
                        elif kind == "O":
                            dve.wait_ge(*done(act_O, b, "O", t))
                            nc.vector.tensor_tensor(o_lo[:], o_ps[:, 0:NH * P], o_hi[:].bitcast(F32),
                                                    ALU.subtract).then_inc(dve_O, 1)
                        elif kind == "gate":
                            if t == 0:
                                dve.wait_ge(l_bgt, 16)
                            dve.wait_ge(*done(pe_gate, b, "gate", t))
                            nc.vector.tensor_tensor(logits[:, t, :], o_ps[:, NH * P:NH * P + NG], bgt_sb[:],
                                                    ALU.add).then_inc(dve_logits, 1)
                        elif kind == "G1":
                            made = lambda n: dve.wait_ge(*done(dve_G1, b, "G1", t, 0, G1_STEPS, G1_STEPS - n))
                            tiles = slice(t * GT, (t + 1) * GT)
                            dve.wait_ge(*done(dve_logits, b, "gate", t * GT + GT - 1))
                            if t > 0:
                                dve.wait_ge(*done(dve_G2, b, "G2", t - 1, 0, G2_STEPS))
                            nc.vector.reduce_max(row_a[:], logits[:, tiles, 0:E], axis=AX_X).then_inc(dve_G1, 1)
                            made(1)
                            nc.vector.tensor_tensor(less_max[:], logits[:, tiles, 0:E], wide(row_a),
                                                    ALU.subtract).then_inc(dve_G1, 1)
                        elif kind == "G2":
                            def step(ins, n):
                                ins.then_inc(dve_G2, 1)
                                dve.wait_ge(*done(dve_G2, b, "G2", t, 0, G2_STEPS, G2_STEPS - n))

                            dve.wait_ge(*done(act_G1, b, "G1", t, 0, 2))
                            step(nc.vector.reduce_sum(row_a[:], exps[:], axis=AX_X), 1)
                            step(nc.vector.reciprocal(row_b[:], row_a[:]), 2)
                            step(nc.vector.tensor_tensor(less_max[:], exps[:], wide(row_b), ALU.mult), 3)
                            step(nc.vector.tensor_scalar_add(thr_a[:], exp_z[:], 1.0), 4)
                            step(nc.vector.reciprocal(thr_b[:], thr_a[:]), 5)
                            step(nc.vector.tensor_scalar(thr_a[:], thr_b[:], MAX_THRESHOLD, None, ALU.mult), 6)
                            step(nc.vector.tensor_tensor(exps[:], less_max[:], wide(thr_a), ALU.subtract), 7)
                            step(nc.vector.scalar_tensor_tensor(weights[:], exps[:], 0.0, exps[:],
                                                                ALU.is_ge, ALU.mult), 8)
                            step(nc.vector.reduce_sum(row_a[:], weights[:], axis=AX_X), 9)
                            step(nc.vector.scalar_tensor_tensor(row_b[:], row_a[:], 0.0, row_a[:],
                                                                ALU.is_equal, ALU.add), 10)
                            step(nc.vector.reciprocal(thr_b[:], row_b[:]), 11)
                            nc.vector.tensor_tensor(gates[:, bass.ds(b * NT + t * GT, GT), :], weights[:],
                                                    wide(thr_b), ALU.mult).then_inc(dve_G2, 1)
                        elif kind == "rope":
                            turned = lambda a, eo: a[:, 0:ROT].rearrange("p (h e i) -> p h e i", e=2,
                                                                         i=HS // 2)[:, :, eo, :]
                            dve.wait_ge(*done(pool_cos, b, "rope", t))
                            dve.wait_ge(*done(pool_sin, b, "rope", t))
                            if t > 0:
                                dve.wait_ge(*done(pe_rotT, b, "rotT", t - 1))
                            nc.vector.tensor_tensor(turned(rot, 0), turned(rot_c, 0), turned(rot_s, 1),
                                                    ALU.subtract).then_inc(dve_even, 1)
                            nc.vector.tensor_tensor(turned(rot, 1), turned(rot_c, 1), turned(rot_s, 0),
                                                    ALU.add).then_inc(dve_odd, 1)
                        elif kind == "rotT":
                            dve.wait_ge(*done(act_rot, b, "rotT", t, 0, 2))
                            nc.vector.tensor_tensor(q_lo[:, t % 2, :], m_ps[:, 0:NH * P],
                                                    q_hi[:, t % 2, :].bitcast(F32), ALU.subtract)
                            nc.vector.tensor_tensor(k_lo[:, t * P:(t + 1) * P], m_ps[:, NH * P:ROT],
                                                    k_hi[:, t * P:(t + 1) * P].bitcast(F32),
                                                    ALU.subtract).then_inc(dve_rot, 1)
                        elif kind == "Y":
                            if t > 0:
                                dve.wait_ge(*done(dve_x1, b, "Y", t - 1))
                            nc.vector.reduce_sum(sum_sb[:], sums[:, t % 4, :, 0:chunks_of(t)],
                                                 axis=AX_X).then_inc(dve_sum, 1)
                            dve.wait_ge(*done(dve_sum, b, "Y", t))
                            nc.vector.reciprocal(rsums[:], sum_sb[:]).then_inc(dve_recip, 1)
                            dve.wait_ge(*done(dve_recip, b, "Y", t))
                            dve.wait_ge(*done(pe_Y, b, "Y", t))
                            nc.vector.scalar_tensor_tensor(y0_sb[:], m_ps[:, 0:D], rsums[:, 0:1], x_sb[:, t % XS, :],
                                                           ALU.mult, ALU.add).then_inc(dve_y0, 1)
                            dve.wait_ge(*done(dve_y0, b, "Y", t))
                            if t >= 2:
                                dve.wait_ge(*done(dve_xn, b, "xn", t))
                            dve.wait_ge(s_st[t % 2], b * (NT // 2 * 16) + t // 2 * 16 + 16)
                            nc.vector.scalar_tensor_tensor(x1_sb[:, t % 2, :], m_ps[:, D:2 * D], rsums[:, 1:2],
                                                           y0_sb[:], ALU.mult, ALU.add).then_inc(dve_x1, 1)
                        elif kind == "norm":
                            s = t
                            if s > -3:
                                dve.wait_ge(*done(dve_xn, b, "xn", s - 1))
                            if ok(s + 3):
                                dve.wait_ge(*x_loaded(b, s + 3))
                                last = nc.vector.bn_stats(stats[:, 0, :], x_sb[:, (s + 3) % XS, :])
                            if ok(s - 2):
                                dve.wait_ge(*done(dve_x1, b, "Y", s - 2))
                                last = nc.vector.bn_stats(stats[:, 1, :], x1_sb[:, s % 2, :])
                            last.then_inc(dve_stats, 1)
                            wait_alone(dve, done(dve_stats, b, "norm", s))
                            for i, tile in enumerate((s + 3, s - 2)):
                                if ok(tile):
                                    last = nc.vector.bn_aggr(mv[:, i, :], stats[:, i, :])
                            last.then_inc(dve_norm, 1)
                        elif kind == "wo":
                            def step(ins, n):
                                ins.then_inc(dve_wo, 1)
                                dve.wait_ge(*done(dve_wo, b, "wo", 0, 0, WO_STEPS, WO_STEPS - n))

                            raw = out_gates[:, bass.ds(b, 1), :]
                            size = wo_ga[:].rearrange("p h d -> p (h d)").unsqueeze(1)
                            dve.wait_ge(s_pre_a, 2)
                            dve.wait_ge(l_wo, 16)
                            step(nc.vector.scalar_tensor_tensor(size, raw, -1.0, raw, ALU.mult, ALU.max), 1)
                            step(nc.vector.tensor_scalar(size, size, 0.25, None, ALU.max), 2)
                            step(nc.vector.tensor_scalar(raw, raw, 0.0, 2.0, ALU.is_ge, ALU.mult), 3)
                            step(nc.vector.scalar_tensor_tensor(raw, raw, 1.0, size, ALU.subtract, ALU.mult), 4)
                            step(nc.vector.tensor_tensor(wo_ga[:], wo_raw[:],
                                                         raw[:, :, 0:D].broadcast_to([P, NH, D]), ALU.mult), 5)
                            step(nc.vector.tensor_copy(wo_hi[:], wo_ga[:]), 6)
                            nc.vector.tensor_tensor(wo_lo[:], wo_ga[:], wo_hi[:].bitcast(F32),
                                                    ALU.subtract).then_inc(dve_wo, 1)
                        elif kind == "xn":
                            dve.wait_ge(*done(pool_ln, b, "rstd", t, 0, 4))
                            if t > -3:
                                dve.wait_ge(*done(pe_normT, b, "normT", t))
                            if ok(t + 3):
                                last = nc.vector.tensor_scalar(xn[:, 0, :], x_sb[:, (t + 3) % XS, :], mv[:, 0, 0:1],
                                                               rstd[:, 0:1], ALU.subtract, ALU.mult)
                            if ok(t - 2):
                                last = nc.vector.tensor_scalar(xn[:, 1, :], x1_sb[:, t % 2, :], mv[:, 1, 0:1],
                                                               rstd[:, 1:2], ALU.subtract, ALU.mult)
                            last.then_inc(dve_xn, 1)
                    batch_end(dve, b)

            @block.gpsimd
            def _(pool):
                pool.wait_ge(l_wqkv, 16)
                nc.gpsimd.tensor_copy(wqkv_hi[:], wqkv_raw).then_inc(s_pre_p, 1)
                pool.wait_ge(s_pre_p, 1)
                nc.gpsimd.tensor_tensor(wqkv_lo[:], wqkv_raw, wqkv_hi[:].bitcast(F32),
                                        ALU.subtract).then_inc(s_pre_p, 1)
                pool.wait_ge(s_pre_p, 2)
                with pool.Fori(0, B) as b:
                    for kind, t, g in ORDER["POOL"]:
                        if kind == "hT":
                            pool.wait_ge(*done(act_hT, b, "hT", t))
                            nc.gpsimd.tensor_tensor(hT_lo[:], hf[:, 0, :, :], hT_hi[:].bitcast(F32),
                                                    ALU.subtract).then_inc(pool_hT, 1)
                        elif kind == "qkv":
                            pool.wait_ge(*done(act_V, b, "qkv", t))
                            nc.gpsimd.tensor_tensor(v_lo[:, t, :], qkv[:, ROT:QKV], v_hi[:, t, :].bitcast(F32),
                                                    ALU.subtract).then_inc(pool_V, 1)
                        elif kind == "rope":
                            half = lambda a: a[:, 0:ROT].rearrange("p (n i) -> p n i", i=HS // 2)
                            if t == 0:
                                pool.wait_ge(l_cos, 16)
                                pool.wait_ge(l_sin, 16)
                            pool.wait_ge(*done(act_qkv, b, "qkv", t))
                            if t > 0:
                                pool.wait_ge(*done(dve_odd, b, "rope", t - 1))
                            for to, table, made in ((rot_c, cos_sb, pool_cos), (rot_s, sin_sb, pool_sin)):
                                nc.gpsimd.tensor_tensor(half(to), half(qkv),
                                                        table[:, t:t + 1, :].broadcast_to(
                                                            [P, 2 * (NH + 1), HS // 2]),
                                                        ALU.mult).then_inc(made, 1)
                        elif kind == "norm":
                            wait_alone(pool, done(dve_norm, b, "norm", t))
                            nc.gpsimd.tensor_scalar(var_eps[:], mv[:, :, 1], EPS, None, ALU.add).then_inc(pool_var, 1)
                        elif kind == "rstd":
                            made = lambda n: done(pool_ln, b, "rstd", t, 0, 4, 4 - n)
                            pool.wait_ge(*done(act_rstd, b, "norm", t))
                            nc.gpsimd.tensor_tensor(rs1[:], rs0[:], rs0[:], ALU.mult).then_inc(pool_ln, 1)
                            pool.wait_ge(*made(1))
                            nc.gpsimd.tensor_tensor(rs2[:], rs1[:], var_eps[:], ALU.mult).then_inc(pool_ln, 1)
                            wait_alone(pool, made(2))
                            nc.gpsimd.tensor_scalar(rs3[:], rs2[:], -0.5, 1.5, ALU.mult, ALU.add).then_inc(pool_ln, 1)
                            pool.wait_ge(*made(3))
                            if t > -3:
                                pool.wait_ge(*done(dve_xn, b, "xn", t - 1))
                            nc.gpsimd.tensor_tensor(rstd[:], rs0[:], rs3[:], ALU.mult).then_inc(pool_ln, 1)
                        elif kind == "h2":
                            wait_alone(pool, done(act_h2, b, "h2", t))
                            tok = bass.ds(b * T + t * P, P)
                            nc.gpsimd.tensor_tensor(h2_lo[:, :, tok], hf[:, 1, :, :], h2_hi[:, :, tok].bitcast(F32),
                                                    ALU.subtract).then_inc(pool_h2, 1)
                    batch_end(pool, b)

            attention_block.close()

        mixture = ExitStack()
        with mixture:
            def mx(name, shape, dt=F32, ctx=mixture):
                return ctx.enter_context(nc.sbuf_tensor(name, shape, dt))

            w1_hi = [mx(f"w1_hi{i}", [P, KD, FF], F32R) for i in range(2)]
            w1_lo = [mx(f"w1_lo{i}", [P, KD, FF], F32R) for i in range(2)]
            acc = mx("acc", [P, TILES, D])
            g_sb = probs_even[:, 1, 0:2 * UTOK].rearrange("p (n k) -> p n k", n=2)
            y_sb = probs_even[:, 1, 2 * UTOK:2 * UTOK + 4 * D].rearrange("p (n k) -> p n k", n=2)
            h_hi, h_lo = mx("h_hi", [P, 4, UTOK], F32R), mx("h_lo", [P, 4, UTOK], F32R)
            w2_both = [mx("w2_both0", [P, FT, 2, D], F32R)]

            w2_both.append(mx("w2_both1", [P, FT, 2, D], F32R))
            b2_rows = mx("b2_rows", [P, 2, D])
            up_ps = [score_ps[:, i, :] for i in range(4)]
            down_ps = [tr_ps[:, 0, :], tr_ps[:, 1, :], o_ps[:], m_ps[:]]
            slabs = [w1_raw[:].rearrange("p k n -> p (k n)")[:, i * UNIT * D:(i + 1) * UNIT * D].rearrange(
                "p (t d) -> p t d", t=UNIT) for i in range(2)]

            def experts(eng, unit):
                def expert(e, par, last):
                    with eng.Fori(0, UNITS - 1) as t:
                        unit(e, par, t, (e, par, t + 1), last)
                    unit(e, par, UNITS - 1, None if last else (e + 1, 1 - par, 0), last)

                with eng.Fori(0, E // 2 - 1) as pair:
                    expert(pair * 2, 0, False)
                    expert(pair * 2 + 1, 1, False)
                expert(E - 2, 0, False)
                expert(E - 1, 1, True)

            def hidden(e, t, f):
                return e * (UNITS * FT) + t * FT + f

            AHEAD = 2

            def gate_of(e, t, j):
                return gates[:].rearrange("p t e -> p (t e)")[:, bass.ds(t * (UNIT * E) + (j * E + e), 1)]

            def wait_slot(eng, e, t, f):
                u = e * UNITS + t
                if f >= 4:
                    wait_alone(eng, (h_free, u * (FT - 1) + (f - 4) + 1 + 3))
                elif f == 3:
                    wait_alone(eng, (down_done, u * UNIT + 1))
                else:
                    wait_alone(eng, (h_free, u * (FT - 1) + f + 1))

            with nc.Block() as block:
                @block.sync
                def _(sp):
                    for e in range(2):
                        sp.dma_start(b2_rows[:, e:e + 1, :], b2[e:e + 1].partition_broadcast(P)).then_inc(l_b2[e], 16)
                    sp.wait_ge(first_w1, 2)
                    sp.dma_start(w1_raw[:], w1[1].rearrange("(k p) n -> p k n", p=P)).then_inc(l_w1, 16)
                    sp.wait_ge(first_w2, 2)
                    sp.dma_start(w2_raw, w2[1].rearrange("(f p) n -> p f n", p=P)).then_inc(l_w2, 16)
                    with sp.Fori(0, E // 2 - 1) as pair:
                        for par in range(2):
                            e = pair * 2 + par
                            sp.wait_ge(w_split, (e + 1) * (2 * UNITS))
                            sp.dma_start(w1_raw[:].unsqueeze(1), w1[bass.ds(e + 2, 1)].rearrange(
                                "e (k p) n -> p e k n", p=P)).then_inc(l_w1, 16)
                            sp.dma_start(w2_raw.unsqueeze(1), w2[bass.ds(e + 2, 1)].rearrange(
                                "e (f p) n -> p e f n", p=P)).then_inc(l_w2, 16)
                            sp.wait_ge(dve_bias, (e + 1) * (UNITS * UNIT))
                            sp.dma_start(b2_rows[:, par:par + 1, :],
                                         b2[bass.ds(e + 2, 1)].partition_broadcast(P)).then_inc(l_b2[par], 16)
                    sp.wait_ge(w_split, (E - 1) * (2 * UNITS))
                    for t in range(UNITS + 1):
                        if 0 < t < UNITS:
                            sp.wait_ge(pool_out, t)
                            sp.dma_start(of[:, (t - 1) * UNIT:t * UNIT, :],
                                         acc[:, (t - 1) * UNIT:t * UNIT, :]).then_inc(s_out[t % 2], 16)
                        if t < UNITS:
                            if t >= 2:
                                sp.wait_ge(pool_out, t - 1)
                            sp.dma_start(slabs[t % 2], x1_dram[:, t * UNIT:(t + 1) * UNIT, :]).then_inc(l_x1[t % 2], 16)
                    for i, (made, n) in enumerate(((dve_out, 2), (pool_out, UNITS))):
                        tiles = slice(TILES - UNIT + i * UNIT // 2, TILES - UNIT + (i + 1) * UNIT // 2)
                        sp.wait_ge(made, n)
                        sp.dma_start(of[:, tiles, :], acc[:, tiles, :]).then_inc(s_out[i], 16)
                    for i, s in enumerate(s_out):
                        sp.wait_ge(s, (UNITS // 2 + i) * 16)

                @block.tensor
                def _(pe):
                    pe.sem_inc(h_free, 3)
                    pe.sem_inc(down_done, 1)

                    def up(e, par, t, f):
                        n = hidden(e, t, f)
                        pe.wait_ge(up_free, n + 1)
                        tok = bass.ds(t * UTOK, UTOK)
                        i = 0
                        for k in range(KD):
                            for w, h in ((w1_hi, h2_hi), (w1_hi, h2_lo), (w1_lo, h2_hi)):
                                last = nc.tensor.matmul(up_ps[f % 4], w[par][:, k, f * P:(f + 1) * P], h[:, k, tok],
                                                        start=(i == 0), stop=(i == 3 * KD - 1))
                                i += 1
                        last.then_inc(up_done, 1)

                    def down(e, par, t, f):
                        n = hidden(e, t, f)
                        pe.wait_ge(lo_done, n + 2 + 1)
                        for j in range(UNIT):
                            if f == 0:
                                u = e * UNITS + t
                                pe.wait_ge(*((dve_evict, 2 * u + j + 1) if j < 2 else (act_evict, 2 * u + j - 1)))
                            tok = slice(j * P, (j + 1) * P)
                            nc.tensor.matmul(down_ps[j], h_hi[:, f % 4, tok],
                                             w2_both[par][:, f, :, :].rearrange("p a d -> p (a d)"),
                                             start=(f == 0), stop=False)
                            last = nc.tensor.matmul(down_ps[j][:, 0:D], h_lo[:, f % 4, tok],
                                                    w2_both[par][:, f, 0, :], start=False, stop=(f == FT - 1))
                            if f == FT - 1:
                                last.then_inc(down_done, 1)
                        if f < FT - 1:
                            last.then_inc(h_free, 1)

                    def unit(e, par, t, following, last):
                        for f in range(FT):
                            if f + AHEAD < FT:
                                up(e, par, t, f + AHEAD)
                            elif following:
                                if following[1] != par and f + AHEAD == FT:
                                    pe.wait_ge(w_split, (e + 1) * (2 * UNITS))
                                up(*following, f + AHEAD - FT)
                            down(e, par, t, f)

                    pe.wait_ge(first_w1, 2)
                    for f in range(AHEAD):
                        up(0, 0, 0, f)
                    pe.wait_ge(first_w2, 2)
                    experts(pe, unit)

                @block.scalar
                def _(act):
                    act.sem_inc(up_free, 4)
                    act.sem_inc(act_evict, 2)

                    def gelu(e, par, t, f):
                        n = hidden(e, t, f)
                        wait_alone(act, (up_done, n + 1), (lo_done, n + 1))
                        bias = b1_cols[:, bass.ds(e * FT + f, 1)]
                        nc.scalar.activation(g_sb[:, f % 2, :], up_ps[f % 4], ACT.Gelu_apprx_tanh,
                                             bias=bias).then_inc(g_done, 1)
                        wait_slot(act, e, t, f)
                        nc.scalar.activation(h_hi[:, f % 4, :], up_ps[f % 4], ACT.Gelu_apprx_tanh,
                                             bias=bias).then_inc(up_free, 1)

                    def unit(e, par, t, following, last):
                        for f in range(AHEAD, FT):
                            gelu(e, par, t, f)
                        if following:
                            for f in range(AHEAD):
                                gelu(*following, f)
                        u = e * UNITS + t
                        for j in (2, 3):
                            wait_alone(act, (down_done, u * UNIT + j + 2), (pool_evict, 2 * u + j - 1))
                            nc.scalar.activation(y_sb[:, j - 2, :], down_ps[j], ACT.Copy,
                                                 scale=gate_of(e, t, j)).then_inc(act_evict, 1)

                    act.wait_ge(l_w1, 16)
                    nc.scalar.activation(w1_hi[0][:], w1_raw[:], ACT.Copy).then_inc(first_w1, 1)
                    act.wait_ge(l_w2, 16)
                    nc.scalar.activation(w2_both[0][:, :, 0, :], w2_raw, ACT.Copy).then_inc(first_w2, 1)
                    for f in range(AHEAD):
                        gelu(0, 0, 0, f)
                    experts(act, unit)

                @block.vector
                def _(dve):
                    dve.sem_inc(lo_done, 2)
                    dve.sem_inc(dve_evict, 2)

                    def low(e, par, t, f):
                        n = hidden(e, t, f)
                        dve.wait_ge(g_done, n + 1)
                        dve.wait_ge(up_free, n + 4 + 1)
                        nc.vector.tensor_tensor(h_lo[:, f % 4, :], g_sb[:, f % 2, :], h_hi[:, f % 4, :].bitcast(F32),
                                                ALU.subtract).then_inc(lo_done, 1)

                    def unit(e, par, t, following, last):
                        u = e * UNITS + t
                        tile = lambda j: acc[:, bass.ds(t * UNIT + j, 1), :]
                        dve.wait_ge(l_b2[par], (e - par) * 8 + 16)
                        for f in range(AHEAD, FT):
                            low(e, par, t, f)
                            j = f - AHEAD - 1
                            if 0 <= j < UNIT:
                                nc.vector.scalar_tensor_tensor(tile(j), b2_rows[:, par:par + 1, :], gate_of(e, t, j),
                                                               tile(j), ALU.mult, ALU.add).then_inc(dve_bias, 1)
                        if following:
                            low(*following, 0)
                        for j in (0, 1):
                            wait_alone(dve, (dve_bias, u * UNIT + j + 1), (down_done, u * UNIT + j + 2))
                            nc.vector.scalar_tensor_tensor(tile(j), down_ps[j][:, 0:D].unsqueeze(1), gate_of(e, t, j),
                                                           tile(j), ALU.mult, ALU.add).then_inc(dve_first, 1)
                        for j in (0, 1):
                            dve.wait_ge(dve_first, 2 * u + j + 1)
                            nc.vector.scalar_tensor_tensor(tile(j), down_ps[j][:, D:2 * D].unsqueeze(1),
                                                           gate_of(e, t, j), tile(j),
                                                           ALU.mult, ALU.add).then_inc(dve_evict, 1)
                        if following:
                            low(*following, 1)
                        elif last:
                            half = acc[:, TILES - UNIT:TILES - UNIT // 2, :]
                            dve.wait_ge(dve_evict, 2 * E * UNITS + 2)
                            nc.vector.tensor_tensor(half, half, out_gates[:, B - 1:B, D:2 * D].broadcast_to(
                                [P, UNIT // 2, D]), ALU.mult).then_inc(dve_out, 1)
                            dve.wait_ge(dve_out, 1)
                            dve.wait_ge(l_x1[(UNITS - 1) % 2], UNITS // 2 * 16)
                            nc.vector.tensor_tensor(half, half, slabs[(UNITS - 1) % 2][:, 0:UNIT // 2, :],
                                                    ALU.add).then_inc(dve_out, 1)

                    dve.wait_ge(first_w1, 1)
                    nc.vector.tensor_tensor(w1_lo[0][:], w1_raw[:], w1_hi[0][:].bitcast(F32),
                                            ALU.subtract).then_inc(first_w1, 1)
                    dve.wait_ge(first_w2, 1)
                    nc.vector.tensor_tensor(w2_both[0][:, :, 1, :], w2_raw, w2_both[0][:, :, 0, :].bitcast(F32),
                                            ALU.subtract).then_inc(first_w2, 1)
                    for f in range(AHEAD):
                        low(0, 0, 0, f)
                    dve.wait_ge(acc_zero, 1)
                    experts(dve, unit)

                @block.gpsimd
                def _(pool):
                    pool.sem_inc(pool_evict, 2)
                    nc.gpsimd.memset(acc[:], 0.0).then_inc(acc_zero, 1)

                    def add(e, t):
                        u = e * UNITS + t
                        tile = lambda j: acc[:, bass.ds(t * UNIT + j, 1), :]
                        for n, sem_, before in ((0, pool_first, act_evict), (1, pool_evict, pool_first)):
                            for j in (2, 3):
                                if n == 0:
                                    wait_alone(pool, (dve_bias, u * UNIT + j + 1), (before, 2 * u + j - 1 + 2))
                                else:
                                    wait_alone(pool, (before, 2 * u + j - 1))
                                nc.gpsimd.tensor_tensor(tile(j), tile(j),
                                                        y_sb[:, j - 2:j - 1, n * D:(n + 1) * D],
                                                        ALU.add).then_inc(sem_, 1)

                    def split(e, par, t):
                        to = 1 - par
                        cols = bass.ds(t * P, P)
                        row = bass.ds(t, 1)
                        done_ = e * (2 * UNITS) + t * 2
                        nc.gpsimd.tensor_copy(w1_hi[to][:, :, cols], w1_raw[:, :, cols]).then_inc(split_chain, 1)
                        nc.gpsimd.tensor_copy(w2_both[to][:, row, 0, :], w2_raw[:, row, :]).then_inc(split_chain, 1)
                        wait_alone(pool, (split_chain, done_ + 1))
                        nc.gpsimd.tensor_tensor(w1_lo[to][:, :, cols], w1_raw[:, :, cols],
                                                w1_hi[to][:, :, cols].bitcast(F32), ALU.subtract).then_inc(w_split, 1)
                        wait_alone(pool, (split_chain, done_ + 2))
                        nc.gpsimd.tensor_tensor(w2_both[to][:, row, 1, :], w2_raw[:, row, :],
                                                w2_both[to][:, row, 0, :].bitcast(F32),
                                                ALU.subtract).then_inc(w_split, 1)

                    def expert(e, par):
                        wait_alone(pool, (down_done, e * (UNITS * UNIT) + 1), (l_w1, e * 16 + 32), (l_w2, e * 16 + 32))
                        with pool.Fori(0, UNITS) as t:
                            split(e, par, t)
                            add(e, t)

                    with pool.Fori(0, E // 2 - 1) as pair:
                        expert(pair * 2, 0)
                        expert(pair * 2 + 1, 1)
                    expert(E - 2, 0)

                    def finish(b, t, i, loads, first):
                        u = (E - 1) * UNITS + t
                        if first == 0:
                            wait_alone(pool, (dve_evict, 2 * u + 2 + 2))
                        wait_alone(pool, (pool_evict, 2 * u + 2 + 2))
                        tiles = acc[:, bass.ds(t * UNIT + first, UNIT - first), :]
                        nc.gpsimd.tensor_tensor(tiles, tiles, out_gates[:, b:b + 1, D:2 * D].broadcast_to(
                            [P, UNIT - first, D]), ALU.mult).then_inc(pool_scaled, 1)
                        wait_alone(pool, (pool_scaled, t + 1), (l_x1[i], loads * 16))
                        nc.gpsimd.tensor_tensor(tiles, tiles, slabs[i][:, first:UNIT, :], ALU.add).then_inc(pool_out, 1)

                    for b in range(B):
                        pairs = UNITS // B // 2
                        with pool.Fori(0, pairs - (b == B - 1)) as half:
                            for i in range(2):
                                t = half * 2 + (b * 2 * pairs + i)
                                add(E - 1, t)
                                finish(b, t, i, half + (b * pairs + 1), 0)
                    for i in range(2):
                        add(E - 1, UNITS - 2 + i)
                        finish(B - 1, UNITS - 2 + i, i, UNITS // 2, i * UNIT // 2)


def kernel(L0_attn_x, L0_attn_Wq, L0_attn_Wk, L0_attn_Wv, L0_attn_Wo, L0_ffn_Wg, L0_ffn_bg, L0_ffn_Wt, L0_ffn_bt,
           L0_ffn_W1, L0_ffn_b1, L0_ffn_W2, L0_ffn_b2, L0_c, L0_wmod):
    import numpy as np
    import concourse.bacc as bacc
    from concourse.bass_utils import run_bass_kernel_spmd

    A = np.asarray
    order = np.r_[0:HS:2, 1:HS:2]
    heads = [A(L0_attn_Wq)[0][order], A(L0_attn_Wq)[1][order], A(L0_attn_Wk)[order], A(L0_attn_Wv)]
    theta = np.float32(10000.0) ** (np.float32(-2.0) * np.arange(0, HS, 2, dtype=np.float32) / np.float32(HS))
    angles = np.arange(T, dtype=np.float32)[:, None] * theta.astype(np.float32)[None, :]
    rows = np.arange(P)
    mask = np.where(rows[None, :] > rows[:, None], np.float32(-2.0 ** 127), np.float32(0))
    arrays = {
        "x": A(L0_attn_x),
        "wqkvT": np.concatenate(heads, axis=0).T,
        "woT": A(L0_attn_Wo).T,
        "wgt": np.concatenate([A(L0_ffn_Wg), A(L0_ffn_Wt)], axis=1),
        "bgt": np.concatenate([A(L0_ffn_bg), A(L0_ffn_bt)]),
        "w1": A(L0_ffn_W1),
        "b1": A(L0_ffn_b1).reshape(E * FT, P).T,
        "w2": A(L0_ffn_W2),
        "b2": A(L0_ffn_b2),
        "c": A(L0_c).reshape(B, KD, P).transpose(2, 1, 0),
        "wmod": A(L0_wmod),
        "cos": np.cos(angles.astype(np.float64)).astype(np.float32),
        "sin": np.sin(angles.astype(np.float64)).astype(np.float32),
        "ident": np.eye(P, dtype=np.float32),
        "mask": mask.astype(np.float32),
    }
    arrays = {f"{n}_dram": np.ascontiguousarray(a) for n, a in arrays.items()}
    nc = bacc.Bacc("TRN2", target_bir_lowering=False, num_devices=1)
    args = [nc.dram_tensor(n, a.shape, mybir.dt.from_np(a.dtype), kind="ExternalInput").ap()
            for n, a in arrays.items()]
    args.append(nc.dram_tensor("out_dram", (B, T, D), F32, kind="ExternalOutput").ap())
    adaln_block(nc, *args)
    r = run_bass_kernel_spmd(nc, [arrays], core_ids=[0])
    return r.results[0]["out_dram"]
```
